# Optimizing a Trainium2 kernel written in Bass

```python
import numpy as np
import jax
import jax.numpy as jnp

def _softmax(x, axis=-1):
    return jax.nn.softmax(x, axis=axis)

def _gelu(x):
    return jax.nn.gelu(x, approximate=True)

def _silu(x):
    return jax.nn.silu(x)

def _sigmoid(x):
    return jax.nn.sigmoid(x)

def _layernorm(x, axis=-1, eps=1e-05):
    m = jnp.mean(x, axis=axis, keepdims=True)
    v = jnp.var(x, axis=axis, keepdims=True)
    return (x - m) / jnp.sqrt(v + eps)

def _scatter_add(tgt, idx, src, axis=0):
    return tgt.at[idx].add(src)

def _segment_sum(src, seg, n):
    return jax.ops.segment_sum(src, seg, n)
kernel_name = 'mk_adaln_d1_jaxref_r4_3fd88b'

def setup_inputs(seed: int=0):
    np.random.seed(seed)
    _w = jnp.asarray

    def _L0_attn_setup():
        import jax, jax.numpy as jnp
        import numpy as np
        D_MODEL = 256
        NHEAD = 16
        D_K = D_MODEL // NHEAD
        MAX_REL = 256
        key = jax.random.key(seed)
        ks = jax.random.split(key, 6)
        B, S = (4, 512)
        s = 1.0 / np.sqrt(D_MODEL)
        x = jax.random.normal(ks[0], (B, S, D_MODEL), dtype=jnp.float32)
        W_qkv = jax.random.normal(ks[1], (D_MODEL, 3 * D_MODEL), dtype=jnp.float32) * s
        b_qkv = jnp.zeros((3 * D_MODEL,), dtype=jnp.float32)
        W_out = jax.random.normal(ks[2], (D_MODEL, D_MODEL), dtype=jnp.float32) * s
        b_out = jnp.zeros((D_MODEL,), dtype=jnp.float32)
        rel_bias = jax.random.normal(ks[3], (2 * MAX_REL + 1, NHEAD), dtype=jnp.float32) * 0.02
        return {'x': x, 'W_qkv': W_qkv, 'b_qkv': b_qkv, 'W_out': W_out, 'b_out': b_out, 'rel_bias': rel_bias}
    _L0_attn_in = _L0_attn_setup()

    def _L0_ffn_setup():
        import jax, jax.numpy as jnp
        import numpy as np
        B, S, H, E, K, I = (4, 512, 256, 8, 2, 1024)
        GATE_EPS = 1e-06
        LN_EPS = 1e-05
        key = jax.random.key(seed)
        k0, k1, k2, k3 = jax.random.split(key, 4)
        x = jax.random.normal(k0, (B, S, H), jnp.float32)
        gate_w = jax.random.normal(k1, (E, H), jnp.float32) * np.float32(np.sqrt(2.0 / (H + E)))
        expert_bias = jnp.zeros((E,), jnp.float32)
        w_up = jax.random.normal(k2, (E, I, H), jnp.float32) * np.float32(np.sqrt(2.0 / (H + I)))
        w_down = jax.random.normal(k3, (E, H, I), jnp.float32) * np.float32(np.sqrt(2.0 / (H + I)))
        return {'x': x, 'gate_w': gate_w, 'expert_bias': expert_bias, 'w_up': w_up, 'w_down': w_down}
    _L0_ffn_in = _L0_ffn_setup()
    _L0_c = _w((lambda *s: np.random.randn(*s).astype(np.float32) * 0.05)(8, 256))
    _L0_wmod = _w((lambda *s: np.random.randn(*s).astype(np.float32) * 0.05)(256, 6 * 256) * 256 ** (-0.5))
    _d = {'L0_attn_x': _L0_attn_in['x'], 'L0_attn_W_qkv': _L0_attn_in['W_qkv'], 'L0_attn_b_qkv': _L0_attn_in['b_qkv'], 'L0_attn_W_out': _L0_attn_in['W_out'], 'L0_attn_b_out': _L0_attn_in['b_out'], 'L0_attn_rel_bias': _L0_attn_in['rel_bias'], 'L0_ffn_gate_w': _L0_ffn_in['gate_w'], 'L0_ffn_expert_bias': _L0_ffn_in['expert_bias'], 'L0_ffn_w_up': _L0_ffn_in['w_up'], 'L0_ffn_w_down': _L0_ffn_in['w_down'], 'L0_c': _L0_c, 'L0_wmod': _L0_wmod}
    _x0 = _d['L0_attn_x']
    _d['L0_attn_x'] = jax.random.normal(jax.random.fold_in(jax.random.key(seed), 1), (8, 512, 256), dtype=_x0.dtype)
    del _x0
    return _d

def reference(L0_attn_x, L0_attn_W_qkv, L0_attn_b_qkv, L0_attn_W_out, L0_attn_b_out, L0_attn_rel_bias, L0_ffn_gate_w, L0_ffn_expert_bias, L0_ffn_w_up, L0_ffn_w_down, L0_c, L0_wmod):

    def _L0_attn_ref(x, W_qkv, b_qkv, W_out, b_out, rel_bias):
        import jax, jax.numpy as jnp
        import numpy as np
        D_MODEL = 256
        NHEAD = 16
        D_K = D_MODEL // NHEAD
        MAX_REL = 256
        B, S, D = x.shape
        qkv = x @ W_qkv + b_qkv
        qkv = qkv.reshape(B, S, 3, NHEAD, D_K)
        q, k, v = (qkv[:, :, 0], qkv[:, :, 1], qkv[:, :, 2])
        scores = jnp.einsum('bihd,bjhd->bhij', q, k) / jnp.sqrt(jnp.float32(D_K))
        idxs = jnp.arange(S)
        rel = jnp.clip(idxs[:, None] - idxs[None, :] + MAX_REL, 0, 2 * MAX_REL)
        bias = rel_bias[rel]
        scores = scores + jnp.transpose(bias, (2, 0, 1))[None]
        attn = jax.nn.softmax(scores, axis=-1)
        out = jnp.einsum('bhij,bjhd->bihd', attn, v).reshape(B, S, D)
        return out @ W_out + b_out

    def _L0_ffn_ref(x, gate_w, expert_bias, w_up, w_down):
        import jax, jax.numpy as jnp
        import numpy as np
        B, S, H, E, K, I = (4, 512, 256, 8, 2, 1024)
        GATE_EPS = 1e-06
        LN_EPS = 1e-05
        logits = jnp.einsum('bsh,eh->bse', x, gate_w) + expert_bias
        weights = jax.nn.softmax(logits, axis=-1)
        top_w, top_i = jax.lax.top_k(weights, K)
        top_w = top_w / (jnp.sum(top_w, axis=-1, keepdims=True) + GATE_EPS)
        sparse_w = jnp.sum(jax.nn.one_hot(top_i, E, dtype=weights.dtype) * top_w[..., None], axis=-2)
        out = jnp.zeros_like(x)
        for e in range(E):
            h = jax.nn.gelu(jnp.einsum('bsh,ih->bsi', x, w_up[e]), approximate=False)
            y = jnp.einsum('bsi,hi->bsh', h, w_down[e])
            out = out + sparse_w[..., e:e + 1] * y
        mu = jnp.mean(out, axis=-1, keepdims=True)
        var = jnp.mean(jnp.square(out - mu), axis=-1, keepdims=True)
        out = (out - mu) * jax.lax.rsqrt(var + LN_EPS)
        return out + x
    x = L0_attn_x
    mod = (_silu(L0_c) @ L0_wmod).reshape(L0_c.shape[0], 6, 1, -1)
    sa, ca, ga, sb, cb, gb = (mod[:, 0], mod[:, 1], mod[:, 2], mod[:, 3], mod[:, 4], mod[:, 5])
    ga = (2 * (ga >= 0) - 1) * jnp.maximum(jnp.abs(ga), 0.25)
    gb = (2 * (gb >= 0) - 1) * jnp.maximum(jnp.abs(gb), 0.25)
    h = _layernorm(x, axis=-1) * (1 + ca) + sa
    x = x + ga * _L0_attn_ref(h, L0_attn_W_qkv, L0_attn_b_qkv, L0_attn_W_out, L0_attn_b_out, L0_attn_rel_bias)
    h = _layernorm(x, axis=-1) * (1 + cb) + sb
    x = x + gb * _L0_ffn_ref(h, L0_ffn_gate_w, L0_ffn_expert_bias, L0_ffn_w_up, L0_ffn_w_down)
    return x

_drawn_inputs = setup_inputs


def setup_inputs(seed=0):
    import zlib

    import numpy as np

    out = dict(_drawn_inputs(seed))
    spreads = {'L0_attn_b_qkv': (0.0, 0.1), 'L0_attn_b_out': (0.0, 0.1), 'L0_ffn_expert_bias': (0.0, 0.1)}
    factors = {'L0_attn_rel_bias': 62.397}
    for name, (base, spread) in spreads.items():
        noise = np.random.default_rng([zlib.crc32(name.encode()), seed]).standard_normal(out[name].shape)
        drawn = base * np.exp(spread * noise) if base else spread * noise
        out[name] = jnp.asarray(drawn.astype(out[name].dtype))
    for name, factor in factors.items():
        out[name] = (out[name] * factor).astype(out[name].dtype)
    return out
```

```python
from contextlib import ExitStack

import numpy as np

import concourse.bass as bass
from concourse import mybir

F32 = mybir.dt.float32
BF16 = mybir.dt.bfloat16
I32 = mybir.dt.int32
U32 = mybir.dt.uint32
ALU = mybir.AluOpType
ACT = mybir.ActivationFunctionType
AX = mybir.AxisListType

P = 128
B, S, D = 8, 512, 256
NH, DK = 16, 16
MAXREL = 256
NE, NI = 8, 1024
LN_EPS = 1e-5
GATE_EPS = 1e-6
TB = S // P
DC = D // P
NT = B * TB
ZW = S + (TB - 1) * P
EXT = ZW + P - 1
HALF = NH // 2
PARTS = 3
Q_PART = (0, 0, 1, 1, 0, 2)
K_PART = (0, 1, 0, 1, 2, 0)
KS = len(Q_PART) * DK
BIG = 3.0e38


def at_least(engine, semaphore, value):
    if not isinstance(value, int) or value > 0:
        engine.wait_ge(semaphore, value)


def by_pairs(engine, step):
    for u in range(2):
        step(u, u)
    with engine.Fori(1, B // 2) as i:
        for u in range(2):
            step(i * 2 + u, u)


def apart(engine, passed):
    engine.sem_inc(passed, 1)


def make_identity(pool, ident, zeroed, done):
    pool.memset(ident[:, :], 0.0).then_inc(zeroed, 1)
    pool.wait_ge(zeroed, 1)
    pool.affine_select(out=ident[:, :], in_=ident[:, :], compare_op=ALU.not_equal, fill=1.0, base=0,
                       pattern=[[-1, P]], channel_multiplier=1).then_inc(done, 1)


def prepare(nc, x, c_t, wmod, rel_rev, mod_rows, ext_rows, h1t):
    with ExitStack() as ctx:
        def sb(name, shape, dt=F32):
            return ctx.enter_context(nc.sbuf_tensor("a_" + name, shape, dt))

        def sem(name):
            return ctx.enter_context(nc.semaphore("a_" + name))

        ident = sb("ident", [P, P])
        ct = sb("ct", [P, DC, B])
        ct_e = sb("ct_e", [P, DC, B])
        silu = sb("silu", [P, DC, B])
        wm = sb("wm", [P, DC, 6 * D])
        rows = sb("rows", [B, 6 * D])
        sgn = sb("sgn", [B, 2, D])
        scale = sb("scale", [P, DC, B])
        shift = sb("shift", [P, DC, B])
        ext = sb("ext", [NH, EXT])
        xt = sb("xt", [P, 2, TB, D])
        stats = sb("stats", [P, 2, TB, 6])
        mv = sb("mv", [P, 2, TB, 2])
        std = sb("std", [P, 2, TB])
        rstd = sb("rstd", [P, 2, TB])
        xh = sb("xh", [P, 2, TB, D])
        ht = sb("ht", [P, 2, DC, S])
        ps_mod = ctx.enter_context(nc.psum_tensor("a_ps_mod", [P, 3, 512], F32))
        ps_col = ctx.enter_context(nc.psum_tensor("a_ps_col", [P, 512], F32))
        ps_t = ctx.enter_context(nc.psum_tensor("a_ps_t", [P, 2, DC, S], F32))

        eps = sb("eps", [P, 1])
        zeroed, ident_ready, eps_set = sem("zeroed"), sem("ident_ready"), sem("eps_set")
        dve_passed = sem("dve_passed")
        c_in, wm_in, rel_in = sem("c_in"), sem("wm_in"), sem("rel_in")
        exp_done, one_done, rec_done, silu_done = sem("exp_done"), sem("one_done"), sem("rec_done"), sem("silu_done")
        mod_ready, rows_copied, rows_step, rows_done = sem("mod_ready"), sem("rows_copied"), sem("rows_step"), sem("rows_done")
        cols_ready, ext_done, stored = sem("cols_ready"), sem("ext_done"), sem("stored")
        x_in = [sem("x_in0"), sem("x_in1")]
        stats_done, mv_done, std_done, rstd_done, xh_done = (
            sem("stats_done"), sem("mv_done"), sem("std_done"), sem("rstd_done"), sem("xh_done"))
        t_done, h_dve, h_act = sem("t_done"), sem("h_dve"), sem("h_act")
        h_out = [sem("h_out0"), sem("h_out1")]
        block = ctx.enter_context(nc.Block())

        @block.sync
        def _(sp):
            sp.dma_start(ct[:, :, :], c_t.rearrange("(c p) b -> p c b", p=P)).then_inc(c_in, 16)
            sp.dma_start(wm[:, :, :], wmod.rearrange("(c p) n -> p c n", p=P)).then_inc(wm_in, 16)
            sp.dma_start(ext[:, MAXREL - 1:3 * MAXREL], rel_rev).then_inc(rel_in, 16)

            def load(b, u):
                at_least(sp, xh_done, (b - 1) * TB)
                sp.dma_start(xt[:, u, :, :], x[bass.ds(b, 1), :, :].rearrange("b (t p) d -> p (b t) d", p=P)).then_inc(x_in[u], 16)

            by_pairs(sp, load)
            sp.wait_ge(rows_done, 1)
            sp.dma_start(mod_rows, rows[:, :]).then_inc(stored, 16)
            sp.wait_ge(ext_done, 2)
            sp.dma_start(ext_rows, ext[:, :]).then_inc(stored, 16)
            sp.wait_ge(stored, 32)

        @block.gpsimd
        def _(pool):
            make_identity(pool, ident, zeroed, ident_ready)
            def store(b, u):
                pool.wait_ge(h_dve, b + 1)
                pool.wait_ge(h_act, b + 1)
                pool.dma_start(h1t[bass.ds(b, 1), :, :, :].rearrange("b p c s -> (b p) c s"),
                               ht[:, u, :, :]).then_inc(h_out[u], 16)

            by_pairs(pool, store)
            for u in range(2):
                pool.wait_ge(h_out[u], 16 * (B // 2))

        @block.scalar
        def _(act):
            act.wait_ge(c_in, 16)
            act.activation(ct_e[:, :, :], ct[:, :, :], ACT.Exp, scale=-1.0).then_inc(exp_done, 1)
            act.wait_ge(eps_set, 1)

            def normalise(b, u):
                act.wait_ge(mv_done, (b + 1) * TB)
                at_least(act, rstd_done, b - 1)
                act.activation(std[:, u, :], mv[:, u, :, 1], ACT.Sqrt, bias=eps[:, :], scale=1.0).then_inc(std_done, 1)
                act.wait_ge(t_done, b + 1)
                act.wait_ge(cols_ready, 2)
                at_least(act, h_out[u], (b - u) * 8)
                act.activation(ht[:, u, 1, :], ps_t[:, u, 1, :], ACT.Identity, bias=shift[:, 1, bass.ds(b, 1)],
                               scale=scale[:, 1, bass.ds(b, 1)]).then_inc(h_act, 1)

            by_pairs(act, normalise)

        @block.vector
        def _(dve):
            dve.memset(eps[:, :], LN_EPS).then_inc(eps_set, 1)
            dve.wait_ge(exp_done, 1)
            dve.tensor_scalar(ct_e[:, :, :], ct_e[:, :, :], 1.0, None, ALU.add).then_inc(one_done, 1)
            dve.wait_ge(one_done, 1)
            dve.reciprocal(ct_e[:, :, :], ct_e[:, :, :]).then_inc(rec_done, 1)
            dve.wait_ge(rec_done, 1)
            dve.tensor_tensor(silu[:, :, :], ct[:, :, :], ct_e[:, :, :], ALU.mult).then_inc(silu_done, 1)
            dve.wait_ge(mod_ready, 1)
            dve.tensor_copy(shift[:, :, :], ps_col[:, 0:DC * B]).then_inc(cols_ready, 1)
            dve.tensor_scalar(scale[:, :, :], ps_col[:, DC * B:2 * DC * B], 1.0, None, ALU.add).then_inc(cols_ready, 1)
            dve.wait_ge(mod_ready, 2)
            dve.tensor_copy(rows[:, :], ps_mod[0:B, :, :]).then_inc(rows_copied, 1)
            dve.wait_ge(rows_copied, 1)
            for k, g in enumerate((2, 5)):
                dve.tensor_scalar(sgn[:, k, :], rows[:, g * D:(g + 1) * D], 0.0, 2.0, ALU.is_ge, ALU.mult).then_inc(rows_step, 1)
            for k, g in enumerate((1, 4)):
                dve.tensor_scalar(rows[:, g * D:(g + 1) * D], rows[:, g * D:(g + 1) * D], 1.0, None, ALU.add).then_inc(rows_step, 1)
            dve.wait_ge(rows_step, 4)
            dve.tensor_scalar(sgn[:, :, :], sgn[:, :, :], -1.0, None, ALU.add).then_inc(rows_step, 1)
            dve.wait_ge(rows_step, 5)
            for k, g in enumerate((2, 5)):
                dve.tensor_tensor(rows[:, g * D:(g + 1) * D], rows[:, g * D:(g + 1) * D], sgn[:, k, :], ALU.mult).then_inc(rows_step, 1)
            dve.wait_ge(rows_step, 7)
            for k, g in enumerate((2, 5)):
                last = dve.scalar_tensor_tensor(out=rows[:, g * D:(g + 1) * D], in0=rows[:, g * D:(g + 1) * D], scalar=0.25,
                                                in1=sgn[:, k, :], op0=ALU.max, op1=ALU.mult)
            last.then_inc(rows_done, 1)
            dve.wait_ge(rel_in, 16)
            dve.tensor_copy(ext[:, 0:MAXREL - 1], ext[:, MAXREL - 1:MAXREL].to_broadcast([NH, MAXREL - 1])).then_inc(ext_done, 1)
            dve.tensor_copy(ext[:, 3 * MAXREL:EXT], ext[:, 3 * MAXREL - 1:3 * MAXREL].to_broadcast([NH, EXT - 3 * MAXREL])).then_inc(ext_done, 1)

            def normalise(b, u):
                dve.wait_ge(x_in[u], (b - u) * 8 + 16)
                for t in range(TB):
                    dve.bn_stats(stats[:, u, t, :], xt[:, u, t, :]).then_inc(stats_done, 1)
                at_least(dve, std_done, b - 1)
                for t in range(TB):
                    dve.wait_ge(stats_done, b * TB + t + 1)
                    apart(dve, dve_passed)
                    dve.bn_aggr(mv[:, u, t, :], stats[:, u, t, :]).then_inc(mv_done, 1)
                dve.wait_ge(std_done, b + 1)
                dve.reciprocal(rstd[:, u, :], std[:, u, :]).then_inc(rstd_done, 1)
                dve.wait_ge(rstd_done, b + 1)
                at_least(dve, t_done, b - 1)
                for t in range(TB):
                    dve.tensor_scalar(xh[:, u, t, :], xt[:, u, t, :], mv[:, u, t, 0:1], rstd[:, u, t:t + 1],
                                      ALU.subtract, ALU.mult).then_inc(xh_done, 1)
                dve.wait_ge(t_done, b + 1)
                at_least(dve, h_out[u], (b - u) * 8)
                dve.tensor_scalar(ht[:, u, 0, :], ps_t[:, u, 0, :], scale[:, 0, bass.ds(b, 1)], shift[:, 0, bass.ds(b, 1)],
                                  ALU.mult, ALU.add).then_inc(h_dve, 1)

            by_pairs(dve, normalise)

        @block.tensor
        def _(pe):
            pe.wait_ge(silu_done, 1)
            pe.wait_ge(wm_in, 16)
            for j in range(2 * DC):
                for c in range(DC):
                    mm = pe.matmul(ps_col[:, j * B:(j + 1) * B], wm[:, c, j * P:(j + 1) * P], silu[:, c, :],
                                   start=(c == 0), stop=(c == DC - 1))
            mm.then_inc(mod_ready, 1)
            for j in range(3):
                for c in range(DC):
                    mm = pe.matmul(ps_mod[0:B, j, :], silu[:, c, :], wm[:, c, j * 512:(j + 1) * 512],
                                   start=(c == 0), stop=(c == DC - 1))
            mm.then_inc(mod_ready, 1)
            pe.wait_ge(ident_ready, 1)

            def turn(b, u):
                pe.wait_ge(xh_done, (b + 1) * TB)
                at_least(pe, h_dve, b - 1)
                at_least(pe, h_act, b - 1)
                for c in range(DC):
                    for t in range(TB):
                        mm = pe.transpose(ps_t[:, u, c, t * P:(t + 1) * P], xh[:, u, t, c * P:(c + 1) * P], ident[:, :])
                mm.then_inc(t_done, 1)

            by_pairs(pe, turn)


USES = ((1, "q0"), (2, "back3"), (3, "k0"), (3, "turn0"), (4, "turn1"), (5, "out0"), (6, "back0"), (7, "out1"),
        (8, "q1"), (9, "k1"), (10, "back1"), (11, "v0"), (12, "v1"), (14, "back2"))
FROM_BEFORE = ("back3", "turn0", "turn1", "out0", "out1")
FOR_NEXT = ("q0", "k0", "q1", "k1", "v0", "v1")


def attention(nc, x, h1t, w_qkv, b_qkv, w_out, b_out, mod_rows, ext_rows, splits, x1):
    GROUPS = NH // TB

    with ExitStack() as ctx:
        def sb(name, shape, dt=F32):
            return ctx.enter_context(nc.sbuf_tensor("b_" + name, shape, dt))

        def sem(name):
            return ctx.enter_context(nc.semaphore("b_" + name))

        ident = sb("ident", [P, P])
        flip = sb("flip", [P, P])
        bias = sb("bias", [P, NH, ZW])
        wqkv = sb("wqkv", [P, DC, 3 * D])
        wo = sb("wo", [P, DC, D])
        b_col = sb("b_col", [P, 4])
        b_v = sb("b_v", [P, D])
        b_o = sb("b_o", [P, D])
        h1 = sb("h1", [P, DC, S])
        qf = sb("qf", [P, S])
        rest = sb("rest", [P, S])
        parts = sb("parts", [P, 2, PARTS, S], BF16)
        qs = sb("qs", [KS, 2, HALF, S], BF16)
        ks = sb("ks", [KS, 2, HALF, S], BF16)
        v_next = sb("v_next", [P, TB, D])
        v = sb("v", [P, TB, NH, 2 * DK])
        sn = sb("sn", [P, TB, S])
        mn = sb("mn", [P, 2, TB])
        pr = sb("pr", [P, 2, TB, S])
        pt = sb("pt", [P, 2, TB, S])
        ot = sb("ot", [P, S])
        inv = sb("inv", [P, TB, TB])
        on = sb("on", [P, TB, D])
        ont = sb("ont", [P, DC, S])
        xb = sb("xb", [P, TB, D])
        ga = sb("ga", [P, D])
        gab = sb("gab", [P, D])
        gated = sb("gated", [P, TB, D])
        ps_s = ctx.enter_context(nc.psum_tensor("b_ps_s", [P, 2, S], F32))
        ps_t = ctx.enter_context(nc.psum_tensor("b_ps_t", [P, TB, S], F32))
        ps_o = ctx.enter_context(nc.psum_tensor("b_ps_o", [P, S], F32))
        ps_m = ctx.enter_context(nc.psum_tensor("b_ps_m", [P, S], F32))

        flip_zeroed = sem("flip_zeroed")
        dve_passed, pool_passed, sp_passed = sem("dve_passed"), sem("pool_passed"), sem("sp_passed")
        zeroed, ident_ready, ones_set, bq_scaled = sem("zeroed"), sem("ident_ready"), sem("ones_set"), sem("bq_scaled")
        w_in, const_in, bq_in = sem("w_in"), sem("const_in"), sem("bq_in")
        bias_in = [sem(f"bias_in{g}") for g in range(GROUPS)]
        h1_in, x_in = sem("h1_in"), sem("x_in")
        parts_out = [sem("parts_out0"), sem("parts_out1")]
        stack_in = [sem("stack_in0"), sem("stack_in1")]
        scored, biased, exped = sem("scored"), sem("biased"), sem("exped")
        turned, out_dve, out_act, weighed = sem("turned"), sem("out_dve"), sem("out_act"), sem("weighed")
        ot_out, used, freed = sem("ot_out"), sem("used"), sem("freed")
        split_step, split_done, inv_done = sem("split_step"), sem("split_done"), sem("inv_done")
        v_moved, gab_done, xg_done, gated_done, x1_done, x1_out = (
            sem("v_moved"), sem("gab_done"), sem("xg_done"), sem("gated_done"), sem("x1_done"), sem("x1_out"))

        def uses_of(kind):
            return [(n, u) for n, u in USES
                    if not (kind == "first" and u in FROM_BEFORE) and not (kind == "last" and u in FOR_NEXT)]

        def uses_before(b, kind):
            return len(FOR_NEXT) if kind == "first" else len(FOR_NEXT) + len(uses_of("first")) + (b - 1) * len(USES)

        def use(b, kind, name):
            return uses_before(b, kind) + [u for _, u in uses_of(kind)].index(name)

        def end_use(name):
            return uses_before(B - 1, "last") + len(uses_of("last")) + FROM_BEFORE.index(name)

        def by_batches(engine, batch):
            batch(0, "first")
            with engine.Fori(1, B - 1) as b:
                batch(b, "middle")
            batch(B - 1, "last")

        block = ctx.enter_context(nc.Block())

        @block.sync
        def _(sp):
            def load_h1(b, at):
                at_least(sp, used, at)
                sp.dma_start(h1[:, :, :], h1t[bass.ds(b, 1), :, :, :].rearrange("b p c s -> (b p) c s")).then_inc(h1_in, 16)

            def store_parts(b, k, name, k_done):
                of, half = (0 if name[0] == "q" else 1), int(name[1])
                sp.wait_ge(split_done, k_done)
                sp.dma_start(splits[bass.ds(b, 1), of, half, :, :, :].rearrange("b s p t -> p (b s) t"),
                             parts[:, k % 2, :, :]).then_inc(parts_out[k % 2], 16)

            def load_stack(b, half):
                for k in range(2):
                    sp.wait_ge(parts_out[k], b * 32 + half * 16 + 16)
                for stack, of, which in ((qs, 0, Q_PART), (ks, 1, K_PART)):
                    for g, part in enumerate(which):
                        sp.dma_start(stack[g * DK:(g + 1) * DK, half, :, :],
                                     splits[bass.ds(b, 1), of, half, part, :, :].rearrange("b (h d) t -> d (b h) t", d=DK)
                                     ).then_inc(stack_in[half], 16)

            def load_x(b):
                at_least(sp, x1_done, (b * 2))
                sp.dma_start(xb[:, :, :], x[bass.ds(b, 1), :, :].rearrange("b (t p) d -> p (b t) d", p=P)).then_inc(x_in, 16)
                sp.dma_start(ga[:, :], mod_rows[bass.ds(b, 1), 2 * D:3 * D].to_broadcast([P, D])).then_inc(x_in, 16)

            def store_x1(b, j):
                sp.wait_ge(x1_done, b * 2 + j + 1)
                sp.dma_start(x1[bass.ds(b, 1), 2 * j * P:2 * (j + 1) * P, :].rearrange("b (t p) d -> p (b t) d", p=P),
                             gated[:, 2 * j:2 * j + 2, :]).then_inc(x1_out, 16)

            sp.dma_start(wqkv[:, :, :], w_qkv.rearrange("(c p) n -> p c n", p=P)).then_inc(w_in, 16)
            load_h1(0, 0)
            sp.dma_start(b_col[:, :], b_qkv[0:2 * D].rearrange("(c p) -> p c", p=P),
                         allow_slow_non_contiguous=True).then_inc(bq_in, 16)
            sp.dma_start(b_v[:, :], b_qkv[2 * D:3 * D].rearrange("(a n) -> a n", a=1).to_broadcast([P, D])).then_inc(const_in, 16)
            sp.dma_start(b_o[:, :], b_out.rearrange("(a n) -> a n", a=1).to_broadcast([P, D])).then_inc(const_in, 16)
            sp.dma_start(wo[:, :, :], w_out.rearrange("(c p) n -> p c n", p=P)).then_inc(w_in, 16)
            for half in range(2):
                for h in range(half * HALF, (half + 1) * HALF):
                    skewed = bass.AP(ext_rows.tensor, h * EXT, [[1, P], [1, ZW]])
                    sp.dma_start(bias[:, h, :], skewed).then_inc(bias_in[h // TB], 16)
                for k in range(2 * half, 2 * half + 2):
                    store_parts(0, k, FOR_NEXT[k], k + 1)
                load_stack(0, half)

            def batch(b, kind):
                if kind != "last":
                    load_h1(b + 1, uses_before(b, kind) - (kind == "middle"))
                if kind != "first":
                    load_x(b - 1)
                if kind != "last":
                    for k in range(2):
                        store_parts(b + 1, k, FOR_NEXT[k], (b + 1) * 4 + k + 1)
                    sp.wait_ge(scored, (b * NH + HALF) * TB)
                    apart(sp, sp_passed)
                    load_stack(b + 1, 0)
                if kind != "first":
                    for j in range(2):
                        store_x1(b - 1, j)
                if kind != "last":
                    for k in range(2, 4):
                        store_parts(b + 1, k, FOR_NEXT[k], (b + 1) * 4 + k + 1)
                    sp.wait_ge(scored, (b + 1) * NH * TB)
                    apart(sp, sp_passed)
                    load_stack(b + 1, 1)

            by_batches(sp, batch)
            load_x(B - 1)
            for j in range(2):
                store_x1(B - 1, j)
            sp.wait_ge(x1_out, 16 * 2 * B)

        @block.gpsimd
        def _(pool):
            make_identity(pool, ident, zeroed, ident_ready)
            pool.memset(flip[:, :], 0.0).then_inc(flip_zeroed, 1)
            pool.wait_ge(flip_zeroed, 1)
            pool.affine_select(out=flip[:, :], in_=flip[:, :], compare_op=ALU.not_equal, fill=1.0, base=1 - P,
                               pattern=[[1, P]], channel_multiplier=1).then_inc(ident_ready, 1)
            pool.memset(v[:, :, :, :], 0.0).then_inc(zeroed, 1)
            pool.wait_ge(zeroed, 2)
            pool.memset(v[:, :, :, DK:DK + 1], 1.0).then_inc(ones_set, 1)

            def split(k, done, reads):
                pool.wait_ge(freed, reads)
                at_least(pool, parts_out[k % 2], (done - k % 2) * 8)
                out = parts[:, k % 2, :, :]
                apart(pool, pool_passed)
                pool.tensor_copy(out[:, 0, :], qf[:, :]).then_inc(split_step, 1)
                pool.wait_ge(split_step, done * 3 + 1)
                pool.tensor_tensor(rest[:, :], qf[:, :], out[:, 0, :], ALU.subtract).then_inc(split_step, 1)
                pool.wait_ge(split_step, done * 3 + 2)
                apart(pool, pool_passed)
                pool.tensor_copy(out[:, 1, :], rest[:, :]).then_inc(split_step, 1)
                pool.wait_ge(split_step, done * 3 + 3)
                pool.tensor_tensor(out[:, 2, :], rest[:, :], out[:, 1, :], ALU.subtract).then_inc(split_done, 1)
                pool.wait_ge(split_done, done + 1)

            def move_v(b, half, reads):
                pool.wait_ge(freed, reads)
                at_least(pool, weighed, (b - 1) * NH + (half + 1) * HALF)
                apart(pool, pool_passed)
                pool.tensor_copy(v[:, :, half * HALF:(half + 1) * HALF, 0:DK],
                                 v_next[:, :, half * P:(half + 1) * P].rearrange("p t (h d) -> p t h d", d=DK)).then_inc(v_moved, 1)

            def residual(b):
                pool.wait_ge(x_in, b * 32 + 32)
                at_least(pool, xg_done, b * TB)
                pool.tensor_tensor(gab[:, :], ga[:, :], b_o[:, :], ALU.mult).then_inc(gab_done, 1)
                pool.wait_ge(gab_done, b + 1)
                for t in range(TB):
                    pool.tensor_tensor(xb[:, t, :], xb[:, t, :], gab[:, :], ALU.add).then_inc(xg_done, 1)

            def add_x(b, j):
                pool.wait_ge(gated_done, b * 2 + j + 1)
                pool.wait_ge(xg_done, b * TB + TB)
                pool.tensor_tensor(gated[:, 2 * j:2 * j + 2, :], gated[:, 2 * j:2 * j + 2, :], xb[:, 2 * j:2 * j + 2, :],
                                   ALU.add).then_inc(x1_done, 1)

            for k in range(4):
                split(k, k, k + 1)
            pool.wait_ge(const_in, 32)
            pool.wait_ge(ones_set, 1)
            for half in range(2):
                move_v(0, half, len(FOR_NEXT))

            def batch(b, kind):
                if kind != "first":
                    residual(b - 1)
                if kind != "last":
                    split(0, (b + 1) * 4, use(b, kind, "q0") + 1)
                if kind != "first":
                    move_v(b, 1, uses_before(b, kind) - 1)
                if kind != "last":
                    split(1, (b + 1) * 4 + 1, use(b, kind, "k0") + 1)
                if kind != "first":
                    for j in range(2):
                        add_x(b - 1, j)
                if kind != "last":
                    for k in range(2, 4):
                        split(k, (b + 1) * 4 + k, use(b, kind, FOR_NEXT[k]) + 1)
                    move_v(b + 1, 0, use(b, kind, "v1") + 1)

            by_batches(pool, batch)
            residual(B - 1)
            for j in range(2):
                add_x(B - 1, j)

        @block.scalar
        def _(act):
            def project_out(name, done, at):
                c = ("q0", "q1", "k0", "k1").index(name)
                act.wait_ge(used, at + 1)
                at_least(act, split_done, done)
                tiles = ps_m[:, :].rearrange("p (t i) -> p t i", i=P)
                act.activation(qf[:, :].rearrange("p (t i) -> p t i", i=P), tiles[:, :, ::-1] if name[0] == "q" else tiles,
                               ACT.Identity, bias=b_col[:, c:c + 1],
                               scale=(DK ** -0.5 if name[0] == "q" else 1.0)).then_inc(freed, 1)

            def exp(h, m, t):
                act.wait_ge(biased, h * TB + t + 1)
                act.activation(pr[:, m, t, :], sn[:, t, :], ACT.Exp, bias=mn[:, m, t:t + 1], scale=-1.0).then_inc(exped, 1)

            def evacuate(h, m):
                act.wait_ge(turned, h * 2 + 2)
                at_least(act, weighed, h - 1)
                act.activation(pt[:, m, 2:4, :], ps_t[:, 2:4, :], ACT.Copy).then_inc(out_act, 1)

            def turn_out(c, at):
                act.wait_ge(used, at + 1)
                act.activation(ont[:, c, :], ps_m[:, :], ACT.Copy).then_inc(freed, 1)

            def outputs(g, at):
                act.wait_ge(weighed, g * TB + TB)
                at_least(act, used, at)
                act.activation(ot[:, :], ps_o[:, :], ACT.Copy).then_inc(ot_out, 1)

            act.wait_ge(bq_scaled, 1)
            for k in range(4):
                project_out(FOR_NEXT[k], k, k)

            def batch(b, kind):
                for n in range(NH):
                    h = b * NH + n
                    at_least(act, turned, (h - 1) * 2)
                    exp(h, n % 2, 0)
                    exp(h, n % 2, 1)
                    if kind != "first" or n > 0:
                        evacuate(h - 1, (n + 1) % 2)
                    exp(h, n % 2, 2)
                    exp(h, n % 2, 3)
                    if n == 1 and kind != "first":
                        outputs(b * GROUPS - 1, uses_before(b, kind))
                    if n in (5, 9, 13):
                        g = (n - 5) // TB
                        if g == 0:
                            outputs(b * GROUPS, 0 if kind == "first" else use(b, kind, "back3") + 1)
                        else:
                            outputs(b * GROUPS + g, use(b, kind, f"back{g - 1}") + 1)
                    for m, u in uses_of(kind):
                        if m == n and u in FOR_NEXT[:4]:
                            project_out(u, (b + 1) * 4 + FOR_NEXT.index(u), use(b, kind, u))
                        if m == n and u in ("turn0", "turn1"):
                            turn_out(int(u[4]), use(b, kind, u))

            by_batches(act, batch)
            evacuate(B * NH - 1, 1)
            outputs(B * GROUPS - 1, uses_before(B - 1, "last") + len(uses_of("last")))
            for c in range(DC):
                turn_out(c, end_use(f"turn{c}"))

        @block.vector
        def _(dve):
            dve.wait_ge(bq_in, 16)
            dve.tensor_scalar(b_col[:, 0:2], b_col[:, 0:2], DK ** -0.5, None, ALU.mult).then_inc(bq_scaled, 1)
            dve.wait_ge(const_in, 32)

            def add_bias(b, n, t):
                k = (b * NH + n) * TB + t
                dve.wait_ge(scored, k + 1)
                at_least(dve, exped, k - TB + 1)
                apart(dve, dve_passed)
                at = (TB - 1 - t) * P
                dve.tensor_tensor_reduce(sn[:, t, :], ps_s[:, t % 2, :], bias[:, n, at:at + S], -1.0, BIG, ALU.add, ALU.min,
                                         mn[:, n % 2, t:t + 1]).then_inc(biased, 1)

            def evacuate(h, m):
                dve.wait_ge(turned, h * 2 + 1)
                at_least(dve, weighed, h - 1)
                dve.tensor_copy(pt[:, m, 0:2, :], ps_t[:, 0:2, :]).then_inc(out_dve, 1)

            def values(b, j, at):
                dve.wait_ge(used, at + 1)
                at_least(dve, v_moved, b * 2)
                dve.tensor_tensor(v_next[:, 2 * j:2 * j + 2, :], ps_m[:, :].rearrange("p (t n) -> p t n", n=D),
                                  b_v[:, :].unsqueeze(1).to_broadcast([P, 2, D]), ALU.add).then_inc(freed, 1)

            def back(b, g, at):
                dve.wait_ge(used, at + 1)
                turned_back = ps_m[:, :].rearrange("p (h t w) -> p h t w", h=TB, t=TB)
                dve.reciprocal(inv[:, :, :], turned_back[:, :, :, DK]).then_inc(inv_done, 1)
                dve.wait_ge(inv_done, b * GROUPS + g + 1)
                dve.tensor_tensor(on[:, :, g * TB * DK:(g + 1) * TB * DK].rearrange("p t (h d) -> p h t d", d=DK),
                                  turned_back[:, :, :, 0:DK], inv[:, :, :].unsqueeze(3).to_broadcast([P, TB, TB, DK]),
                                  ALU.mult).then_inc(freed, 1)

            def gate(b, j, at):
                dve.wait_ge(used, at + 1)
                dve.wait_ge(x_in, b * 32 + 32)
                at_least(dve, x1_out, b * 32)
                dve.tensor_tensor(gated[:, 2 * j:2 * j + 2, :], ps_m[:, :].rearrange("p (t n) -> p t n", n=D),
                                  ga[:, :].unsqueeze(1).to_broadcast([P, 2, D]), ALU.mult).then_inc(freed, 1)
                dve.wait_ge(freed, at + 1)
                dve.sem_inc(gated_done, 1)

            for j in range(2):
                values(0, j, 4 + j)

            def batch(b, kind):
                for n in range(NH):
                    if kind == "first" and n % TB == 0:
                        dve.wait_ge(bias_in[n // TB], 16 * TB)
                    add_bias(b, n, 0)
                    add_bias(b, n, 1)
                    if kind != "first" or n > 0:
                        evacuate(b * NH + n - 1, (n + 1) % 2)
                    add_bias(b, n, 2)
                    add_bias(b, n, 3)
                    for m, u in uses_of(kind):
                        if m == n and u == "back3":
                            back(b - 1, 3, use(b, kind, u))
                        elif m == n and u[:4] == "back":
                            back(b, int(u[4]), use(b, kind, u))
                        elif m == n and u[:3] == "out":
                            gate(b - 1, int(u[3]), use(b, kind, u))
                        elif m == n and u[0] == "v":
                            values(b + 1, int(u[1]), use(b, kind, u))

            by_batches(dve, batch)
            evacuate(B * NH - 1, 1)
            back(B - 1, 3, end_use("back3"))
            for j in range(2):
                gate(B - 1, j, end_use(f"out{j}"))

        @block.tensor
        def _(pe):
            def score(b, n, t):
                k = (b * NH + n) * TB + t
                at_least(pe, biased, k - 1)
                half, m = n // HALF, n % HALF
                pe.matmul(ps_s[:, t % 2, :], qs[:, half, m, t * P:(t + 1) * P], ks[:, half, m, :],
                          start=True, stop=True).then_inc(scored, 1)

            def turn_probabilities(h, m, pair):
                at_least(pe, out_act if pair else out_dve, h)
                for j in (2 * pair, 2 * pair + 1):
                    for t in range(TB):
                        mm = pe.transpose(ps_t[:, j, t * P:(t + 1) * P], pr[:, m, t, j * P:(j + 1) * P], ident[:, :])
                mm.then_inc(turned, 1)

            def weigh(b, n):
                h = b * NH + n
                pe.wait_ge(out_dve, h + 1)
                pe.wait_ge(out_act, h + 1)
                if n % HALF == 0:
                    pe.wait_ge(v_moved, b * 2 + n // HALF + 1)
                if n % TB == 0:
                    at_least(pe, ot_out, b * GROUPS + n // TB)
                for j in range(TB):
                    for t in range(TB):
                        mm = pe.matmul(ps_o[2 * DK * t:2 * DK * (t + 1), n % TB * P:(n % TB + 1) * P], v[:, j, n, :],
                                       pt[:, n % 2, j, t * P:(t + 1) * P], start=(j == 0), stop=(j == TB - 1))
                mm.then_inc(weighed, 1)

            def project(b, name, at):
                at_least(pe, freed, at)
                pe.wait_ge(h1_in, b * 16 + 16)
                if name[0] == "v":
                    for t in range(2):
                        for c in range(DC):
                            j = 2 * int(name[1]) + t
                            mm = pe.matmul(ps_m[:, t * D:(t + 1) * D], h1[:, c, j * P:(j + 1) * P], wqkv[:, c, 2 * D:3 * D],
                                           start=(c == 0), stop=(c == DC - 1))
                else:
                    col = ("q0", "q1", "k0", "k1").index(name) * P
                    for c in range(DC):
                        mm = pe.matmul(ps_m[:, :], wqkv[:, c, col:col + P], h1[:, c, :], start=(c == 0), stop=(c == DC - 1))
                mm.then_inc(used, 1)

            def back(g, at):
                pe.wait_ge(ot_out, g + 1)
                at_least(pe, freed, at)
                for i in range(TB):
                    mm = pe.transpose(ps_m[:, i * P:(i + 1) * P], ot[:, i * P:(i + 1) * P], ident[:, :])
                mm.then_inc(used, 1)

            def turn_outputs(c, at):
                at_least(pe, freed, at)
                for t in range(TB):
                    mm = pe.transpose(ps_m[:, t * P:(t + 1) * P], on[:, t, c * P:(c + 1) * P], flip[:, :])
                mm.then_inc(used, 1)

            def project_outputs(j, at):
                at_least(pe, freed, at)
                for t in range(2):
                    for c in range(DC):
                        mm = pe.matmul(ps_m[:, t * D:(t + 1) * D], ont[:, c, (2 * j + t) * P:(2 * j + t + 1) * P], wo[:, c, :],
                                       start=(c == 0), stop=(c == DC - 1))
                mm.then_inc(used, 1)

            pe.wait_ge(w_in, 32)
            for k, name in enumerate(FOR_NEXT):
                project(0, name, k)
            pe.wait_ge(ident_ready, 2)

            def batch(b, kind):
                for n in range(NH):
                    h = b * NH + n
                    if n % HALF == 0:
                        pe.wait_ge(stack_in[n // HALF], (b + 1) * 32 * len(Q_PART))
                    score(b, n, 0)
                    score(b, n, 1)
                    if kind != "first" or n > 0:
                        pe.wait_ge(exped, h * TB)
                        turn_probabilities(h - 1, (n + 1) % 2, 0)
                        score(b, n, 2)
                        turn_probabilities(h - 1, (n + 1) % 2, 1)
                    else:
                        score(b, n, 2)
                    score(b, n, 3)
                    if n > 1:
                        weigh(b, n - 2)
                    elif kind != "first":
                        weigh(b - 1, n + NH - 2)
                    for m, u in uses_of(kind):
                        at = use(b, kind, u)
                        if m == n and u in FOR_NEXT:
                            project(b + 1, u, at)
                        elif m == n and u == "back3":
                            back(b * GROUPS - 1, at)
                        elif m == n and u[:4] == "back":
                            back(b * GROUPS + int(u[4]), at)
                        elif m == n and u[:4] == "turn":
                            turn_outputs(int(u[4]), at)
                        elif m == n:
                            project_outputs(int(u[3]), at)

            by_batches(pe, batch)
            pe.wait_ge(exped, B * NH * TB)
            for pair in range(2):
                turn_probabilities(B * NH - 1, 1, pair)
            weigh(B - 1, NH - 2)
            weigh(B - 1, NH - 1)
            back(B * GROUPS - 1, end_use("back3"))
            for c in range(DC):
                turn_outputs(c, end_use(f"turn{c}"))
            for j in range(2):
                project_outputs(j, end_use(f"out{j}"))


REGION = B * S + P
MAX_TILES = 2 * B * S // P + NE - 1
RUN_TILES = MAX_TILES + MAX_TILES % 2
TABLE = RUN_TILES + 2
ROW, SLOT, ROUND = range(3)


class Kept:

    def __init__(self, nc, ctx):
        def sb(name, shape, dt=F32):
            return ctx.enter_context(nc.sbuf_tensor("k_" + name, shape, dt))

        self.x1 = sb("x1", [P, NT, D])
        self.h2 = sb("h2", [P, NT, D])
        self.mod = sb("mod", [P, B, 3 * D])
        self.eps = sb("eps", [P, 1])
        self.gates = sb("gates", [P, 2, NT])
        self.rows = sb("rows", [P, 2, NT], U32)
        self.outs = sb("outs", [P, 2, NT], U32)
        self.tiles = sb("tiles", [P, 3, TABLE], I32)
        self.filled = sb("filled", [P, NE], I32)


def route(nc, kept, x1, mod_rows, gate_t, expert_bias, expert_rows):
    with ExitStack() as ctx:
        def sb(name, shape, dt=F32):
            return ctx.enter_context(nc.sbuf_tensor("c_" + name, shape, dt))

        def sem(name):
            return ctx.enter_context(nc.semaphore("c_" + name))

        ident = sb("ident", [P, P])
        before = sb("before", [P, P], BF16)
        ones = sb("ones", [P, P], BF16)
        up_to = sb("up_to", [P, NE, NE])
        ints = sb("ints", [P, 2 * NE + NT + TABLE + 1], I32)
        nums = sb("nums", [P, 2 * NE + NT + TABLE + 1])
        zero = sb("zero", [P, D])
        swing = sb("swing", [P, NE])
        gate = sb("gate", [P, DC, NE])
        e_bias = sb("e_bias", [P, NE])
        stats = sb("stats", [P, NT, 6])
        mv = sb("mv", [P, NT, 2])
        std = sb("std", [P, NT])
        xh = sb("xh", [P, 2, D])
        ht = sb("ht", [P, 2, DC, P])
        logits = sb("logits", [P, NT, NE])
        weights = sb("weights", [P, NT, NE])
        per_tok = sb("per_tok", [P, 4, NT])
        top = sb("top", [P, NT, 8])
        top_i = sb("top_i", [P, NT, 8], U32)
        top_f = sb("top_f", [P, NT, 2])
        hot = sb("hot", [P, 2, NT, NE])
        both = sb("both", [P, NT, NE], BF16)
        run = sb("run", [P, 2, NT, NE])
        rank = sb("rank", [P, NT, NE])
        picked = sb("picked", [P, 2, NT, NE])
        places = sb("places", [P, 2, NT])
        more = sb("more", [P, NE, NT])
        n_tiles = sb("n_tiles", [P, NE])
        mixed = sb("mixed", [P, NE, NE])
        filled = sb("filled", [P, NE])
        last_tile = sb("last_tile", [P, 1])
        index = sb("index", [P, TABLE])
        passed = sb("passed", [P, TABLE, NE])
        scaled = sb("scaled", [P, TABLE, NE])
        row = sb("row", [P, 4, TABLE])
        pads = sb("pads", [P, NE])
        pads_u = sb("pads_u", [P, NE], U32)
        ps_t = ctx.enter_context(nc.psum_tensor("c_ps_t", [P, 2, 512], F32))
        ps_l = ctx.enter_context(nc.psum_tensor("c_ps_l", [P, NT, 2 * NE], F32))
        ps_r = ctx.enter_context(nc.psum_tensor("c_ps_r", [P, 2, NT, 2 * NE], F32))
        iota_e, base, steps_128, iota_t, iota_p = (
            nums[:, 0:NE], nums[:, NE:2 * NE], nums[:, 2 * NE:2 * NE + NT],
            nums[:, 2 * NE + NT:2 * NE + NT + TABLE], nums[:, 2 * NE + NT + TABLE:])

        zeroed, ident_ready, consts_ready, pool_step = sem("zeroed"), sem("ident_ready"), sem("consts_ready"), sem("pool_step")
        x1_in, mod_in, gate_in = [sem(f"x1_in{i}") for i in range(B)], sem("mod_in"), sem("gate_in")
        stats_done, mv_done, std_done, eps_set = sem("stats_done"), sem("mv_done"), sem("std_done"), sem("eps_set")
        xh_done, scaled_done, h2_done = sem("xh_done"), sem("scaled_done"), sem("h2_done")
        turned, turned_out, logged = sem("turned"), sem("turned_out"), sem("logged")
        shifted, exped, hot_done, ranked, placed = sem("shifted"), sem("exped"), sem("hot_done"), sem("ranked"), sem("placed")
        chained, scattered = sem("chained"), sem("scattered")
        block = ctx.enter_context(nc.Block())

        @block.sync
        def _(sp):
            for b in range(B):
                sp.dma_start(kept.x1[:, b * TB:(b + 1) * TB, :], x1[b, :, :].rearrange("(t p) d -> p t d", p=P)).then_inc(x1_in[b], 16)
            sp.dma_start(kept.mod[:, :, :], mod_rows[:, 3 * D:6 * D].unsqueeze(0).to_broadcast([P, B, 3 * D])).then_inc(mod_in, 16)
            sp.dma_start(gate[:, :, :], gate_t.rearrange("(c p) e -> p c e", p=P)).then_inc(gate_in, 16)
            sp.dma_start(e_bias[:, :], expert_bias.rearrange("(a e) -> a e", a=1).to_broadcast([P, NE])).then_inc(gate_in, 16)

        @block.gpsimd
        def _(pool):
            make_identity(pool, ident, zeroed, ident_ready)
            pool.memset(before[:, :], 1.0).then_inc(pool_step, 1)
            pool.memset(up_to[:, :, :], 1.0).then_inc(pool_step, 1)
            pool.memset(ones[:, :], 1.0).then_inc(consts_ready, 1)
            pool.memset(zero[:, :], 0.0).then_inc(consts_ready, 1)
            for at, n, first, step, by_p in ((0, NE, 0, 1, 0), (NE, NE, 0, REGION, 0), (2 * NE, NT, 0, P, 0),
                                             (2 * NE + NT, TABLE, 0, 1, 0), (2 * NE + NT + TABLE, 1, 0, 1, 1)):
                pool.iota(ints[:, at:at + n], pattern=[[step, n]], base=first, channel_multiplier=by_p).then_inc(pool_step, 1)
            pool.wait_ge(pool_step, 7)
            pool.tensor_copy(nums[:, :], ints[:, :]).then_inc(consts_ready, 1)
            pool.affine_select(out=before[:, :], in_=before[:, :], compare_op=ALU.is_gt, fill=0.0, base=0,
                               pattern=[[1, P]], channel_multiplier=-1).then_inc(consts_ready, 1)
            pool.affine_select(out=up_to[:, :, :], in_=up_to[:, :, :], compare_op=ALU.is_ge, fill=0.0, base=0,
                               pattern=[[1, NE], [-1, NE]], channel_multiplier=0).then_inc(consts_ready, 1)
            pool.wait_ge(placed, 1)
            pool.wait_ge(h2_done, NT)
            for t in range(NT):
                for k in range(2):
                    pool.indirect_dma_start(expert_rows, bass.IndirectOffsetOnAxis(ap=kept.rows[:, k, t:t + 1], axis=0),
                                            kept.h2[:, t, :], None).then_inc(scattered, 16)
            for e in range(NE):
                pool.indirect_dma_start(expert_rows, bass.IndirectOffsetOnAxis(ap=pads_u[:, e:e + 1], axis=0),
                                        zero[:, :], None).then_inc(scattered, 16)
            pool.wait_ge(scattered, 16 * (2 * NT + NE))

        @block.scalar
        def _(act):
            act.wait_ge(eps_set, 1)
            act.wait_ge(mv_done, NT)
            act.activation(std[:, :], mv[:, :, 1], ACT.Sqrt, bias=kept.eps[:, :], scale=1.0).then_inc(std_done, 1)
            for t in range(NT):
                act.wait_ge(turned, t + 1)
                at_least(act, logged, t - 1)
                act.activation(ht[:, t % 2, :, :], ps_t[:, t % 2, 0:D], ACT.Copy).then_inc(turned_out, 1)
            act.wait_ge(shifted, 1)
            act.activation(weights[:, :, :], logits[:, :, :], ACT.Exp).then_inc(exped, 1)

        @block.vector
        def _(dve):
            count = [0]

            def link(ins):
                count[0] += 1
                ins.then_inc(chained, 1)
                dve.wait_ge(chained, count[0])

            dve.memset(kept.eps[:, :], LN_EPS).then_inc(eps_set, 1)
            dve.memset(swing[:, 0:NE:2], 1.0)
            link(dve.memset(swing[:, 1:NE:2], -1.0))
            for t in range(NT):
                if t % TB == 0:
                    dve.wait_ge(x1_in[t // TB], 16)
                dve.bn_stats(stats[:, t, :], kept.x1[:, t, :]).then_inc(stats_done, 1)
            for t in range(NT):
                dve.wait_ge(stats_done, t + 1)
                dve.bn_aggr(mv[:, t, :], stats[:, t, :]).then_inc(mv_done, 1)
            dve.wait_ge(std_done, 1)
            link(dve.reciprocal(std[:, :], std[:, :]))
            dve.wait_ge(mod_in, 16)
            for t in range(NT + 2):
                if t < NT:
                    at_least(dve, scaled_done, t - 1)
                    dve.tensor_scalar(xh[:, t % 2, :], kept.x1[:, t, :], mv[:, t, 0:1], std[:, t:t + 1],
                                      ALU.subtract, ALU.mult).then_inc(xh_done, 1)
                if 0 < t <= NT:
                    dve.wait_ge(xh_done, t)
                    dve.tensor_tensor(kept.h2[:, t - 1, :], xh[:, (t - 1) % 2, :], kept.mod[:, (t - 1) // TB, D:2 * D],
                                      ALU.mult).then_inc(scaled_done, 1)
                if t > 1:
                    dve.wait_ge(scaled_done, t - 1)
                    dve.tensor_tensor(kept.h2[:, t - 2, :], kept.h2[:, t - 2, :], kept.mod[:, (t - 2) // TB, 0:D],
                                      ALU.add).then_inc(h2_done, 1)

            dve.wait_ge(logged, NT)
            dve.wait_ge(gate_in, 32)
            link(dve.tensor_tensor(logits[:, :, :], ps_l[:, :, 0:NE], e_bias[:, :].unsqueeze(1).to_broadcast([P, NT, NE]), ALU.add))
            link(dve.tensor_reduce(per_tok[:, 0, :], logits[:, :, :], AX.X, ALU.max))
            dve.tensor_tensor(logits[:, :, :], logits[:, :, :], per_tok[:, 0, :].unsqueeze(2).to_broadcast([P, NT, NE]),
                              ALU.subtract).then_inc(shifted, 1)
            dve.wait_ge(exped, 1)
            link(dve.tensor_reduce(per_tok[:, 1, :], weights[:, :, :], AX.X, ALU.add))
            link(dve.reciprocal(per_tok[:, 2, :], per_tok[:, 1, :]))
            link(dve.tensor_tensor(weights[:, :, :], weights[:, :, :], per_tok[:, 2, :].unsqueeze(2).to_broadcast([P, NT, NE]), ALU.mult))
            for t in range(NT):
                ins = dve.max(top[:, t, :], weights[:, t, :])
            link(ins)
            for t in range(NT):
                ins = dve.max_index(top_i[:, t, :], top[:, t, :], weights[:, t, :])
            link(ins)
            link(dve.tensor_tensor(per_tok[:, 3, :], top[:, :, 0], top[:, :, 1], ALU.add))
            link(dve.tensor_scalar(per_tok[:, 3, :], per_tok[:, 3, :], GATE_EPS, None, ALU.add))
            link(dve.reciprocal(per_tok[:, 3, :], per_tok[:, 3, :]))
            for k in range(2):
                dve.tensor_tensor(kept.gates[:, k, :], top[:, :, k], per_tok[:, 3, :], ALU.mult)
            link(dve.tensor_copy(top_f[:, :, :], top_i[:, :, 0:2]))
            dve.wait_ge(consts_ready, 5)
            for k in range(2):
                ins = dve.tensor_tensor(hot[:, k, :, :], iota_e.unsqueeze(1).to_broadcast([P, NT, NE]),
                                        top_f[:, :, k:k + 1].to_broadcast([P, NT, NE]), ALU.is_equal)
            link(ins)
            dve.tensor_tensor(both[:, :, :], hot[:, 0, :, :], hot[:, 1, :, :], ALU.add).then_inc(hot_done, 1)
            dve.wait_ge(ranked, 1)
            link(dve.tensor_copy(run[:, 0, :, :], ps_r[:, 1, :, 0:NE]))
            a, shift = 0, 1
            while shift < NT:
                dve.tensor_copy(run[:, 1 - a, 0:shift, :], run[:, a, 0:shift, :])
                link(dve.tensor_tensor(run[:, 1 - a, shift:NT, :], run[:, a, shift:NT, :], run[:, a, 0:NT - shift, :], ALU.add))
                a, shift = 1 - a, 2 * shift
            counts = run[:, a, NT - 1, :]
            link(dve.tensor_tensor(rank[:, :, :], run[:, a, :, :], ps_r[:, 1, :, 0:NE], ALU.subtract))
            link(dve.tensor_tensor(rank[:, :, :], rank[:, :, :], ps_r[:, 0, :, 0:NE], ALU.add))
            link(dve.tensor_tensor(rank[:, :, :], rank[:, :, :], base.unsqueeze(1).to_broadcast([P, NT, NE]), ALU.add))
            for k in range(2):
                ins = dve.tensor_tensor(picked[:, k, :, :], hot[:, k, :, :], rank[:, :, :], ALU.mult)
            link(ins)
            link(dve.tensor_reduce(places[:, :, :], picked[:, :, :, :], AX.X, ALU.add))
            dve.tensor_copy(kept.rows[:, :, :], places[:, :, :])
            link(dve.tensor_tensor(pads[:, :], counts, base, ALU.add))
            link(dve.tensor_scalar(pads[:, :], pads[:, :], iota_p, None, ALU.add))
            link(dve.tensor_copy(pads_u[:, :], pads[:, :]))
            dve.sem_inc(placed, 1)
            link(dve.tensor_tensor(more[:, :, :], counts.unsqueeze(2).to_broadcast([P, NE, NT]),
                                   steps_128.unsqueeze(1).to_broadcast([P, NE, NT]), ALU.is_gt))
            link(dve.tensor_reduce(n_tiles[:, :], more[:, :, :], AX.X, ALU.add))
            link(dve.tensor_tensor(mixed[:, :, :], up_to[:, :, :], n_tiles[:, :].unsqueeze(1).to_broadcast([P, NE, NE]), ALU.mult))
            link(dve.tensor_reduce(filled[:, :], mixed[:, :, :], AX.X, ALU.add))
            dve.tensor_scalar(kept.filled[:, :], filled[:, :], 1.0, None, ALU.add)
            link(dve.tensor_tensor(pads[:, :], filled[:, :], n_tiles[:, :], ALU.subtract))
            link(dve.scalar_tensor_tensor(out=pads[:, :], in0=pads[:, :], scalar=float(P), in1=base, op0=ALU.mult, op1=ALU.subtract))
            link(dve.tensor_tensor(rank[:, :, :], rank[:, :, :], pads[:, :].unsqueeze(1).to_broadcast([P, NT, NE]), ALU.add))
            for k in range(2):
                ins = dve.tensor_tensor(picked[:, k, :, :], hot[:, k, :, :], rank[:, :, :], ALU.mult)
            link(ins)
            link(dve.tensor_reduce(places[:, :, :], picked[:, :, :, :], AX.X, ALU.add))
            dve.tensor_copy(kept.outs[:, :, :], places[:, :, :])
            link(dve.tensor_scalar(last_tile[:, :], filled[:, NE - 1:NE], -1.0, None, ALU.add))
            link(dve.tensor_scalar(index[:, :], iota_t, last_tile[:, :], None, ALU.min))
            link(dve.tensor_tensor(passed[:, :, :], index[:, :].unsqueeze(2).to_broadcast([P, TABLE, NE]),
                                   filled[:, :].unsqueeze(1).to_broadcast([P, TABLE, NE]), ALU.is_ge))
            link(dve.tensor_reduce(row[:, 0, :], passed[:, :, :], AX.X, ALU.add))
            link(dve.tensor_tensor(scaled[:, :, :], passed[:, :, :], n_tiles[:, :].unsqueeze(1).to_broadcast([P, TABLE, NE]), ALU.mult))
            link(dve.tensor_reduce(row[:, 1, :], scaled[:, :, :], AX.X, ALU.add))
            link(dve.tensor_tensor(scaled[:, :, :], passed[:, :, :], swing[:, :].unsqueeze(1).to_broadcast([P, TABLE, NE]), ALU.mult))
            link(dve.tensor_reduce(row[:, 2, :], scaled[:, :, :], AX.X, ALU.add))
            link(dve.tensor_tensor(row[:, 1, :], index[:, :], row[:, 1, :], ALU.subtract))
            link(dve.tensor_scalar(row[:, 1, :], row[:, 1, :], float(P), None, ALU.mult))
            link(dve.scalar_tensor_tensor(out=row[:, 1, :], in0=row[:, 0, :], scalar=float(REGION), in1=row[:, 1, :],
                                          op0=ALU.mult, op1=ALU.add))
            dve.tensor_copy(kept.tiles[:, ROW, :], row[:, 1, :])
            dve.tensor_copy(kept.tiles[:, SLOT, :], row[:, 2, :])
            link(dve.tensor_tensor(row[:, 0, :], row[:, 0, :], row[:, 2, :], ALU.subtract))
            link(dve.tensor_scalar(kept.tiles[:, ROUND, :], row[:, 0, :], 0.5, 1.0, ALU.mult, ALU.add))

        @block.tensor
        def _(pe):
            pe.wait_ge(ident_ready, 1)
            pe.wait_ge(gate_in, 32)
            for t in range(NT + 1):
                if t < NT:
                    pe.wait_ge(h2_done, t + 1)
                    at_least(pe, turned_out, t - 1)
                    for c in range(DC):
                        mm = pe.transpose(ps_t[:, t % 2, c * P:(c + 1) * P], kept.h2[:, t, c * P:(c + 1) * P], ident[:, :])
                    mm.then_inc(turned, 1)
                if t > 0:
                    pe.wait_ge(turned_out, t)
                    for c in range(DC):
                        mm = pe.matmul(ps_l[:, t - 1, 0:NE], ht[:, (t - 1) % 2, c, :], gate[:, c, :],
                                       start=(c == 0), stop=(c == DC - 1))
                    mm.then_inc(logged, 1)
            pe.wait_ge(hot_done, 1)
            pe.wait_ge(consts_ready, 5)
            for k, m in enumerate((before, ones)):
                mm = pe.matmul(ps_r[:, k, :, 0:NE], m[:, :], both[:, :, :], start=True, stop=True)
            mm.then_inc(ranked, 1)


def experts(nc, kept, w_up_t, w_down_t, expert_rows, expert_out):
    NIC = NI // P
    PIECES = 2
    with ExitStack() as ctx:
        def sb(name, shape, dt=F32):
            return ctx.enter_context(nc.sbuf_tensor("d_" + name, shape, dt))

        def sem(name):
            return ctx.enter_context(nc.semaphore("d_" + name))

        ident = sb("ident", [P, P])
        raw = sb("raw", [P, 2, 2 * NI])
        wu = sb("wu", [P, 2, PIECES, DC, NI], BF16)
        wd = sb("wd", [P, 2, PIECES, NIC, D], BF16)
        xg = sb("xg", [P, 2, D])
        xp = sb("xp", [P, 2, PIECES, DC, P], BF16)
        g = sb("g", [P, 2, NI])
        gp = sb("gp", [P, 2, PIECES, NI], BF16)
        yo = sb("yo", [P, 2, D])
        ps_x = ctx.enter_context(nc.psum_tensor("d_ps_x", [P, 2, 512], F32))
        ps_u = ctx.enter_context(nc.psum_tensor("d_ps_u", [P, 2, 2, 512], F32))
        ps_y = ctx.enter_context(nc.psum_tensor("d_ps_y", [P, 2, 512], F32))

        zeroed, ident_ready = sem("zeroed"), sem("ident_ready")
        raw_in, w_step = sem("raw_in"), sem("w_step")
        w_ready = [sem("w_ready0"), sem("w_ready1")]
        x_in = [sem("x_in0"), sem("x_in1")]
        turned, x_split, upped, gelued, g_split, downed, y_ready = (
            sem("turned"), sem("x_split"), sem("upped"), sem("gelued"), sem("g_split"), sem("downed"), sem("y_ready"))
        x_high, g_high, pool_passed = sem("x_high"), sem("g_high"), sem("pool_passed")
        y_out = [sem("y_out0"), sem("y_out1")]

        def by_pairs_of_tiles(engine, step):
            for u in range(2):
                step(u, u)
            with engine.Fori(1, RUN_TILES // 2) as i:
                for u in range(2):
                    step(i * 2 + u, u)

        block = ctx.enter_context(nc.Block())

        @block.sync
        def _(sp):
            def row_of(t):
                return sp.value_load(kept.tiles[0:1, ROW, bass.ds(t, 1)], min_val=0, max_val=NE * REGION - P)

            def load(t, u):
                row = row_of(t)
                at_least(sp, turned, t - 1)
                sp.dma_start(xg[:, u, :], expert_rows[bass.ds(row, P), :]).then_inc(x_in[u], 16)

            def step(t, u):
                load(t + 2, u)
                sp.wait_ge(y_ready, t + 1)
                sp.dma_start(expert_out[bass.ds(t * P, P), :], yo[:, u, :]).then_inc(y_out[u], 16)

            for u in range(2):
                load(u, u)
            by_pairs_of_tiles(sp, step)
            for u in range(2):
                sp.wait_ge(y_out[u], 16 * (RUN_TILES // 2))
                sp.wait_ge(x_in[u], 16 * (RUN_TILES // 2 + 1))

        @block.gpsimd
        def _(pool):
            make_identity(pool, ident, zeroed, ident_ready)
            for e in range(NE):
                at_least(pool, w_step, 4 * e)
                pool.dma_start(raw[:, 0, :].rearrange("p (c n) -> p c n", c=DC),
                               w_up_t[e, :, :].rearrange("(c p) n -> p c n", p=P)).then_inc(raw_in, 16)
                pool.dma_start(raw[:, 1, :].rearrange("p (c n) -> p c n", c=NIC),
                               w_down_t[e, :, :].rearrange("(c p) n -> p c n", p=P)).then_inc(raw_in, 16)
                pool.wait_ge(raw_in, 32 * (e + 1))
                if e > 1:
                    pool.wait_ge(downed, pool.value_load(kept.filled[0:1, e - 2:e - 1], min_val=1, max_val=MAX_TILES + 1))
                    apart(pool, pool_passed)
                s = e % 2
                for k, w in enumerate((wu, wd)):
                    high, low = (w[:, s, i, :, :].rearrange("p c n -> p (c n)") for i in range(2))
                    pool.tensor_copy(high, raw[:, k, :]).then_inc(w_step, 1)
                    pool.wait_ge(w_step, 4 * e + 2 * k + 1)
                    pool.tensor_tensor(low, raw[:, k, :], high, ALU.subtract).then_inc(w_step, 1)
                pool.wait_ge(w_step, 4 * e + 4)
                pool.sem_inc(w_ready[s], 1)

        @block.scalar
        def _(act):
            def step(t, u):
                for j in range(2):
                    act.wait_ge(upped, t * 2 + j + 1)
                    at_least(act, g_split, (t - 2) * 2 + j + 1)
                    act.activation(g[:, u, j * 512:(j + 1) * 512], ps_u[:, u, j, :], ACT.Gelu).then_inc(gelued, 1)
                if not isinstance(t, int) or t > 0:
                    result(t - 1, 1 - u)

            def result(t, u):
                act.wait_ge(downed, t + 2)
                at_least(act, y_out[u], (t - u) * 8)
                act.activation(yo[:, u, :], ps_y[:, u, 0:D], ACT.Copy).then_inc(y_ready, 1)

            by_pairs_of_tiles(act, step)
            result(RUN_TILES - 1, 1)

        @block.vector
        def _(dve):
            def split_x(t, u):
                dve.wait_ge(turned, t + 1)
                at_least(dve, upped, (t - 1) * 2)
                dve.tensor_copy(xp[:, u, 0, :, :], ps_x[:, u, 0:D]).then_inc(x_high, 1)
                dve.wait_ge(x_high, t + 1)
                dve.tensor_tensor(xp[:, u, 1, :, :], ps_x[:, u, 0:D].rearrange("p (c n) -> p c n", c=DC), xp[:, u, 0, :, :], ALU.subtract).then_inc(x_split, 1)

            def step(t, u):
                split_x(t + 1, 1 - u)
                at_least(dve, downed, t)
                for j in range(2):
                    dve.wait_ge(gelued, t * 2 + j + 1)
                    dve.tensor_copy(gp[:, u, 0, j * 512:(j + 1) * 512], g[:, u, j * 512:(j + 1) * 512]).then_inc(g_high, 1)
                    dve.wait_ge(g_high, t * 2 + j + 1)
                    dve.tensor_tensor(gp[:, u, 1, j * 512:(j + 1) * 512], g[:, u, j * 512:(j + 1) * 512],
                                      gp[:, u, 0, j * 512:(j + 1) * 512], ALU.subtract).then_inc(g_split, 1)

            split_x(0, 0)
            by_pairs_of_tiles(dve, step)

        @block.tensor
        def _(pe):
            def turn(t, u):
                pe.wait_ge(x_in[u], (t - u) * 8 + 16)
                at_least(pe, x_split, t - 1)
                for c in range(DC):
                    mm = pe.transpose(ps_x[:, u, c * P:(c + 1) * P], xg[:, u, c * P:(c + 1) * P], ident[:, :])
                mm.then_inc(turned, 1)

            PRODUCTS = ((0, 0), (0, 1), (1, 0))

            def up(t, u, slot, rounds):
                pe.wait_ge(w_ready[slot], rounds)
                for j in range(NIC):
                    n = 0
                    for c in range(DC):
                        for w, x in PRODUCTS:
                            mm = pe.matmul(ps_u[:, u, j // 4, j % 4 * P:(j % 4 + 1) * P], wu[:, slot, w, c, j * P:(j + 1) * P],
                                           xp[:, u, x, c, :], start=(n == 0), stop=(n == 5))
                            n += 1
                    if j % 4 == 3:
                        mm.then_inc(upped, 1)

            def down(t, u, slot):
                n = 0
                for j in range(NIC):
                    for w, x in PRODUCTS:
                        mm = pe.matmul(ps_y[:, u, 0:D], gp[:, u, x, j * P:(j + 1) * P], wd[:, slot, w, j, :],
                                       start=(n == 0), stop=(n == 3 * NIC - 1))
                        n += 1
                mm.then_inc(downed, 1)

            def read(which, t, high):
                return pe.value_load(kept.tiles[0:1, which, bass.ds(t, 1)], min_val=0 if which == SLOT else 1, max_val=high)

            def by_slot(slot, body):
                with pe.If(slot == 0):
                    body(0)
                with pe.Else():
                    body(1)

            def down_step(t, u):
                slot = read(SLOT, t, 1)
                pe.wait_ge(g_split, t * 2 + 2)
                at_least(pe, y_ready, t - 1)
                by_slot(slot, lambda s: down(t, u, s))

            def step(t, u):
                slot, rounds = read(SLOT, t, 1), read(ROUND, t, NE // 2)
                turn(t + 1, 1 - u)
                pe.wait_ge(x_split, t + 1)
                at_least(pe, gelued, (t - 1) * 2)
                by_slot(slot, lambda s: up(t, u, s, rounds))
                if not isinstance(t, int) or t > 0:
                    down_step(t - 1, 1 - u)

            pe.wait_ge(ident_ready, 1)
            pe.sem_inc(downed, 1)
            turn(0, 0)
            by_pairs_of_tiles(pe, step)
            down_step(RUN_TILES - 1, 1)


def combine(nc, kept, expert_out, out):
    with ExitStack() as ctx:
        def sb(name, shape, dt=F32):
            return ctx.enter_context(nc.sbuf_tensor("e_" + name, shape, dt))

        def sem(name):
            return ctx.enter_context(nc.semaphore("e_" + name))

        y = sb("y", [P, 2, TB, 2, D])
        stats = sb("stats", [P, 2, TB, 6])
        mv = sb("mv", [P, 2, TB, 2])
        std = sb("std", [P, 2, TB])
        y_in = [[sem(f"y_in{u}{t}") for t in range(TB)] for u in range(2)]
        first, mixed, stats_done, mv_done, std_done, inverted = (
            sem("first"), sem("mixed"), sem("stats_done"), sem("mv_done"), sem("std_done"), sem("inverted"))
        normal, added, gated, done = sem("normal"), sem("added"), sem("gated"), sem("done")
        stored = [sem("stored0"), sem("stored1")]
        block = ctx.enter_context(nc.Block())

        @block.gpsimd
        def _(pool):
            for b in range(B):
                u = b % 2
                at_least(pool, stored[u], b // 2 * 16)
                for t in range(TB):
                    for k in range(2):
                        pool.indirect_dma_start(y[:, u, t, k, :], None, expert_out,
                                                bass.IndirectOffsetOnAxis(ap=kept.outs[:, k, b * TB + t:b * TB + t + 1], axis=0)
                                                ).then_inc(y_in[u][t], 16)

        @block.scalar
        def _(act):
            for b in range(B):
                act.wait_ge(mv_done, (b + 1) * TB)
                at_least(act, normal, (b - 1) * TB)
                act.activation(std[:, b % 2, :], mv[:, b % 2, :, 1], ACT.Sqrt, bias=kept.eps[:, :], scale=1.0).then_inc(std_done, 1)

        @block.vector
        def _(dve):
            def mix(b):
                u = b % 2
                for t in range(TB):
                    dve.wait_ge(y_in[u][t], (b // 2 + 1) * 32)
                    dve.tensor_scalar(y[:, u, t, 0, :], y[:, u, t, 0, :], kept.gates[:, 0, b * TB + t:b * TB + t + 1], None,
                                      ALU.mult).then_inc(first, 1)
                for t in range(TB):
                    dve.wait_ge(first, b * TB + t + 1)
                    dve.scalar_tensor_tensor(out=y[:, u, t, 0, :], in0=y[:, u, t, 1, :],
                                             scalar=kept.gates[:, 1, b * TB + t:b * TB + t + 1], in1=y[:, u, t, 0, :],
                                             op0=ALU.mult, op1=ALU.add).then_inc(mixed, 1)
                for t in range(TB):
                    dve.wait_ge(mixed, b * TB + t + 1)
                    dve.bn_stats(stats[:, u, t, :], y[:, u, t, 0, :]).then_inc(stats_done, 1)
                at_least(dve, std_done, b - 1)
                for t in range(TB):
                    dve.wait_ge(stats_done, b * TB + t + 1)
                    dve.bn_aggr(mv[:, u, t, :], stats[:, u, t, :]).then_inc(mv_done, 1)

            def finish(b):
                u = b % 2
                dve.wait_ge(std_done, b + 1)
                dve.reciprocal(std[:, u, :], std[:, u, :]).then_inc(inverted, 1)
                dve.wait_ge(inverted, b + 1)
                for t in range(TB):
                    dve.tensor_scalar(y[:, u, t, 0, :], y[:, u, t, 0, :], mv[:, u, t, 0:1], std[:, u, t:t + 1],
                                      ALU.subtract, ALU.mult).then_inc(normal, 1)
                for t in range(TB):
                    dve.wait_ge(normal, b * TB + t + 1)
                    dve.tensor_tensor(y[:, u, t, 0, :], y[:, u, t, 0, :], kept.h2[:, b * TB + t, :], ALU.add).then_inc(added, 1)
                for t in range(TB):
                    dve.wait_ge(added, b * TB + t + 1)
                    dve.tensor_tensor(y[:, u, t, 0, :], y[:, u, t, 0, :], kept.mod[:, b, 2 * D:3 * D], ALU.mult).then_inc(gated, 1)
                for t in range(TB):
                    dve.wait_ge(gated, b * TB + t + 1)
                    dve.tensor_tensor(y[:, u, t, 0, :], y[:, u, t, 0, :], kept.x1[:, b * TB + t, :], ALU.add).then_inc(done, 1)

            mix(0)
            for b in range(B):
                if b + 1 < B:
                    mix(b + 1)
                finish(b)

        @block.sync
        def _(sp):
            for b in range(B):
                sp.wait_ge(done, (b + 1) * TB)
                sp.dma_start(out[b, :, :].rearrange("(t p) d -> p t d", p=P), y[:, b % 2, :, 0, :]).then_inc(stored[b % 2], 16)
            for u in range(2):
                sp.wait_ge(stored[u], 16 * (B // 2))


def adaln_block(nc, x, w_qkv, b_qkv, w_out, b_out, rel_rev, gate_t, expert_bias, w_up_t, w_down_t, c_t, wmod, out):
    def scratch(name, shape, dt=F32):
        return nc.dram_tensor(name, shape, dt, kind="Internal").ap()

    mod_rows = scratch("mod_rows", (B, 6 * D))
    ext_rows = scratch("ext_rows", (NH, EXT))
    h1t = scratch("h1t", (B, P, DC, S))
    splits = scratch("splits", (B, 2, 2, PARTS, P, S), BF16)
    x1 = scratch("x1", (B, S, D))
    expert_rows = scratch("expert_rows", (NE * REGION, D))
    expert_out = scratch("expert_out", (RUN_TILES * P, D))
    prepare(nc, x, c_t, wmod, rel_rev, mod_rows, ext_rows, h1t)
    attention(nc, x, h1t, w_qkv, b_qkv, w_out, b_out, mod_rows, ext_rows, splits, x1)
    with ExitStack() as ctx:
        kept = Kept(nc, ctx)
        route(nc, kept, x1, mod_rows, gate_t, expert_bias, expert_rows)
        experts(nc, kept, w_up_t, w_down_t, expert_rows, expert_out)
        combine(nc, kept, expert_out, out)


def kernel(**inputs):
    import numpy as _np
    import concourse.bacc as _bacc
    from concourse.bass_utils import run_bass_kernel_spmd as _run

    a = {name: _np.asarray(value) for name, value in inputs.items()}
    given = {
        "x": a["L0_attn_x"],
        "w_qkv": a["L0_attn_W_qkv"],
        "b_qkv": a["L0_attn_b_qkv"],
        "w_out": a["L0_attn_W_out"],
        "b_out": a["L0_attn_b_out"],
        "rel_rev": a["L0_attn_rel_bias"].T[:, ::-1],
        "gate_t": a["L0_ffn_gate_w"].T,
        "expert_bias": a["L0_ffn_expert_bias"],
        "w_up_t": a["L0_ffn_w_up"].transpose(0, 2, 1),
        "w_down_t": a["L0_ffn_w_down"].transpose(0, 2, 1),
        "c_t": a["L0_c"].T,
        "wmod": a["L0_wmod"],
    }
    nc = _bacc.Bacc("TRN2", target_bir_lowering=False, num_devices=1)
    arrays, args = {}, {}
    for name, value in given.items():
        value = _np.ascontiguousarray(value)
        arrays[f"in_{name}"] = value
        args[name] = nc.dram_tensor(f"in_{name}", value.shape, mybir.dt.from_np(value.dtype), kind="ExternalInput").ap()
    out = nc.dram_tensor("out", (B, S, D), F32, kind="ExternalOutput").ap()
    adaln_block(nc, out=out, **args)
    r = _run(nc, [arrays], core_ids=[0])
    return r.results[0]["out"]
```

```python
from contextlib import ExitStack

import numpy as np

import concourse.bass as bass
from concourse import mybir

F32 = mybir.dt.float32
BF16 = mybir.dt.bfloat16
I32 = mybir.dt.int32
U32 = mybir.dt.uint32
ALU = mybir.AluOpType
ACT = mybir.ActivationFunctionType
AX = mybir.AxisListType

P = 128
B, S, D = 8, 512, 256
NH, DK = 16, 16
MAXREL = 256
NE, NI = 8, 1024
LN_EPS = 1e-5
GATE_EPS = 1e-6
TB = S // P
DC = D // P
NT = B * TB
ZW = S + (TB - 1) * P
EXT = ZW + P - 1
HALF = NH // 2
PARTS = 3
Q_PART = (0, 0, 1, 1, 0, 2)
K_PART = (0, 1, 0, 1, 2, 0)
KS = len(Q_PART) * DK
BIG = 3.0e38


def at_least(engine, semaphore, value):
    if not isinstance(value, int) or value > 0:
        engine.wait_ge(semaphore, value)


def by_pairs(engine, step):
    for u in range(2):
        step(u, u)
    with engine.Fori(1, B // 2) as i:
        for u in range(2):
            step(i * 2 + u, u)


def apart(engine, passed):
    engine.sem_inc(passed, 1)


def make_identity(pool, ident, zeroed, done):
    pool.memset(ident[:, :], 0.0).then_inc(zeroed, 1)
    pool.wait_ge(zeroed, 1)
    pool.affine_select(out=ident[:, :], in_=ident[:, :], compare_op=ALU.not_equal, fill=1.0, base=0,
                       pattern=[[-1, P]], channel_multiplier=1).then_inc(done, 1)


def prepare(nc, x, c_t, wmod, rel_rev, mod_rows, ext_rows, h1t):
    with ExitStack() as ctx:
        def sb(name, shape, dt=F32):
            return ctx.enter_context(nc.sbuf_tensor("a_" + name, shape, dt))

        def sem(name):
            return ctx.enter_context(nc.semaphore("a_" + name))

        ident = sb("ident", [P, P])
        ct = sb("ct", [P, DC, B])
        ct_e = sb("ct_e", [P, DC, B])
        silu = sb("silu", [P, DC, B])
        wm = sb("wm", [P, DC, 6 * D])
        rows = sb("rows", [B, 6 * D])
        sgn = sb("sgn", [B, 2, D])
        scale = sb("scale", [P, DC, B])
        shift = sb("shift", [P, DC, B])
        ext = sb("ext", [NH, EXT])
        xt = sb("xt", [P, 2, TB, D])
        stats = sb("stats", [P, 2, TB, 6])
        mv = sb("mv", [P, 2, TB, 2])
        std = sb("std", [P, 2, TB])
        rstd = sb("rstd", [P, 2, TB])
        xh = sb("xh", [P, 2, TB, D])
        ht = sb("ht", [P, 2, DC, S])
        ps_mod = ctx.enter_context(nc.psum_tensor("a_ps_mod", [P, 3, 512], F32))
        ps_col = ctx.enter_context(nc.psum_tensor("a_ps_col", [P, 512], F32))
        ps_t = ctx.enter_context(nc.psum_tensor("a_ps_t", [P, 2, DC, S], F32))

        eps = sb("eps", [P, 1])
        zeroed, ident_ready, eps_set = sem("zeroed"), sem("ident_ready"), sem("eps_set")
        dve_passed = sem("dve_passed")
        c_in, wm_in, rel_in = sem("c_in"), sem("wm_in"), sem("rel_in")
        exp_done, one_done, rec_done, silu_done = sem("exp_done"), sem("one_done"), sem("rec_done"), sem("silu_done")
        mod_ready, rows_copied, rows_step, rows_done = sem("mod_ready"), sem("rows_copied"), sem("rows_step"), sem("rows_done")
        cols_ready, ext_done, stored = sem("cols_ready"), sem("ext_done"), sem("stored")
        x_in = [sem("x_in0"), sem("x_in1")]
        stats_done, mv_done, std_done, rstd_done, xh_done = (
            sem("stats_done"), sem("mv_done"), sem("std_done"), sem("rstd_done"), sem("xh_done"))
        t_done, h_dve, h_act = sem("t_done"), sem("h_dve"), sem("h_act")
        h_out = [sem("h_out0"), sem("h_out1")]
        block = ctx.enter_context(nc.Block())

        @block.sync
        def _(sp):
            sp.dma_start(ct[:, :, :], c_t.rearrange("(c p) b -> p c b", p=P)).then_inc(c_in, 16)
            sp.dma_start(wm[:, :, :], wmod.rearrange("(c p) n -> p c n", p=P)).then_inc(wm_in, 16)
            sp.dma_start(ext[:, MAXREL - 1:3 * MAXREL], rel_rev).then_inc(rel_in, 16)

            def load(b, u):
                at_least(sp, xh_done, (b - 1) * TB)
                sp.dma_start(xt[:, u, :, :], x[bass.ds(b, 1), :, :].rearrange("b (t p) d -> p (b t) d", p=P)).then_inc(x_in[u], 16)

            by_pairs(sp, load)
            sp.wait_ge(rows_done, 1)
            sp.dma_start(mod_rows, rows[:, :]).then_inc(stored, 16)
            sp.wait_ge(ext_done, 2)
            sp.dma_start(ext_rows, ext[:, :]).then_inc(stored, 16)
            sp.wait_ge(stored, 32)

        @block.gpsimd
        def _(pool):
            make_identity(pool, ident, zeroed, ident_ready)
            def store(b, u):
                pool.wait_ge(h_dve, b + 1)
                pool.wait_ge(h_act, b + 1)
                pool.dma_start(h1t[bass.ds(b, 1), :, :, :].rearrange("b p c s -> (b p) c s"),
                               ht[:, u, :, :]).then_inc(h_out[u], 16)

            by_pairs(pool, store)
            for u in range(2):
                pool.wait_ge(h_out[u], 16 * (B // 2))

        @block.scalar
        def _(act):
            act.wait_ge(c_in, 16)
            act.activation(ct_e[:, :, :], ct[:, :, :], ACT.Exp, scale=-1.0).then_inc(exp_done, 1)
            act.wait_ge(eps_set, 1)

            def normalise(b, u):
                act.wait_ge(mv_done, (b + 1) * TB)
                at_least(act, rstd_done, b - 1)
                act.activation(std[:, u, :], mv[:, u, :, 1], ACT.Sqrt, bias=eps[:, :], scale=1.0).then_inc(std_done, 1)
                act.wait_ge(t_done, b + 1)
                act.wait_ge(cols_ready, 2)
                at_least(act, h_out[u], (b - u) * 8)
                act.activation(ht[:, u, 1, :], ps_t[:, u, 1, :], ACT.Identity, bias=shift[:, 1, bass.ds(b, 1)],
                               scale=scale[:, 1, bass.ds(b, 1)]).then_inc(h_act, 1)

            by_pairs(act, normalise)

        @block.vector
        def _(dve):
            dve.memset(eps[:, :], LN_EPS).then_inc(eps_set, 1)
            dve.wait_ge(exp_done, 1)
            dve.tensor_scalar(ct_e[:, :, :], ct_e[:, :, :], 1.0, None, ALU.add).then_inc(one_done, 1)
            dve.wait_ge(one_done, 1)
            dve.reciprocal(ct_e[:, :, :], ct_e[:, :, :]).then_inc(rec_done, 1)
            dve.wait_ge(rec_done, 1)
            dve.tensor_tensor(silu[:, :, :], ct[:, :, :], ct_e[:, :, :], ALU.mult).then_inc(silu_done, 1)
            dve.wait_ge(mod_ready, 1)
            dve.tensor_copy(shift[:, :, :], ps_col[:, 0:DC * B]).then_inc(cols_ready, 1)
            dve.tensor_scalar(scale[:, :, :], ps_col[:, DC * B:2 * DC * B], 1.0, None, ALU.add).then_inc(cols_ready, 1)
            dve.wait_ge(mod_ready, 2)
            dve.tensor_copy(rows[:, :], ps_mod[0:B, :, :]).then_inc(rows_copied, 1)
            dve.wait_ge(rows_copied, 1)
            for k, g in enumerate((2, 5)):
                dve.tensor_scalar(sgn[:, k, :], rows[:, g * D:(g + 1) * D], 0.0, 2.0, ALU.is_ge, ALU.mult).then_inc(rows_step, 1)
            for k, g in enumerate((1, 4)):
                dve.tensor_scalar(rows[:, g * D:(g + 1) * D], rows[:, g * D:(g + 1) * D], 1.0, None, ALU.add).then_inc(rows_step, 1)
            dve.wait_ge(rows_step, 4)
            dve.tensor_scalar(sgn[:, :, :], sgn[:, :, :], -1.0, None, ALU.add).then_inc(rows_step, 1)
            dve.wait_ge(rows_step, 5)
            for k, g in enumerate((2, 5)):
                dve.tensor_tensor(rows[:, g * D:(g + 1) * D], rows[:, g * D:(g + 1) * D], sgn[:, k, :], ALU.mult).then_inc(rows_step, 1)
            dve.wait_ge(rows_step, 7)
            for k, g in enumerate((2, 5)):
                last = dve.scalar_tensor_tensor(out=rows[:, g * D:(g + 1) * D], in0=rows[:, g * D:(g + 1) * D], scalar=0.25,
                                                in1=sgn[:, k, :], op0=ALU.max, op1=ALU.mult)
            last.then_inc(rows_done, 1)
            dve.wait_ge(rel_in, 16)
            dve.tensor_copy(ext[:, 0:MAXREL - 1], ext[:, MAXREL - 1:MAXREL].to_broadcast([NH, MAXREL - 1])).then_inc(ext_done, 1)
            dve.tensor_copy(ext[:, 3 * MAXREL:EXT], ext[:, 3 * MAXREL - 1:3 * MAXREL].to_broadcast([NH, EXT - 3 * MAXREL])).then_inc(ext_done, 1)

            def normalise(b, u):
                dve.wait_ge(x_in[u], (b - u) * 8 + 16)
                for t in range(TB):
                    dve.bn_stats(stats[:, u, t, :], xt[:, u, t, :]).then_inc(stats_done, 1)
                at_least(dve, std_done, b - 1)
                for t in range(TB):
                    dve.wait_ge(stats_done, b * TB + t + 1)
                    apart(dve, dve_passed)
                    dve.bn_aggr(mv[:, u, t, :], stats[:, u, t, :]).then_inc(mv_done, 1)
                dve.wait_ge(std_done, b + 1)
                dve.reciprocal(rstd[:, u, :], std[:, u, :]).then_inc(rstd_done, 1)
                dve.wait_ge(rstd_done, b + 1)
                at_least(dve, t_done, b - 1)
                for t in range(TB):
                    dve.tensor_scalar(xh[:, u, t, :], xt[:, u, t, :], mv[:, u, t, 0:1], rstd[:, u, t:t + 1],
                                      ALU.subtract, ALU.mult).then_inc(xh_done, 1)
                dve.wait_ge(t_done, b + 1)
                at_least(dve, h_out[u], (b - u) * 8)
                dve.tensor_scalar(ht[:, u, 0, :], ps_t[:, u, 0, :], scale[:, 0, bass.ds(b, 1)], shift[:, 0, bass.ds(b, 1)],
                                  ALU.mult, ALU.add).then_inc(h_dve, 1)

            by_pairs(dve, normalise)

        @block.tensor
        def _(pe):
            pe.wait_ge(silu_done, 1)
            pe.wait_ge(wm_in, 16)
            for j in range(2 * DC):
                for c in range(DC):
                    mm = pe.matmul(ps_col[:, j * B:(j + 1) * B], wm[:, c, j * P:(j + 1) * P], silu[:, c, :],
                                   start=(c == 0), stop=(c == DC - 1))
            mm.then_inc(mod_ready, 1)
            for j in range(3):
                for c in range(DC):
                    mm = pe.matmul(ps_mod[0:B, j, :], silu[:, c, :], wm[:, c, j * 512:(j + 1) * 512],
                                   start=(c == 0), stop=(c == DC - 1))
            mm.then_inc(mod_ready, 1)
            pe.wait_ge(ident_ready, 1)

            def turn(b, u):
                pe.wait_ge(xh_done, (b + 1) * TB)
                at_least(pe, h_dve, b - 1)
                at_least(pe, h_act, b - 1)
                for c in range(DC):
                    for t in range(TB):
                        mm = pe.transpose(ps_t[:, u, c, t * P:(t + 1) * P], xh[:, u, t, c * P:(c + 1) * P], ident[:, :])
                mm.then_inc(t_done, 1)

            by_pairs(pe, turn)


USES = ((1, "q0"), (2, "k0"), (3, "back3"), (4, "turn0"), (5, "turn1"), (6, "out0"), (7, "back0"), (8, "out1"),
        (9, "q1"), (10, "k1"), (11, "back1"), (12, "v0"), (13, "v1"), (15, "back2"))
FROM_BEFORE = ("back3", "turn0", "turn1", "out0", "out1")
FOR_NEXT = ("q0", "k0", "q1", "k1", "v0", "v1")


def attention(nc, x, h1t, w_qkv, b_qkv, w_out, b_out, mod_rows, ext_rows, splits, x1):
    GROUPS = NH // TB

    with ExitStack() as ctx:
        def sb(name, shape, dt=F32):
            return ctx.enter_context(nc.sbuf_tensor("b_" + name, shape, dt))

        def sem(name):
            return ctx.enter_context(nc.semaphore("b_" + name))

        ident = sb("ident", [P, P])
        flip = sb("flip", [P, P])
        bias = sb("bias", [P, NH, ZW])
        wqkv = sb("wqkv", [P, DC, 3 * D])
        wo = sb("wo", [P, DC, D])
        b_col = sb("b_col", [P, 4])
        b_v = sb("b_v", [P, D])
        b_o = sb("b_o", [P, D])
        h1 = sb("h1", [P, DC, S])
        qf = sb("qf", [P, 2, S])
        rest = sb("rest", [P, S])
        parts = sb("parts", [P, 2, PARTS, S], BF16)
        qs = sb("qs", [KS, 2, HALF, S], BF16)
        ks = sb("ks", [KS, 2, HALF, S], BF16)
        v_next = sb("v_next", [P, TB, D])
        v = sb("v", [P, TB, NH, 2 * DK])
        sn = sb("sn", [P, TB, S])
        mn = sb("mn", [P, 2, TB])
        pr = sb("pr", [P, 2, TB, S])
        pt = sb("pt", [P, 2, TB, S])
        ot = sb("ot", [P, S])
        inv = sb("inv", [P, TB, TB])
        on = sb("on", [P, TB, D])
        ont = sb("ont", [P, DC, S])
        xb = sb("xb", [P, TB, D])
        ga = sb("ga", [P, D])
        gab = sb("gab", [P, D])
        gated = sb("gated", [P, TB, D])
        ps_s = ctx.enter_context(nc.psum_tensor("b_ps_s", [P, 2, S], F32))
        ps_t = ctx.enter_context(nc.psum_tensor("b_ps_t", [P, TB, S], F32))
        ps_o = ctx.enter_context(nc.psum_tensor("b_ps_o", [P, S], F32))
        ps_m = ctx.enter_context(nc.psum_tensor("b_ps_m", [P, S], F32))

        flip_zeroed = sem("flip_zeroed")
        dve_passed, pool_passed, sp_passed = sem("dve_passed"), sem("pool_passed"), sem("sp_passed")
        zeroed, ident_ready, ones_set, bq_scaled = sem("zeroed"), sem("ident_ready"), sem("ones_set"), sem("bq_scaled")
        w_in, const_in, bq_in = sem("w_in"), sem("const_in"), sem("bq_in")
        bias_in = [sem(f"bias_in{g}") for g in range(GROUPS)]
        h1_in, x_in = sem("h1_in"), sem("x_in")
        parts_out = [sem("parts_out0"), sem("parts_out1")]
        stack_in = [sem("stack_in0"), sem("stack_in1")]
        scored, biased, exped = sem("scored"), sem("biased"), sem("exped")
        turned, out_dve, out_act, weighed = sem("turned"), sem("out_dve"), sem("out_act"), sem("weighed")
        ot_out, used, freed = sem("ot_out"), sem("used"), sem("freed")
        split_step, split_done, inv_done = sem("split_step"), sem("split_done"), sem("inv_done")
        v_moved, gab_done, xg_done, gated_done, x1_done, x1_out = (
            sem("v_moved"), sem("gab_done"), sem("xg_done"), sem("gated_done"), sem("x1_done"), sem("x1_out"))

        def uses_of(kind):
            return [(n, u) for n, u in USES
                    if not (kind == "first" and u in FROM_BEFORE) and not (kind == "last" and u in FOR_NEXT)]

        def uses_before(b, kind):
            return len(FOR_NEXT) if kind == "first" else len(FOR_NEXT) + len(uses_of("first")) + (b - 1) * len(USES)

        def use(b, kind, name):
            return uses_before(b, kind) + [u for _, u in uses_of(kind)].index(name)

        def end_use(name):
            return uses_before(B - 1, "last") + len(uses_of("last")) + FROM_BEFORE.index(name)

        def by_batches(engine, batch):
            batch(0, "first")
            with engine.Fori(1, B - 1) as b:
                batch(b, "middle")
            batch(B - 1, "last")

        block = ctx.enter_context(nc.Block())

        @block.sync
        def _(sp):
            def store_parts(b, k, name, k_done):
                of, half = (0 if name[0] == "q" else 1), int(name[1])
                sp.wait_ge(split_done, k_done)
                sp.dma_start(splits[bass.ds(b, 1), of, half, :, :, :].rearrange("b s p t -> p (b s) t"),
                             parts[:, k % 2, :, :]).then_inc(parts_out[k % 2], 16)

            def load_stack(b, half):
                for k in range(2):
                    sp.wait_ge(parts_out[k], b * 32 + half * 16 + 16)
                for stack, of, which in ((qs, 0, Q_PART), (ks, 1, K_PART)):
                    for g, part in enumerate(which):
                        sp.dma_start(stack[g * DK:(g + 1) * DK, half, :, :],
                                     splits[bass.ds(b, 1), of, half, part, :, :].rearrange("b (h d) t -> d (b h) t", d=DK)
                                     ).then_inc(stack_in[half], 16)

            def load_x(b):
                at_least(sp, x1_done, (b * 2))
                sp.dma_start(xb[:, :, :], x[bass.ds(b, 1), :, :].rearrange("b (t p) d -> p (b t) d", p=P)).then_inc(x_in, 16)
                sp.dma_start(ga[:, :], mod_rows[bass.ds(b, 1), 2 * D:3 * D].to_broadcast([P, D])).then_inc(x_in, 16)

            def store_x1(b, j):
                sp.wait_ge(x1_done, b * 2 + j + 1)
                sp.dma_start(x1[bass.ds(b, 1), 2 * j * P:2 * (j + 1) * P, :].rearrange("b (t p) d -> p (b t) d", p=P),
                             gated[:, 2 * j:2 * j + 2, :]).then_inc(x1_out, 16)

            sp.dma_start(wqkv[:, :, :], w_qkv.rearrange("(c p) n -> p c n", p=P)).then_inc(w_in, 16)
            sp.dma_start(b_col[:, :], b_qkv[0:2 * D].rearrange("(c p) -> p c", p=P),
                         allow_slow_non_contiguous=True).then_inc(bq_in, 16)
            sp.dma_start(b_v[:, :], b_qkv[2 * D:3 * D].rearrange("(a n) -> a n", a=1).to_broadcast([P, D])).then_inc(const_in, 16)
            sp.dma_start(b_o[:, :], b_out.rearrange("(a n) -> a n", a=1).to_broadcast([P, D])).then_inc(const_in, 16)
            sp.dma_start(wo[:, :, :], w_out.rearrange("(c p) n -> p c n", p=P)).then_inc(w_in, 16)
            for half in range(2):
                for h in range(half * HALF, (half + 1) * HALF):
                    skewed = bass.AP(ext_rows.tensor, h * EXT, [[1, P], [1, ZW]])
                    sp.dma_start(bias[:, h, :], skewed).then_inc(bias_in[h // TB], 16)
                for k in range(2 * half, 2 * half + 2):
                    store_parts(0, k, FOR_NEXT[k], k + 1)
                load_stack(0, half)

            def batch(b, kind):
                if kind != "first":
                    load_x(b - 1)
                if kind != "last":
                    for k in range(2):
                        store_parts(b + 1, k, FOR_NEXT[k], (b + 1) * 4 + k + 1)
                    sp.wait_ge(scored, (b * NH + HALF) * TB)
                    apart(sp, sp_passed)
                    load_stack(b + 1, 0)
                if kind != "first":
                    for j in range(2):
                        store_x1(b - 1, j)
                if kind != "last":
                    for k in range(2, 4):
                        store_parts(b + 1, k, FOR_NEXT[k], (b + 1) * 4 + k + 1)
                    sp.wait_ge(scored, (b + 1) * NH * TB)
                    apart(sp, sp_passed)
                    load_stack(b + 1, 1)

            by_batches(sp, batch)
            load_x(B - 1)
            for j in range(2):
                store_x1(B - 1, j)
            sp.wait_ge(x1_out, 16 * 2 * B)

        @block.gpsimd
        def _(pool):
            pool.dma_start(h1[:, :, :], h1t[0, :, :, :]).then_inc(h1_in, 16)
            make_identity(pool, ident, zeroed, ident_ready)
            pool.memset(flip[:, :], 0.0).then_inc(flip_zeroed, 1)
            pool.wait_ge(flip_zeroed, 1)
            pool.affine_select(out=flip[:, :], in_=flip[:, :], compare_op=ALU.not_equal, fill=1.0, base=1 - P,
                               pattern=[[1, P]], channel_multiplier=1).then_inc(ident_ready, 1)
            pool.memset(v[:, :, :, :], 0.0).then_inc(zeroed, 1)
            pool.wait_ge(zeroed, 2)
            pool.memset(v[:, :, :, DK:DK + 1], 1.0).then_inc(ones_set, 1)

            def load_h1(b, at):
                at_least(pool, used, at)
                pool.dma_start(h1[:, :, :], h1t[bass.ds(b, 1), :, :, :].rearrange("b p c s -> (b p) c s")).then_inc(h1_in, 16)

            def split(k, done, reads):
                pool.wait_ge(freed, reads)
                at_least(pool, parts_out[k % 2], (done - k % 2) * 8)
                out = parts[:, k % 2, :, :]
                apart(pool, pool_passed)
                pool.tensor_copy(out[:, 0, :], qf[:, k % 2, :]).then_inc(split_step, 1)
                pool.wait_ge(split_step, done * 3 + 1)
                pool.tensor_tensor(rest[:, :], qf[:, k % 2, :], out[:, 0, :], ALU.subtract).then_inc(split_step, 1)
                pool.wait_ge(split_step, done * 3 + 2)
                apart(pool, pool_passed)
                pool.tensor_copy(out[:, 1, :], rest[:, :]).then_inc(split_step, 1)
                pool.wait_ge(split_step, done * 3 + 3)
                pool.tensor_tensor(out[:, 2, :], rest[:, :], out[:, 1, :], ALU.subtract).then_inc(split_done, 1)
                pool.wait_ge(split_done, done + 1)

            def move_v(b, half, reads):
                pool.wait_ge(freed, reads)
                at_least(pool, weighed, (b - 1) * NH + (half + 1) * HALF)
                apart(pool, pool_passed)
                pool.tensor_copy(v[:, :, half * HALF:(half + 1) * HALF, 0:DK],
                                 v_next[:, :, half * P:(half + 1) * P].rearrange("p t (h d) -> p t h d", d=DK)).then_inc(v_moved, 1)

            def residual(b):
                pool.wait_ge(x_in, b * 32 + 32)
                at_least(pool, xg_done, b * TB)
                pool.tensor_tensor(gab[:, :], ga[:, :], b_o[:, :], ALU.mult).then_inc(gab_done, 1)
                pool.wait_ge(gab_done, b + 1)
                for t in range(TB):
                    pool.tensor_tensor(xb[:, t, :], xb[:, t, :], gab[:, :], ALU.add).then_inc(xg_done, 1)

            def add_x(b, j):
                pool.wait_ge(gated_done, b * 2 + j + 1)
                pool.wait_ge(xg_done, b * TB + TB)
                pool.tensor_tensor(gated[:, 2 * j:2 * j + 2, :], gated[:, 2 * j:2 * j + 2, :], xb[:, 2 * j:2 * j + 2, :],
                                   ALU.add).then_inc(x1_done, 1)

            for k in range(4):
                split(k, k, k + 1)
            pool.wait_ge(const_in, 32)
            pool.wait_ge(ones_set, 1)
            for half in range(2):
                move_v(0, half, len(FOR_NEXT))

            def batch(b, kind):
                if kind != "last":
                    load_h1(b + 1, uses_before(b, kind) - (kind == "middle"))
                if kind != "first":
                    residual(b - 1)
                if kind != "last":
                    split(0, (b + 1) * 4, use(b, kind, "q0") + 1)
                if kind != "first":
                    move_v(b, 1, uses_before(b, kind) - 1)
                if kind != "last":
                    split(1, (b + 1) * 4 + 1, use(b, kind, "k0") + 1)
                if kind != "first":
                    for j in range(2):
                        add_x(b - 1, j)
                if kind != "last":
                    for k in range(2, 4):
                        split(k, (b + 1) * 4 + k, use(b, kind, FOR_NEXT[k]) + 1)
                    move_v(b + 1, 0, use(b, kind, "v1") + 1)

            by_batches(pool, batch)
            residual(B - 1)
            for j in range(2):
                add_x(B - 1, j)

        @block.scalar
        def _(act):
            def project_out(name, done, at):
                c = ("q0", "q1", "k0", "k1").index(name)
                act.wait_ge(used, at + 1)
                at_least(act, split_done, done - 1)
                k = FOR_NEXT.index(name)
                tiles = ps_m[:, :].rearrange("p (t i) -> p t i", i=P)
                act.activation(qf[:, k % 2, :].rearrange("p (t i) -> p t i", i=P), tiles[:, :, ::-1] if name[0] == "q" else tiles,
                               ACT.Identity, bias=b_col[:, c:c + 1],
                               scale=(DK ** -0.5 if name[0] == "q" else 1.0)).then_inc(freed, 1)

            def exp(h, m, t):
                act.wait_ge(biased, h * TB + t + 1)
                act.activation(pr[:, m, t, :], sn[:, t, :], ACT.Exp, bias=mn[:, m, t:t + 1], scale=-1.0).then_inc(exped, 1)

            def evacuate(h, m):
                act.wait_ge(turned, h * 2 + 2)
                at_least(act, weighed, h - 1)
                act.activation(pt[:, m, 2:4, :], ps_t[:, 2:4, :], ACT.Copy).then_inc(out_act, 1)

            def turn_out(c, at):
                act.wait_ge(used, at + 1)
                act.activation(ont[:, c, :], ps_m[:, :], ACT.Copy).then_inc(freed, 1)

            def outputs(g, at):
                act.wait_ge(weighed, g * TB + TB)
                at_least(act, used, at)
                act.activation(ot[:, :], ps_o[:, :], ACT.Copy).then_inc(ot_out, 1)

            act.wait_ge(bq_scaled, 1)
            for k in range(4):
                project_out(FOR_NEXT[k], k, k)

            def batch(b, kind):
                for n in range(NH):
                    h = b * NH + n
                    at_least(act, turned, (h - 1) * 2)
                    exp(h, n % 2, 0)
                    exp(h, n % 2, 1)
                    for m, u in uses_of(kind):
                        if m == n and u in FOR_NEXT[:4]:
                            project_out(u, (b + 1) * 4 + FOR_NEXT.index(u), use(b, kind, u))
                        if m == n and u in ("turn0", "turn1"):
                            turn_out(int(u[4]), use(b, kind, u))
                    if kind != "first" or n > 0:
                        evacuate(h - 1, (n + 1) % 2)
                    exp(h, n % 2, 2)
                    exp(h, n % 2, 3)
                    if n == 1 and kind != "first":
                        outputs(b * GROUPS - 1, uses_before(b, kind))
                    if n in (5, 9, 13):
                        g = (n - 5) // TB
                        if g == 0:
                            outputs(b * GROUPS, 0 if kind == "first" else use(b, kind, "back3") + 1)
                        else:
                            outputs(b * GROUPS + g, use(b, kind, f"back{g - 1}") + 1)

            by_batches(act, batch)
            evacuate(B * NH - 1, 1)
            outputs(B * GROUPS - 1, uses_before(B - 1, "last") + len(uses_of("last")))
            for c in range(DC):
                turn_out(c, end_use(f"turn{c}"))

        @block.vector
        def _(dve):
            dve.wait_ge(bq_in, 16)
            dve.tensor_scalar(b_col[:, 0:2], b_col[:, 0:2], DK ** -0.5, None, ALU.mult).then_inc(bq_scaled, 1)
            dve.wait_ge(const_in, 32)

            def add_bias(b, n, t):
                k = (b * NH + n) * TB + t
                dve.wait_ge(scored, k + 1)
                at_least(dve, exped, k - TB + 1)
                apart(dve, dve_passed)
                at = (TB - 1 - t) * P
                dve.tensor_tensor_reduce(sn[:, t, :], ps_s[:, t % 2, :], bias[:, n, at:at + S], -1.0, BIG, ALU.add, ALU.min,
                                         mn[:, n % 2, t:t + 1]).then_inc(biased, 1)

            def evacuate(h, m):
                dve.wait_ge(turned, h * 2 + 1)
                at_least(dve, weighed, h - 1)
                dve.tensor_copy(pt[:, m, 0:2, :], ps_t[:, 0:2, :]).then_inc(out_dve, 1)

            def values(b, j, at):
                dve.wait_ge(used, at + 1)
                at_least(dve, v_moved, b * 2)
                dve.tensor_tensor(v_next[:, 2 * j:2 * j + 2, :], ps_m[:, :].rearrange("p (t n) -> p t n", n=D),
                                  b_v[:, :].unsqueeze(1).to_broadcast([P, 2, D]), ALU.add).then_inc(freed, 1)

            def back(b, g, at):
                dve.wait_ge(used, at + 1)
                turned_back = ps_m[:, :].rearrange("p (h t w) -> p h t w", h=TB, t=TB)
                dve.reciprocal(inv[:, :, :], turned_back[:, :, :, DK]).then_inc(inv_done, 1)
                dve.wait_ge(inv_done, b * GROUPS + g + 1)
                dve.tensor_tensor(on[:, :, g * TB * DK:(g + 1) * TB * DK].rearrange("p t (h d) -> p h t d", d=DK),
                                  turned_back[:, :, :, 0:DK], inv[:, :, :].unsqueeze(3).to_broadcast([P, TB, TB, DK]),
                                  ALU.mult).then_inc(freed, 1)

            def gate(b, j, at):
                dve.wait_ge(used, at + 1)
                dve.wait_ge(x_in, b * 32 + 32)
                at_least(dve, x1_out, b * 32)
                dve.tensor_tensor(gated[:, 2 * j:2 * j + 2, :], ps_m[:, :].rearrange("p (t n) -> p t n", n=D),
                                  ga[:, :].unsqueeze(1).to_broadcast([P, 2, D]), ALU.mult).then_inc(freed, 1)
                dve.wait_ge(freed, at + 1)
                dve.sem_inc(gated_done, 1)

            for j in range(2):
                values(0, j, 4 + j)

            def batch(b, kind):
                for n in range(NH):
                    if kind == "first" and n % TB == 0:
                        dve.wait_ge(bias_in[n // TB], 16 * TB)
                    add_bias(b, n, 0)
                    add_bias(b, n, 1)
                    for m, u in uses_of(kind):
                        if m == n and u == "back3":
                            back(b - 1, 3, use(b, kind, u))
                        elif m == n and u[:4] == "back":
                            back(b, int(u[4]), use(b, kind, u))
                        elif m == n and u[:3] == "out":
                            gate(b - 1, int(u[3]), use(b, kind, u))
                        elif m == n and u[0] == "v":
                            values(b + 1, int(u[1]), use(b, kind, u))
                    if kind != "first" or n > 0:
                        evacuate(b * NH + n - 1, (n + 1) % 2)
                    add_bias(b, n, 2)
                    add_bias(b, n, 3)

            by_batches(dve, batch)
            evacuate(B * NH - 1, 1)
            back(B - 1, 3, end_use("back3"))
            for j in range(2):
                gate(B - 1, j, end_use(f"out{j}"))

        @block.tensor
        def _(pe):
            def score(b, n, t):
                k = (b * NH + n) * TB + t
                at_least(pe, biased, k - 1)
                half, m = n // HALF, n % HALF
                pe.matmul(ps_s[:, t % 2, :], qs[:, half, m, t * P:(t + 1) * P], ks[:, half, m, :],
                          start=True, stop=True).then_inc(scored, 1)

            def turn_probabilities(h, m, pair):
                at_least(pe, out_act if pair else out_dve, h)
                for j in (2 * pair, 2 * pair + 1):
                    for t in range(TB):
                        mm = pe.transpose(ps_t[:, j, t * P:(t + 1) * P], pr[:, m, t, j * P:(j + 1) * P], ident[:, :])
                mm.then_inc(turned, 1)

            def weigh(b, n):
                h = b * NH + n
                pe.wait_ge(out_dve, h + 1)
                pe.wait_ge(out_act, h + 1)
                if n % HALF == 0:
                    pe.wait_ge(v_moved, b * 2 + n // HALF + 1)
                if n % TB == 0:
                    at_least(pe, ot_out, b * GROUPS + n // TB)
                for j in range(TB):
                    for t in range(TB):
                        mm = pe.matmul(ps_o[2 * DK * t:2 * DK * (t + 1), n % TB * P:(n % TB + 1) * P], v[:, j, n, :],
                                       pt[:, n % 2, j, t * P:(t + 1) * P], start=(j == 0), stop=(j == TB - 1))
                mm.then_inc(weighed, 1)

            def project(b, name, at):
                at_least(pe, freed, at)
                pe.wait_ge(h1_in, b * 16 + 16)
                if name[0] == "v":
                    for t in range(2):
                        for c in range(DC):
                            j = 2 * int(name[1]) + t
                            mm = pe.matmul(ps_m[:, t * D:(t + 1) * D], h1[:, c, j * P:(j + 1) * P], wqkv[:, c, 2 * D:3 * D],
                                           start=(c == 0), stop=(c == DC - 1))
                else:
                    col = ("q0", "q1", "k0", "k1").index(name) * P
                    for c in range(DC):
                        mm = pe.matmul(ps_m[:, :], wqkv[:, c, col:col + P], h1[:, c, :], start=(c == 0), stop=(c == DC - 1))
                mm.then_inc(used, 1)

            def back(g, at):
                pe.wait_ge(ot_out, g + 1)
                at_least(pe, freed, at)
                for i in range(TB):
                    mm = pe.transpose(ps_m[:, i * P:(i + 1) * P], ot[:, i * P:(i + 1) * P], ident[:, :])
                mm.then_inc(used, 1)

            def turn_outputs(c, at):
                at_least(pe, freed, at)
                for t in range(TB):
                    mm = pe.transpose(ps_m[:, t * P:(t + 1) * P], on[:, t, c * P:(c + 1) * P], flip[:, :])
                mm.then_inc(used, 1)

            def project_outputs(j, at):
                at_least(pe, freed, at)
                for t in range(2):
                    for c in range(DC):
                        mm = pe.matmul(ps_m[:, t * D:(t + 1) * D], ont[:, c, (2 * j + t) * P:(2 * j + t + 1) * P], wo[:, c, :],
                                       start=(c == 0), stop=(c == DC - 1))
                mm.then_inc(used, 1)

            pe.wait_ge(w_in, 32)
            for k, name in enumerate(FOR_NEXT):
                project(0, name, k)
            pe.wait_ge(ident_ready, 2)

            def batch(b, kind):
                for n in range(NH):
                    h = b * NH + n
                    if n % HALF == 0:
                        pe.wait_ge(stack_in[n // HALF], (b + 1) * 32 * len(Q_PART))
                    score(b, n, 0)
                    score(b, n, 1)
                    for m, u in uses_of(kind):
                        at = use(b, kind, u)
                        if m == n and u in FOR_NEXT:
                            project(b + 1, u, at)
                        elif m == n and u == "back3":
                            back(b * GROUPS - 1, at)
                        elif m == n and u[:4] == "back":
                            back(b * GROUPS + int(u[4]), at)
                        elif m == n and u[:4] == "turn":
                            turn_outputs(int(u[4]), at)
                        elif m == n:
                            project_outputs(int(u[3]), at)
                    if kind != "first" or n > 0:
                        pe.wait_ge(exped, h * TB)
                        turn_probabilities(h - 1, (n + 1) % 2, 0)
                        score(b, n, 2)
                        turn_probabilities(h - 1, (n + 1) % 2, 1)
                    else:
                        score(b, n, 2)
                    score(b, n, 3)
                    if n > 1:
                        weigh(b, n - 2)
                    elif kind != "first":
                        weigh(b - 1, n + NH - 2)

            by_batches(pe, batch)
            pe.wait_ge(exped, B * NH * TB)
            for pair in range(2):
                turn_probabilities(B * NH - 1, 1, pair)
            weigh(B - 1, NH - 2)
            weigh(B - 1, NH - 1)
            back(B * GROUPS - 1, end_use("back3"))
            for c in range(DC):
                turn_outputs(c, end_use(f"turn{c}"))
            for j in range(2):
                project_outputs(j, end_use(f"out{j}"))


TT = 2
ROWS = TT * P
REGION = B * S + ROWS
MAX_TILES = 2 * B * S // ROWS + NE - 1
NIC = NI // P
PIECES = 2
RUN_TILES = MAX_TILES + MAX_TILES % 2
TABLE = RUN_TILES + 2
ROW, SLOT, EXPERT = range(3)
STEPS = B * S // ROWS


def load_weights(engine, kept, w_up_t, w_down_t, e, done):
    engine.dma_start(kept.raw[:, 0, :].rearrange("p (c n) -> p c n", c=DC),
                     w_up_t[e, :, :].rearrange("(c p) n -> p c n", p=P)).then_inc(done, 16)
    engine.dma_start(kept.raw[:, 1, :].rearrange("p (c n) -> p c n", c=NIC),
                     w_down_t[e, :, :].rearrange("(c p) n -> p c n", p=P)).then_inc(done, 16)


def halves(kept, k, slot):
    return ((kept.wu, kept.wd)[k][:, slot, i, :, :].rearrange("p c n -> p (c n)") for i in range(2))


class Kept:

    def __init__(self, nc, ctx):
        def sb(name, shape, dt=F32):
            return ctx.enter_context(nc.sbuf_tensor("k_" + name, shape, dt))

        self.x1 = sb("x1", [P, NT, D])
        self.h2 = sb("h2", [P, NT, D])
        self.mod = sb("mod", [P, B, 3 * D])
        self.eps = sb("eps", [P, 1])
        self.gates = sb("gates", [P, 2, NT])
        self.rows = sb("rows", [P, 2, NT], U32)
        self.outs = sb("outs", [P, 2, NT], U32)
        self.tiles = sb("tiles", [P, 3, TABLE], I32)
        self.filled = sb("filled", [P, NE], I32)
        self.raw = sb("raw", [P, 2, 2 * NI])
        self.wu = sb("wu", [P, 2, PIECES, DC, NI], BF16)
        self.wd = sb("wd", [P, 2, PIECES, NIC, D], BF16)


def route(nc, kept, x1, mod_rows, gate_t, expert_bias, w_up_t, w_down_t, expert_rows):
    AHEAD = 4
    with ExitStack() as ctx:
        def sb(name, shape, dt=F32):
            return ctx.enter_context(nc.sbuf_tensor("c_" + name, shape, dt))

        def sem(name):
            return ctx.enter_context(nc.semaphore("c_" + name))

        ident = sb("ident", [P, P])
        before = sb("before", [P, P], BF16)
        ones = sb("ones", [P, P], BF16)
        up_to = sb("up_to", [P, NE, NE])
        ints = sb("ints", [P, 2 * NE + STEPS + TABLE], I32)
        nums = sb("nums", [P, 2 * NE + STEPS + TABLE])
        zero = sb("zero", [P, TT, D])
        swing = sb("swing", [P, NE])
        gate = sb("gate", [P, DC, NE])
        e_bias = sb("e_bias", [P, NE])
        stats = sb("stats", [P, NT, 6])
        mv = sb("mv", [P, NT, 2])
        std = sb("std", [P, NT])
        less = sb("less", [P, NT])
        ht = sb("ht", [P, 2, DC, P])
        logits = sb("logits", [P, NT, NE])
        weights = sb("weights", [P, NT, NE])
        per_tok = sb("per_tok", [P, 4, NT])
        top = sb("top", [P, NT, 8])
        top_i = sb("top_i", [P, NT, 8], U32)
        top_f = sb("top_f", [P, NT, 2])
        hot = sb("hot", [P, 2, NT, NE])
        both = sb("both", [P, NT, NE], BF16)
        run = sb("run", [P, 2, NT, NE])
        rank = sb("rank", [P, NT, NE])
        picked = sb("picked", [P, 2, NT, NE])
        places = sb("places", [P, 2, NT])
        more = sb("more", [P, NE, STEPS])
        n_tiles = sb("n_tiles", [P, NE])
        mixed = sb("mixed", [P, NE, NE])
        filled = sb("filled", [P, NE])
        last_tile = sb("last_tile", [P, 1])
        index = sb("index", [P, TABLE])
        passed = sb("passed", [P, TABLE, NE])
        scaled = sb("scaled", [P, TABLE, NE])
        row = sb("row", [P, 4, TABLE])
        pads = sb("pads", [P, NE])
        pads_i = sb("pads_i", [P, NE], I32)
        ps_t = ctx.enter_context(nc.psum_tensor("c_ps_t", [P, 2, 512], F32))
        ps_l = ctx.enter_context(nc.psum_tensor("c_ps_l", [P, NT, 2 * NE], F32))
        ps_r = ctx.enter_context(nc.psum_tensor("c_ps_r", [P, 2, NT, 2 * NE], F32))
        iota_e, base, steps, iota_t = (
            nums[:, 0:NE], nums[:, NE:2 * NE], nums[:, 2 * NE:2 * NE + STEPS],
            nums[:, 2 * NE + STEPS:])

        zeroed, ident_ready, consts_ready, pool_step = sem("zeroed"), sem("ident_ready"), sem("consts_ready"), sem("pool_step")
        x1_in, mod_in, gate_in = [sem(f"x1_in{i}") for i in range(B)], sem("mod_in"), sem("gate_in")
        stats_done, mv_done, std_done, eps_set = sem("stats_done"), sem("mv_done"), sem("std_done"), sem("eps_set")
        less_done, xh_done, scaled_done, h2_done = sem("less_done"), sem("xh_done"), sem("scaled_done"), sem("h2_done")
        turned, turned_out, logged = sem("turned"), sem("turned_out"), sem("logged")
        shifted, exped, hot_done, ranked, placed = sem("shifted"), sem("exped"), sem("hot_done"), sem("ranked"), sem("placed")
        chained, scattered, padded = sem("chained"), sem("scattered"), sem("padded")
        raw_in, high_done, low_done = sem("raw_in"), sem("high_done"), sem("low_done")
        block = ctx.enter_context(nc.Block())

        @block.sync
        def _(sp):
            for b in range(B):
                sp.dma_start(kept.x1[:, b * TB:(b + 1) * TB, :], x1[b, :, :].rearrange("(t p) d -> p t d", p=P)).then_inc(x1_in[b], 16)
            sp.dma_start(kept.mod[:, :, :], mod_rows[:, 3 * D:6 * D].unsqueeze(0).to_broadcast([P, B, 3 * D])).then_inc(mod_in, 16)
            sp.dma_start(gate[:, :, :], gate_t.rearrange("(c p) e -> p c e", p=P)).then_inc(gate_in, 16)
            sp.dma_start(e_bias[:, :], expert_bias.rearrange("(a e) -> a e", a=1).to_broadcast([P, NE])).then_inc(gate_in, 16)
            load_weights(sp, kept, w_up_t, w_down_t, 0, raw_in)
            sp.wait_ge(placed, 1)
            sp.wait_ge(consts_ready, 5)
            for e in range(NE):
                row = sp.value_load(pads_i[0:1, e:e + 1], min_val=0, max_val=NE * REGION - ROWS)
                sp.dma_start(expert_rows[bass.ds(row, ROWS), :].rearrange("(t p) d -> p t d", p=P), zero[:, :, :]).then_inc(padded, 16)
            sp.wait_ge(low_done, 2)
            load_weights(sp, kept, w_up_t, w_down_t, 1, raw_in)
            sp.wait_ge(padded, 16 * NE)

        @block.gpsimd
        def _(pool):
            make_identity(pool, ident, zeroed, ident_ready)
            pool.memset(before[:, :], 1.0).then_inc(pool_step, 1)
            pool.memset(up_to[:, :, :], 1.0).then_inc(pool_step, 1)
            pool.memset(ones[:, :], 1.0).then_inc(consts_ready, 1)
            pool.memset(zero[:, :, :], 0.0).then_inc(consts_ready, 1)
            for at, n, step in ((0, NE, 1), (NE, NE, REGION), (2 * NE, STEPS, ROWS), (2 * NE + STEPS, TABLE, 1)):
                pool.iota(ints[:, at:at + n], pattern=[[step, n]], base=0, channel_multiplier=0).then_inc(pool_step, 1)
            pool.wait_ge(pool_step, 6)
            pool.tensor_copy(nums[:, :], ints[:, :]).then_inc(consts_ready, 1)
            pool.affine_select(out=before[:, :], in_=before[:, :], compare_op=ALU.is_gt, fill=0.0, base=0,
                               pattern=[[1, P]], channel_multiplier=-1).then_inc(consts_ready, 1)
            pool.affine_select(out=up_to[:, :, :], in_=up_to[:, :, :], compare_op=ALU.is_ge, fill=0.0, base=0,
                               pattern=[[1, NE], [-1, NE]], channel_multiplier=0).then_inc(consts_ready, 1)
            pool.wait_ge(mod_in, 16)
            for t in range(NT):
                pool.wait_ge(scaled_done, t + 1)
                pool.tensor_tensor(kept.h2[:, t, :], kept.h2[:, t, :], kept.mod[:, t // TB, 0:D], ALU.add).then_inc(h2_done, 1)
            pool.wait_ge(placed, 1)
            pool.wait_ge(h2_done, NT)
            for t in range(NT):
                for k in range(2):
                    pool.indirect_dma_start(expert_rows, bass.IndirectOffsetOnAxis(ap=kept.rows[:, k, t:t + 1], axis=0),
                                            kept.h2[:, t, :], None).then_inc(scattered, 16)
            pool.wait_ge(scattered, 16 * 2 * NT)

        @block.scalar
        def _(act):
            act.wait_ge(eps_set, 1)
            act.wait_ge(mv_done, NT)
            act.activation(std[:, :], mv[:, :, 1], ACT.Sqrt, bias=kept.eps[:, :], scale=1.0).then_inc(std_done, 1)
            act.wait_ge(less_done, 1)
            for n in range(NT + AHEAD):
                if n < NT:
                    act.activation(kept.h2[:, n, :], kept.x1[:, n, :], ACT.Identity, bias=less[:, n:n + 1],
                                   scale=std[:, n:n + 1]).then_inc(xh_done, 1)
                t = n - AHEAD
                if t < 0:
                    continue
                act.wait_ge(turned, t + 1)
                at_least(act, logged, t - 1)
                act.activation(ht[:, t % 2, :, :], ps_t[:, t % 2, 0:D], ACT.Copy).then_inc(turned_out, 1)
            act.wait_ge(shifted, 1)
            act.activation(weights[:, :, :], logits[:, :, :], ACT.Exp).then_inc(exped, 1)
            for e in range(2):
                act.wait_ge(raw_in, 32 * (e + 1))
                for k in range(2):
                    high, _ = halves(kept, k, e)
                    act.activation(high, kept.raw[:, k, :], ACT.Copy).then_inc(high_done, 1)

        @block.vector
        def _(dve):
            count = [0]

            def link(ins):
                count[0] += 1
                ins.then_inc(chained, 1)
                dve.wait_ge(chained, count[0])

            dve.memset(kept.eps[:, :], LN_EPS).then_inc(eps_set, 1)
            dve.memset(swing[:, 0:NE:2], 1.0)
            link(dve.memset(swing[:, 1:NE:2], -1.0))
            for t in range(NT):
                if t % TB == 0:
                    dve.wait_ge(x1_in[t // TB], 16)
                dve.bn_stats(stats[:, t, :], kept.x1[:, t, :]).then_inc(stats_done, 1)
            for t in range(NT):
                dve.wait_ge(stats_done, t + 1)
                dve.bn_aggr(mv[:, t, :], stats[:, t, :]).then_inc(mv_done, 1)
            dve.wait_ge(std_done, 1)
            link(dve.reciprocal(std[:, :], std[:, :]))
            dve.scalar_tensor_tensor(out=less[:, :], in0=mv[:, :, 0], scalar=-1.0, in1=std[:, :],
                                     op0=ALU.mult, op1=ALU.mult).then_inc(less_done, 1)
            dve.wait_ge(mod_in, 16)
            for t in range(NT):
                dve.wait_ge(xh_done, t + 1)
                dve.tensor_tensor(kept.h2[:, t, :], kept.h2[:, t, :], kept.mod[:, t // TB, D:2 * D], ALU.mult).then_inc(scaled_done, 1)

            dve.wait_ge(logged, NT)
            dve.wait_ge(gate_in, 32)
            link(dve.tensor_tensor(logits[:, :, :], ps_l[:, :, 0:NE], e_bias[:, :].unsqueeze(1).to_broadcast([P, NT, NE]), ALU.add))
            link(dve.tensor_reduce(per_tok[:, 0, :], logits[:, :, :], AX.X, ALU.max))
            dve.tensor_tensor(logits[:, :, :], logits[:, :, :], per_tok[:, 0, :].unsqueeze(2).to_broadcast([P, NT, NE]),
                              ALU.subtract).then_inc(shifted, 1)
            dve.wait_ge(exped, 1)
            link(dve.tensor_reduce(per_tok[:, 1, :], weights[:, :, :], AX.X, ALU.add))
            link(dve.reciprocal(per_tok[:, 2, :], per_tok[:, 1, :]))
            link(dve.tensor_tensor(weights[:, :, :], weights[:, :, :], per_tok[:, 2, :].unsqueeze(2).to_broadcast([P, NT, NE]), ALU.mult))
            for t in range(NT):
                ins = dve.max(top[:, t, :], weights[:, t, :])
            link(ins)
            for t in range(NT):
                ins = dve.max_index(top_i[:, t, :], top[:, t, :], weights[:, t, :])
            link(ins)
            link(dve.tensor_tensor(per_tok[:, 3, :], top[:, :, 0], top[:, :, 1], ALU.add))
            link(dve.tensor_scalar(per_tok[:, 3, :], per_tok[:, 3, :], GATE_EPS, None, ALU.add))
            link(dve.reciprocal(per_tok[:, 3, :], per_tok[:, 3, :]))
            for k in range(2):
                dve.tensor_tensor(kept.gates[:, k, :], top[:, :, k], per_tok[:, 3, :], ALU.mult)
            link(dve.tensor_copy(top_f[:, :, :], top_i[:, :, 0:2]))
            dve.wait_ge(consts_ready, 5)
            for k in range(2):
                ins = dve.tensor_tensor(hot[:, k, :, :], iota_e.unsqueeze(1).to_broadcast([P, NT, NE]),
                                        top_f[:, :, k:k + 1].to_broadcast([P, NT, NE]), ALU.is_equal)
            link(ins)
            dve.tensor_tensor(both[:, :, :], hot[:, 0, :, :], hot[:, 1, :, :], ALU.add).then_inc(hot_done, 1)
            dve.wait_ge(ranked, 1)
            link(dve.tensor_copy(run[:, 0, :, :], ps_r[:, 1, :, 0:NE]))
            a, shift = 0, 1
            while shift < NT:
                dve.tensor_copy(run[:, 1 - a, 0:shift, :], run[:, a, 0:shift, :])
                link(dve.tensor_tensor(run[:, 1 - a, shift:NT, :], run[:, a, shift:NT, :], run[:, a, 0:NT - shift, :], ALU.add))
                a, shift = 1 - a, 2 * shift
            counts = run[:, a, NT - 1, :]
            link(dve.tensor_tensor(rank[:, :, :], run[:, a, :, :], ps_r[:, 1, :, 0:NE], ALU.subtract))
            link(dve.tensor_tensor(rank[:, :, :], rank[:, :, :], ps_r[:, 0, :, 0:NE], ALU.add))
            link(dve.tensor_tensor(rank[:, :, :], rank[:, :, :], base.unsqueeze(1).to_broadcast([P, NT, NE]), ALU.add))
            for k in range(2):
                ins = dve.tensor_tensor(picked[:, k, :, :], hot[:, k, :, :], rank[:, :, :], ALU.mult)
            link(ins)
            link(dve.tensor_reduce(places[:, :, :], picked[:, :, :, :], AX.X, ALU.add))
            dve.tensor_copy(kept.rows[:, :, :], places[:, :, :])
            link(dve.tensor_tensor(pads_i[:, :], counts, base, ALU.add))
            dve.sem_inc(placed, 1)
            link(dve.tensor_tensor(more[:, :, :], counts.unsqueeze(2).to_broadcast([P, NE, STEPS]),
                                   steps.unsqueeze(1).to_broadcast([P, NE, STEPS]), ALU.is_gt))
            link(dve.tensor_reduce(n_tiles[:, :], more[:, :, :], AX.X, ALU.add))
            link(dve.tensor_tensor(mixed[:, :, :], up_to[:, :, :], n_tiles[:, :].unsqueeze(1).to_broadcast([P, NE, NE]), ALU.mult))
            link(dve.tensor_reduce(filled[:, :], mixed[:, :, :], AX.X, ALU.add))
            dve.tensor_scalar(kept.filled[:, :], filled[:, :], 1.0, None, ALU.add)
            link(dve.tensor_tensor(pads[:, :], filled[:, :], n_tiles[:, :], ALU.subtract))
            link(dve.scalar_tensor_tensor(out=pads[:, :], in0=pads[:, :], scalar=float(ROWS), in1=base, op0=ALU.mult, op1=ALU.subtract))
            link(dve.tensor_tensor(rank[:, :, :], rank[:, :, :], pads[:, :].unsqueeze(1).to_broadcast([P, NT, NE]), ALU.add))
            for k in range(2):
                ins = dve.tensor_tensor(picked[:, k, :, :], hot[:, k, :, :], rank[:, :, :], ALU.mult)
            link(ins)
            link(dve.tensor_reduce(places[:, :, :], picked[:, :, :, :], AX.X, ALU.add))
            dve.tensor_copy(kept.outs[:, :, :], places[:, :, :])
            link(dve.tensor_scalar(last_tile[:, :], filled[:, NE - 1:NE], -1.0, None, ALU.add))
            link(dve.tensor_scalar(index[:, :], iota_t, last_tile[:, :], None, ALU.min))
            link(dve.tensor_tensor(passed[:, :, :], index[:, :].unsqueeze(2).to_broadcast([P, TABLE, NE]),
                                   filled[:, :].unsqueeze(1).to_broadcast([P, TABLE, NE]), ALU.is_ge))
            link(dve.tensor_reduce(row[:, 0, :], passed[:, :, :], AX.X, ALU.add))
            link(dve.tensor_tensor(scaled[:, :, :], passed[:, :, :], n_tiles[:, :].unsqueeze(1).to_broadcast([P, TABLE, NE]), ALU.mult))
            link(dve.tensor_reduce(row[:, 1, :], scaled[:, :, :], AX.X, ALU.add))
            link(dve.tensor_tensor(scaled[:, :, :], passed[:, :, :], swing[:, :].unsqueeze(1).to_broadcast([P, TABLE, NE]), ALU.mult))
            link(dve.tensor_reduce(row[:, 2, :], scaled[:, :, :], AX.X, ALU.add))
            link(dve.tensor_tensor(row[:, 1, :], index[:, :], row[:, 1, :], ALU.subtract))
            link(dve.tensor_scalar(row[:, 1, :], row[:, 1, :], float(ROWS), None, ALU.mult))
            link(dve.scalar_tensor_tensor(out=row[:, 1, :], in0=row[:, 0, :], scalar=float(REGION), in1=row[:, 1, :],
                                          op0=ALU.mult, op1=ALU.add))
            dve.tensor_copy(kept.tiles[:, ROW, :], row[:, 1, :])
            dve.tensor_copy(kept.tiles[:, SLOT, :], row[:, 2, :])
            dve.tensor_scalar(kept.tiles[:, EXPERT, :], row[:, 0, :], 1.0, None, ALU.add)
            for e in range(2):
                dve.wait_ge(raw_in, 32 * (e + 1))
                for k in range(2):
                    high, low = halves(kept, k, e)
                    dve.wait_ge(high_done, 2 * e + k + 1)
                    dve.tensor_tensor(low, kept.raw[:, k, :], high, ALU.subtract).then_inc(low_done, 1)

        @block.tensor
        def _(pe):
            pe.wait_ge(ident_ready, 1)
            pe.wait_ge(gate_in, 32)
            for t in range(NT + 1):
                if t < NT:
                    pe.wait_ge(h2_done, t + 1)
                    at_least(pe, turned_out, t - 1)
                    for c in range(DC):
                        mm = pe.transpose(ps_t[:, t % 2, c * P:(c + 1) * P], kept.h2[:, t, c * P:(c + 1) * P], ident[:, :])
                    mm.then_inc(turned, 1)
                if t > 0:
                    pe.wait_ge(turned_out, t)
                    for c in range(DC):
                        mm = pe.matmul(ps_l[:, t - 1, 0:NE], ht[:, (t - 1) % 2, c, :], gate[:, c, :],
                                       start=(c == 0), stop=(c == DC - 1))
                    mm.then_inc(logged, 1)
            pe.wait_ge(hot_done, 1)
            pe.wait_ge(consts_ready, 5)
            for k, m in enumerate((before, ones)):
                mm = pe.matmul(ps_r[:, k, :, 0:NE], m[:, :], both[:, :, :], start=True, stop=True)
            mm.then_inc(ranked, 1)


def experts(nc, kept, w_up_t, w_down_t, expert_rows, expert_out):
    BANKS = 4
    with ExitStack() as ctx:
        def sb(name, shape, dt=F32):
            return ctx.enter_context(nc.sbuf_tensor("d_" + name, shape, dt))

        def sem(name):
            return ctx.enter_context(nc.semaphore("d_" + name))

        ident = sb("ident", [P, P])
        xg = sb("xg", [P, 2, TT, D])
        xp = sb("xp", [P, 2, PIECES, DC * ROWS], BF16)
        g = sb("g", [P, BANKS, 512])
        gp = sb("gp", [P, 2, PIECES, NIC * ROWS], BF16)
        yo = sb("yo", [P, 2, TT, D])
        ps_x = ctx.enter_context(nc.psum_tensor("d_ps_x", [P, 2, DC * ROWS], F32))
        ps_u = ctx.enter_context(nc.psum_tensor("d_ps_u", [P, BANKS, 512], F32))
        ps_y = ctx.enter_context(nc.psum_tensor("d_ps_y", [P, TT, 512], F32))

        zeroed, ident_ready = sem("zeroed"), sem("ident_ready")
        raw_in, w_step, w_ready = sem("raw_in"), sem("w_step"), sem("w_ready")
        x_in = [sem("x_in0"), sem("x_in1")]
        turned, x_split, upped, gelued, g_split, downed, y_ready = (
            sem("turned"), sem("x_split"), sem("upped"), sem("gelued"), sem("g_split"), sem("downed"), sem("y_ready"))
        x_high, g_high, pool_passed = sem("x_high"), sem("g_high"), sem("pool_passed")
        y_out = [sem("y_out0"), sem("y_out1")]

        def by_pairs_of_tiles(engine, step):
            for u in range(2):
                step(u, u)
            with engine.Fori(1, RUN_TILES // 2) as i:
                for u in range(2):
                    step(i * 2 + u, u)

        block = ctx.enter_context(nc.Block())

        @block.sync
        def _(sp):
            def load(t, u):
                row = sp.value_load(kept.tiles[0:1, ROW, bass.ds(t, 1)], min_val=0, max_val=NE * REGION - ROWS)
                at_least(sp, turned, t - 1)
                sp.dma_start(xg[:, u, :, :], expert_rows[bass.ds(row, ROWS), :].rearrange("(t p) d -> p t d", p=P)).then_inc(x_in[u], 16)

            def step(t, u):
                load(t + 2, u)
                sp.wait_ge(y_ready, t + 1)
                sp.dma_start(expert_out[bass.ds(t * ROWS, ROWS), :].rearrange("(t p) d -> p t d", p=P),
                             yo[:, u, :, :]).then_inc(y_out[u], 16)

            for u in range(2):
                load(u, u)
            by_pairs_of_tiles(sp, step)
            for u in range(2):
                sp.wait_ge(y_out[u], 16 * (RUN_TILES // 2))
                sp.wait_ge(x_in[u], 16 * (RUN_TILES // 2 + 1))

        @block.gpsimd
        def _(pool):
            make_identity(pool, ident, zeroed, ident_ready)
            pool.sem_inc(w_ready, 2)
            for e in range(2, NE):
                done = e - 2
                at_least(pool, w_step, 4 * done)
                load_weights(pool, kept, w_up_t, w_down_t, e, raw_in)
                pool.wait_ge(raw_in, 32 * (done + 1))
                pool.wait_ge(downed, pool.value_load(kept.filled[0:1, e - 2:e - 1], min_val=1, max_val=MAX_TILES + 1))
                apart(pool, pool_passed)
                for k in range(2):
                    high, low = halves(kept, k, e % 2)
                    pool.tensor_copy(high, kept.raw[:, k, :]).then_inc(w_step, 1)
                    pool.wait_ge(w_step, 4 * done + 2 * k + 1)
                    pool.tensor_tensor(low, kept.raw[:, k, :], high, ALU.subtract).then_inc(w_step, 1)
                pool.wait_ge(w_step, 4 * done + 4)
                pool.sem_inc(w_ready, 1)

        @block.scalar
        def _(act):
            def gelu(t, j):
                act.wait_ge(upped, t * BANKS + j + 1)
                at_least(act, g_split, (t - 1) * BANKS + j + 1)
                act.activation(g[:, j, :], ps_u[:, j, :], ACT.Gelu).then_inc(gelued, 1)

            def result(t, u):
                act.wait_ge(downed, t + 2)
                at_least(act, y_out[u], (t - u) * 8)
                act.activation(yo[:, u, :, :], ps_y[:, :, 0:D], ACT.Copy).then_inc(y_ready, 1)

            def step(t, u):
                if not isinstance(t, int) or t > 0:
                    result(t - 1, 1 - u)
                for j in range(BANKS):
                    gelu(t, j)

            by_pairs_of_tiles(act, step)
            result(RUN_TILES - 1, 1)

        @block.vector
        def _(dve):
            def split_x(t, u):
                dve.wait_ge(turned, t + 1)
                at_least(dve, upped, (t - 1) * BANKS)
                dve.tensor_copy(xp[:, u, 0, :], ps_x[:, u, :]).then_inc(x_high, 1)
                dve.wait_ge(x_high, t + 1)
                dve.tensor_tensor(xp[:, u, 1, :], ps_x[:, u, :], xp[:, u, 0, :], ALU.subtract).then_inc(x_split, 1)

            def step(t, u):
                split_x(t + 1, 1 - u)
                at_least(dve, downed, t)
                for j in range(BANKS):
                    at = slice(j * 512, (j + 1) * 512)
                    dve.wait_ge(gelued, t * BANKS + j + 1)
                    dve.tensor_copy(gp[:, u, 0, at], g[:, j, :]).then_inc(g_high, 1)
                    dve.wait_ge(g_high, t * BANKS + j + 1)
                    dve.tensor_tensor(gp[:, u, 1, at], g[:, j, :], gp[:, u, 0, at], ALU.subtract).then_inc(g_split, 1)

            split_x(0, 0)
            by_pairs_of_tiles(dve, step)

        @block.tensor
        def _(pe):
            def turn(t, u):
                pe.wait_ge(x_in[u], (t - u) * 8 + 16)
                at_least(pe, x_split, t - 1)
                for c in range(DC):
                    for i in range(TT):
                        mm = pe.transpose(ps_x[:, u, c * ROWS + i * P:c * ROWS + (i + 1) * P], xg[:, u, i, c * P:(c + 1) * P], ident[:, :])
                mm.then_inc(turned, 1)

            PRODUCTS = ((0, 0), (0, 1), (1, 0))

            def up(t, u, slot):
                for j in range(NIC):
                    n = 0
                    for c in range(DC):
                        for w, x in PRODUCTS:
                            mm = pe.matmul(ps_u[:, j // 2, j % 2 * ROWS:(j % 2 + 1) * ROWS], kept.wu[:, slot, w, c, j * P:(j + 1) * P],
                                           xp[:, u, x, c * ROWS:(c + 1) * ROWS], start=(n == 0), stop=(n == 5))
                            n += 1
                    if j % 2 == 1:
                        mm.then_inc(upped, 1)

            def down(t, u, slot):
                at_least(pe, y_ready, t)
                for j in range(NIC):
                    if j % 2 == 0:
                        pe.wait_ge(g_split, t * BANKS + j // 2 + 1)
                    for i in range(TT):
                        for n, (w, x) in enumerate(PRODUCTS):
                            mm = pe.matmul(ps_y[:, i, 0:D], gp[:, u, x, j * ROWS + i * P:j * ROWS + (i + 1) * P],
                                           kept.wd[:, slot, w, j, :], start=(j == 0 and n == 0), stop=(j == NIC - 1 and n == 2))
                mm.then_inc(downed, 1)

            def step(t, u):
                expert = pe.value_load(kept.tiles[0:1, EXPERT, bass.ds(t, 1)], min_val=1, max_val=NE)
                slot = pe.value_load(kept.tiles[0:1, SLOT, bass.ds(t, 1)], min_val=0, max_val=1)
                turn(t + 1, 1 - u)
                pe.wait_ge(w_ready, expert)
                pe.wait_ge(x_split, t + 1)
                with pe.If(slot == 0):
                    up(t, u, 0)
                    down(t, u, 0)
                with pe.Else():
                    up(t, u, 1)
                    down(t, u, 1)

            pe.wait_ge(ident_ready, 1)
            pe.sem_inc(downed, 1)
            turn(0, 0)
            by_pairs_of_tiles(pe, step)


def combine(nc, kept, expert_out, out):
    DEEP = 4
    with ExitStack() as ctx:
        def sb(name, shape, dt=F32):
            return ctx.enter_context(nc.sbuf_tensor("e_" + name, shape, dt))

        def sem(name):
            return ctx.enter_context(nc.semaphore("e_" + name))

        y = sb("y", [P, DEEP, 2, TB, D])
        stats = sb("stats", [P, 2, TB, 6])
        mv = sb("mv", [P, 2, TB, 2])
        std = sb("std", [P, 2, TB])
        less = sb("less", [P, 2, TB])
        y_in = [[sem(f"y_in{u}{t}") for t in range(TB)] for u in range(DEEP)]
        first, mixed, stats_done, mv_done, std_done, inverted, less_done = (
            sem("first"), sem("mixed"), sem("stats_done"), sem("mv_done"), sem("std_done"), sem("inverted"), sem("less_done"))
        normal, added, gated, done = sem("normal"), sem("added"), sem("gated"), sem("done")
        stored = [sem(f"stored{u}") for u in range(DEEP)]
        block = ctx.enter_context(nc.Block())

        @block.gpsimd
        def _(pool):
            for b in range(B):
                at_least(pool, stored[b % DEEP], b // DEEP * 16)
                for t in range(TB):
                    for k in range(2):
                        pool.indirect_dma_start(y[:, b % DEEP, k, t, :], None, expert_out,
                                                bass.IndirectOffsetOnAxis(ap=kept.outs[:, k, b * TB + t:b * TB + t + 1], axis=0)
                                                ).then_inc(y_in[b % DEEP][t], 16)

        @block.scalar
        def _(act):
            def weigh(b):
                for t in range(TB):
                    row = y[:, b % DEEP, 0, t, :]
                    act.wait_ge(y_in[b % DEEP][t], (b // DEEP + 1) * 32)
                    act.activation(row, row, ACT.Copy, scale=kept.gates[:, 0, b * TB + t:b * TB + t + 1]).then_inc(first, 1)

            def normalise(b):
                u = b % 2
                act.wait_ge(mv_done, (b + 1) * TB)
                act.activation(std[:, u, :], mv[:, u, :, 1], ACT.Sqrt, bias=kept.eps[:, :], scale=1.0).then_inc(std_done, 1)
                act.wait_ge(less_done, b + 1)
                for t in range(TB):
                    row = y[:, b % DEEP, 0, t, :]
                    act.activation(row, row, ACT.Identity, bias=less[:, u, t:t + 1], scale=std[:, u, t:t + 1]).then_inc(normal, 1)

            weigh(0)
            for b in range(B):
                if b + 1 < B:
                    weigh(b + 1)
                normalise(b)

        @block.vector
        def _(dve):
            def mix(b):
                u = b % 2
                for t in range(TB):
                    i = b * TB + t
                    dve.wait_ge(first, i + 1)
                    dve.scalar_tensor_tensor(out=y[:, b % DEEP, 0, t, :], in0=y[:, b % DEEP, 1, t, :],
                                             scalar=kept.gates[:, 1, i:i + 1], in1=y[:, b % DEEP, 0, t, :],
                                             op0=ALU.mult, op1=ALU.add).then_inc(mixed, 1)
                for t in range(TB):
                    dve.wait_ge(mixed, b * TB + t + 1)
                    dve.bn_stats(stats[:, u, t, :], y[:, b % DEEP, 0, t, :]).then_inc(stats_done, 1)
                at_least(dve, std_done, b - 1)
                for t in range(TB):
                    dve.wait_ge(stats_done, b * TB + t + 1)
                    dve.bn_aggr(mv[:, u, t, :], stats[:, u, t, :]).then_inc(mv_done, 1)

            def invert(b):
                u = b % 2
                dve.wait_ge(std_done, b + 1)
                at_least(dve, normal, (b - 1) * TB)
                dve.reciprocal(std[:, u, :], std[:, u, :]).then_inc(inverted, 1)
                dve.wait_ge(inverted, b + 1)
                dve.scalar_tensor_tensor(out=less[:, u, :], in0=mv[:, u, :, 0], scalar=-1.0, in1=std[:, u, :],
                                         op0=ALU.mult, op1=ALU.mult).then_inc(less_done, 1)

            def finish(b):
                whole = y[:, b % DEEP, 0, :, :]
                dve.wait_ge(normal, (b + 1) * TB)
                dve.tensor_tensor(whole, whole, kept.h2[:, b * TB:(b + 1) * TB, :], ALU.add).then_inc(added, 1)
                dve.wait_ge(added, b + 1)
                dve.tensor_tensor(whole, whole, kept.mod[:, b, 2 * D:3 * D].unsqueeze(1).to_broadcast([P, TB, D]),
                                  ALU.mult).then_inc(gated, 1)
                dve.wait_ge(gated, b + 1)
                dve.tensor_tensor(whole, whole, kept.x1[:, b * TB:(b + 1) * TB, :], ALU.add).then_inc(done, 1)

            mix(0)
            for b in range(B):
                invert(b)
                if b + 1 < B:
                    mix(b + 1)
                finish(b)

        @block.sync
        def _(sp):
            for b in range(B):
                sp.wait_ge(done, b + 1)
                sp.dma_start(out[b, :, :].rearrange("(t p) d -> p t d", p=P), y[:, b % DEEP, 0, :, :]).then_inc(stored[b % DEEP], 16)
            for u in range(DEEP):
                sp.wait_ge(stored[u], 16 * (B // DEEP))


def adaln_block(nc, x, w_qkv, b_qkv, w_out, b_out, rel_rev, gate_t, expert_bias, w_up_t, w_down_t, c_t, wmod, out):
    def scratch(name, shape, dt=F32):
        return nc.dram_tensor(name, shape, dt, kind="Internal").ap()

    mod_rows = scratch("mod_rows", (B, 6 * D))
    ext_rows = scratch("ext_rows", (NH, EXT))
    h1t = scratch("h1t", (B, P, DC, S))
    splits = scratch("splits", (B, 2, 2, PARTS, P, S), BF16)
    x1 = scratch("x1", (B, S, D))
    expert_rows = scratch("expert_rows", (NE * REGION, D))
    expert_out = scratch("expert_out", (RUN_TILES * ROWS, D))
    prepare(nc, x, c_t, wmod, rel_rev, mod_rows, ext_rows, h1t)
    attention(nc, x, h1t, w_qkv, b_qkv, w_out, b_out, mod_rows, ext_rows, splits, x1)
    with ExitStack() as ctx:
        kept = Kept(nc, ctx)
        route(nc, kept, x1, mod_rows, gate_t, expert_bias, w_up_t, w_down_t, expert_rows)
        experts(nc, kept, w_up_t, w_down_t, expert_rows, expert_out)
        combine(nc, kept, expert_out, out)


def kernel(**inputs):
    import numpy as _np
    import concourse.bacc as _bacc
    from concourse.bass_utils import run_bass_kernel_spmd as _run

    a = {name: _np.asarray(value) for name, value in inputs.items()}
    given = {
        "x": a["L0_attn_x"],
        "w_qkv": a["L0_attn_W_qkv"],
        "b_qkv": a["L0_attn_b_qkv"],
        "w_out": a["L0_attn_W_out"],
        "b_out": a["L0_attn_b_out"],
        "rel_rev": a["L0_attn_rel_bias"].T[:, ::-1],
        "gate_t": a["L0_ffn_gate_w"].T,
        "expert_bias": a["L0_ffn_expert_bias"],
        "w_up_t": a["L0_ffn_w_up"].transpose(0, 2, 1),
        "w_down_t": a["L0_ffn_w_down"].transpose(0, 2, 1),
        "c_t": a["L0_c"].T,
        "wmod": a["L0_wmod"],
    }
    nc = _bacc.Bacc("TRN2", target_bir_lowering=False, num_devices=1)
    arrays, args = {}, {}
    for name, value in given.items():
        value = _np.ascontiguousarray(value)
        arrays[f"in_{name}"] = value
        args[name] = nc.dram_tensor(f"in_{name}", value.shape, mybir.dt.from_np(value.dtype), kind="ExternalInput").ap()
    out = nc.dram_tensor("out", (B, S, D), F32, kind="ExternalOutput").ap()
    adaln_block(nc, out=out, **args)
    r = _run(nc, [arrays], core_ids=[0])
    return r.results[0]["out"]
```

```python
from contextlib import ExitStack

import numpy as np

import concourse.bass as bass
from concourse import mybir

F32 = mybir.dt.float32
BF16 = mybir.dt.bfloat16
I32 = mybir.dt.int32
U32 = mybir.dt.uint32
ALU = mybir.AluOpType
ACT = mybir.ActivationFunctionType
AX = mybir.AxisListType

P = 128
B, S, D = 8, 512, 256
NH, DK = 16, 16
MAXREL = 256
NE, NI = 8, 1024
LN_EPS = 1e-5
GATE_EPS = 1e-6
TB = S // P
DC = D // P
NT = B * TB
ZW = S + (TB - 1) * P
EXT = ZW + P - 1
HALF = NH // 2
NIC = NI // P
PIECES = 2
WN = DC * NI
WC = WN // 2
PARTS = 3
Q_PART = (0, 0, 1, 1, 0, 2)
K_PART = (0, 1, 0, 1, 2, 0)
KS = len(Q_PART) * DK
BIG = 3.0e38


def at_least(engine, semaphore, value):
    if not isinstance(value, int) or value > 0:
        engine.wait_ge(semaphore, value)


def apart(engine, passed):
    engine.sem_inc(passed, 1)


def make_identity(pool, ident, zeroed, done):
    pool.memset(ident[:, :], 0.0).then_inc(zeroed, 1)
    pool.wait_ge(zeroed, 1)
    pool.affine_select(out=ident[:, :], in_=ident[:, :], compare_op=ALU.not_equal, fill=1.0, base=0,
                       pattern=[[-1, P]], channel_multiplier=1).then_inc(done, 1)


class Ahead:

    def __init__(self, nc, ctx):
        self.tile = ctx.enter_context(nc.sbuf_tensor("s_tile", [P, NH, ZW], F32))
        self.loaded = [ctx.enter_context(nc.semaphore(f"s_loaded{g}")) for g in range(NH // TB)]

        def sb(name, shape):
            return ctx.enter_context(nc.sbuf_tensor("s_" + name, shape, F32))

        def sem(name):
            return ctx.enter_context(nc.semaphore("s_" + name))

        self.h1 = sb("h1", [P, DC, S])
        self.wqkv = sb("wqkv", [P, DC, 3 * D])
        self.wo = sb("wo", [P, DC, D])
        self.gate = sb("gate", [P, DC, NE])
        self.b_col = sb("b_col", [P, 4])
        self.b_v = sb("b_v", [P, D])
        self.b_o = sb("b_o", [P, D])
        self.h1_in, self.w_in, self.const_in, self.bq_in, self.gate_in = (
            sem("h1_in"), sem("w_in"), sem("const_in"), sem("bq_in"), sem("gate_in"))

    def load_weights(self, engine, w_qkv, b_qkv, w_out, b_out, gate_t):
        engine.dma_start(self.wqkv[:, :, :], w_qkv.rearrange("(c p) n -> p c n", p=P)).then_inc(self.w_in, 16)
        engine.dma_start(self.b_col[:, :], b_qkv[0:2 * D].rearrange("(c p) -> p c", p=P),
                         allow_slow_non_contiguous=True).then_inc(self.bq_in, 16)
        engine.dma_start(self.b_v[:, :], b_qkv[2 * D:3 * D].rearrange("(a n) -> a n", a=1).to_broadcast([P, D])).then_inc(self.const_in, 16)
        engine.dma_start(self.b_o[:, :], b_out.rearrange("(a n) -> a n", a=1).to_broadcast([P, D])).then_inc(self.const_in, 16)
        engine.dma_start(self.gate[:, :, :], gate_t.rearrange("(c p) e -> p c e", p=P)).then_inc(self.gate_in, 16)
        engine.dma_start(self.wo[:, :, :], w_out.rearrange("(c p) n -> p c n", p=P)).then_inc(self.w_in, 16)

    def load(self, engine, ext_rows, group):
        for h in range(group * TB, (group + 1) * TB):
            engine.dma_start(self.tile[:, h, :], bass.AP(ext_rows.tensor, h * EXT, [[1, P], [1, ZW]])).then_inc(self.loaded[group], 16)


def prepare(nc, ahead, x, c_t, wmod, rel_rev, w_qkv, b_qkv, w_out, b_out, gate_t, mod_rows, ext_rows, h1t):
    with ExitStack() as ctx:
        def sb(name, shape, dt=F32):
            return ctx.enter_context(nc.sbuf_tensor("a_" + name, shape, dt))

        def sem(name):
            return ctx.enter_context(nc.semaphore("a_" + name))

        ident = sb("ident", [P, P])
        power = sb("power", [P, TB])
        ct = sb("ct", [P, DC, B])
        ct_e = sb("ct_e", [P, DC, B])
        silu = sb("silu", [P, DC, B])
        wm = sb("wm", [P, DC, 6 * D])
        rows = sb("rows", [B, 6 * D])
        sgn = sb("sgn", [B, 2, D])
        scale = sb("scale", [P, DC, B])
        shift = sb("shift", [P, DC, B])
        ext = sb("ext", [NH, EXT])
        xt = sb("xt", [P, NT, D])
        stats = sb("stats", [P, NT, 6])
        mv = sb("mv", [P, NT, 2])
        rstd = sb("rstd", [P, NT])
        less = sb("less", [P, NT])
        ht = sb("ht", [P, 2, DC, S])
        ps_mod = ctx.enter_context(nc.psum_tensor("a_ps_mod", [P, 3, 512], F32))
        ps_col = ctx.enter_context(nc.psum_tensor("a_ps_col", [P, 512], F32))
        ps_t = ctx.enter_context(nc.psum_tensor("a_ps_t", [P, 2, DC, S], F32))

        zeroed, ident_ready, power_set, eps_added = sem("zeroed"), sem("ident_ready"), sem("power_set"), sem("eps_added")
        c_in, wm_in, rel_in, x_in = sem("c_in"), sem("wm_in"), sem("rel_in"), [sem(f"x_in{i}") for i in range(B // 2)]
        exp_done, one_done, rec_done, silu_done = sem("exp_done"), sem("one_done"), sem("rec_done"), sem("silu_done")
        mod_ready, rows_copied, rows_step, rows_done = sem("mod_ready"), sem("rows_copied"), sem("rows_step"), sem("rows_done")
        cols_ready, ext_done, ext_stored, rows_stored = sem("cols_ready"), sem("ext_done"), sem("ext_stored"), sem("rows_stored")
        stats_done, mv_done, rstd_done, less_done, xh_done = (
            sem("stats_done"), sem("mv_done"), sem("rstd_done"), sem("less_done"), sem("xh_done"))
        t_done, h_dve, h_act = sem("t_done"), sem("h_dve"), sem("h_act")
        h_out = [sem("h_out0"), sem("h_out1")]
        block = ctx.enter_context(nc.Block())

        @block.sync
        def _(sp):
            sp.dma_start(ct[:, :, :], c_t.rearrange("(c p) b -> p c b", p=P)).then_inc(c_in, 16)
            sp.dma_start(ext[:, MAXREL - 1:3 * MAXREL], rel_rev).then_inc(rel_in, 16)
            for i in range(B // 2):
                sp.dma_start(xt[:, 2 * i * TB:2 * (i + 1) * TB, :],
                             x[2 * i:2 * i + 2, :, :].rearrange("b (t p) d -> p (b t) d", p=P)).then_inc(x_in[i], 16)
                if i == 0:
                    sp.dma_start(wm[:, :, :], wmod.rearrange("(c p) n -> p c n", p=P)).then_inc(wm_in, 16)
            sp.wait_ge(ext_done, 2)
            sp.dma_start(ext_rows, ext[:, :]).then_inc(ext_stored, 16)
            sp.wait_ge(ext_stored, 16)
            ahead.load(sp, ext_rows, 0)
            ahead.load_weights(sp, w_qkv, b_qkv, w_out, b_out, gate_t)
            sp.wait_ge(rows_done, 1)
            sp.dma_start(mod_rows, rows[:, :]).then_inc(rows_stored, 16)
            ahead.load(sp, ext_rows, 1)
            sp.wait_ge(rows_stored, 16)

        @block.gpsimd
        def _(pool):
            make_identity(pool, ident, zeroed, ident_ready)
            pool.memset(power[:, :], -0.5).then_inc(power_set, 1)
            pool.wait_ge(power_set, 1)

            def deviations(b):
                at = slice(b * TB, (b + 1) * TB)
                pool.wait_ge(mv_done, (b + 1) * TB)
                pool.tensor_scalar(rstd[:, at], mv[:, at, 1], LN_EPS, None, ALU.add).then_inc(eps_added, 1)
                pool.wait_ge(eps_added, b + 1)
                pool.tensor_tensor(rstd[:, at], rstd[:, at], power[:, :], ALU.pow).then_inc(rstd_done, 1)

            deviations(0)
            deviations(1)
            for b in range(B):
                if b + 2 < B:
                    deviations(b + 2)
                pool.wait_ge(h_dve, b + 1)
                pool.wait_ge(h_act, b + 1)
                pool.dma_start(h1t[b, :, :, :], ht[:, b % 2, :, :]).then_inc(h_out[b % 2], 16)
                if b == 1:
                    pool.wait_ge(h_out[0], 16)
                    pool.dma_start(ahead.h1[:, :, :], h1t[0, :, :, :]).then_inc(ahead.h1_in, 16)
            for u in range(2):
                pool.wait_ge(h_out[u], 16 * (B // 2))

        @block.scalar
        def _(act):
            act.wait_ge(c_in, 16)
            act.activation(ct_e[:, :, :], ct[:, :, :], ACT.Exp, scale=-1.0).then_inc(exp_done, 1)
            for b in range(B + 1):
                if b < B:
                    act.wait_ge(less_done, b + 1)
                    for t in range(b * TB, (b + 1) * TB):
                        act.activation(xt[:, t, :], xt[:, t, :], ACT.Identity, bias=less[:, t:t + 1], scale=rstd[:, t:t + 1]
                                       ).then_inc(xh_done, 1)
                if b > 0:
                    act.wait_ge(t_done, b)
                    act.wait_ge(cols_ready, 2)
                    at_least(act, h_out[(b - 1) % 2], (b - 1) // 2 * 16)
                    act.activation(ht[:, (b - 1) % 2, 1, :], ps_t[:, (b - 1) % 2, 1, :], ACT.Identity, bias=shift[:, 1, b - 1:b],
                                   scale=scale[:, 1, b - 1:b]).then_inc(h_act, 1)

        @block.vector
        def _(dve):
            def moments(b):
                tiles = range(b * TB, (b + 1) * TB)
                dve.wait_ge(x_in[b // 2], 16)
                for t in tiles:
                    dve.bn_stats(stats[:, t, :], xt[:, t, :]).then_inc(stats_done, 1)
                for t in tiles:
                    dve.wait_ge(stats_done, t + 1)
                    dve.bn_aggr(mv[:, t, :], stats[:, t, :]).then_inc(mv_done, 1)

            def offsets(b):
                at = slice(b * TB, (b + 1) * TB)
                dve.wait_ge(rstd_done, b + 1)
                dve.scalar_tensor_tensor(out=less[:, at], in0=mv[:, at, 0], scalar=-1.0, in1=rstd[:, at],
                                         op0=ALU.mult, op1=ALU.mult).then_inc(less_done, 1)

            dve.wait_ge(exp_done, 1)
            dve.tensor_scalar(ct_e[:, :, :], ct_e[:, :, :], 1.0, None, ALU.add).then_inc(one_done, 1)
            dve.wait_ge(one_done, 1)
            dve.reciprocal(ct_e[:, :, :], ct_e[:, :, :]).then_inc(rec_done, 1)
            dve.wait_ge(rec_done, 1)
            dve.tensor_tensor(silu[:, :, :], ct[:, :, :], ct_e[:, :, :], ALU.mult).then_inc(silu_done, 1)
            dve.wait_ge(rel_in, 16)
            dve.tensor_copy(ext[:, 0:MAXREL - 1], ext[:, MAXREL - 1:MAXREL].to_broadcast([NH, MAXREL - 1])).then_inc(ext_done, 1)
            dve.tensor_copy(ext[:, 3 * MAXREL:EXT], ext[:, 3 * MAXREL - 1:3 * MAXREL].to_broadcast([NH, EXT - 3 * MAXREL])).then_inc(ext_done, 1)
            moments(0)
            moments(1)
            offsets(0)
            for b in range(B):
                if b == 0:
                    dve.wait_ge(mod_ready, 1)
                    dve.tensor_copy(shift[:, :, :], ps_col[:, 0:DC * B]).then_inc(cols_ready, 1)
                    dve.tensor_scalar(scale[:, :, :], ps_col[:, DC * B:2 * DC * B], 1.0, None, ALU.add).then_inc(cols_ready, 1)
                    dve.wait_ge(cols_ready, 2)
                if b + 1 < B:
                    offsets(b + 1)
                if b + 2 < B:
                    moments(b + 2)
                dve.wait_ge(t_done, b + 1)
                at_least(dve, h_out[b % 2], b // 2 * 16)
                dve.tensor_scalar(ht[:, b % 2, 0, :], ps_t[:, b % 2, 0, :], scale[:, 0, b:b + 1], shift[:, 0, b:b + 1],
                                  ALU.mult, ALU.add).then_inc(h_dve, 1)
            dve.wait_ge(mod_ready, 2)
            dve.tensor_copy(rows[:, :], ps_mod[0:B, :, :]).then_inc(rows_copied, 1)
            dve.wait_ge(rows_copied, 1)
            for k, g in enumerate((2, 5)):
                dve.tensor_scalar(sgn[:, k, :], rows[:, g * D:(g + 1) * D], 0.0, 2.0, ALU.is_ge, ALU.mult).then_inc(rows_step, 1)
            for k, g in enumerate((1, 4)):
                dve.tensor_scalar(rows[:, g * D:(g + 1) * D], rows[:, g * D:(g + 1) * D], 1.0, None, ALU.add).then_inc(rows_step, 1)
            dve.wait_ge(rows_step, 4)
            dve.tensor_scalar(sgn[:, :, :], sgn[:, :, :], -1.0, None, ALU.add).then_inc(rows_step, 1)
            dve.wait_ge(rows_step, 5)
            for k, g in enumerate((2, 5)):
                dve.tensor_tensor(rows[:, g * D:(g + 1) * D], rows[:, g * D:(g + 1) * D], sgn[:, k, :], ALU.mult).then_inc(rows_step, 1)
            dve.wait_ge(rows_step, 7)
            for k, g in enumerate((2, 5)):
                last = dve.scalar_tensor_tensor(out=rows[:, g * D:(g + 1) * D], in0=rows[:, g * D:(g + 1) * D], scalar=0.25,
                                                in1=sgn[:, k, :], op0=ALU.max, op1=ALU.mult)
            last.then_inc(rows_done, 1)

        @block.tensor
        def _(pe):
            def turn(b):
                pe.wait_ge(xh_done, (b + 1) * TB)
                at_least(pe, h_dve, b - 1)
                at_least(pe, h_act, b - 1)
                for c in range(DC):
                    for t in range(TB):
                        mm = pe.transpose(ps_t[:, b % 2, c, t * P:(t + 1) * P], xt[:, b * TB + t, c * P:(c + 1) * P], ident[:, :])
                mm.then_inc(t_done, 1)

            pe.wait_ge(silu_done, 1)
            pe.wait_ge(wm_in, 16)
            for j in range(2 * DC):
                for c in range(DC):
                    mm = pe.matmul(ps_col[:, j * B:(j + 1) * B], wm[:, c, j * P:(j + 1) * P], silu[:, c, :],
                                   start=(c == 0), stop=(c == DC - 1))
            mm.then_inc(mod_ready, 1)
            pe.wait_ge(ident_ready, 1)
            for b in range(B):
                turn(b)
                if b == 3:
                    for j in range(3):
                        for c in range(DC):
                            mm = pe.matmul(ps_mod[0:B, j, :], silu[:, c, :], wm[:, c, j * 512:(j + 1) * 512],
                                           start=(c == 0), stop=(c == DC - 1))
                    mm.then_inc(mod_ready, 1)


USES = ((1, "q0"), (2, "k0"), (3, "back3"), (4, "turn0"), (5, "turn1"), (6, "out0"), (7, "back0"), (8, "out1"),
        (9, "q1"), (10, "k1"), (11, "back1"), (12, "v0"), (13, "v1"), (14, "rows0"), (14.5, "rows1"), (15, "back2"),
        (15.5, "logits"))
FROM_BEFORE = ("back3", "turn0", "turn1", "out0", "out1", "rows0", "rows1", "logits")
FOR_NEXT = ("q0", "k0", "q1", "k1", "v0", "v1")
MOMENTS, CENTRED, NORMAL = 9.5, 10.5, 12.5


def attention(nc, ahead, logits, x, h1t, mod_rows, ext_rows, splits, w_up_t, w_down_t, w_parts, x1, h2_rows):
    GROUPS = NH // TB

    with ExitStack() as ctx:
        def sb(name, shape, dt=F32):
            return ctx.enter_context(nc.sbuf_tensor("b_" + name, shape, dt))

        def sem(name):
            return ctx.enter_context(nc.semaphore("b_" + name))

        ident = sb("ident", [P, P])
        flip = sb("flip", [P, P])
        qf = sb("qf", [P, 2, S])
        rest = sb("rest", [P, S])
        parts = sb("parts", [P, 2, PARTS, S], BF16)
        qs = sb("qs", [KS, 2, HALF, S], BF16)
        ks = sb("ks", [KS, 2, HALF, S], BF16)
        v_next = sb("v_next", [P, TB, D])
        v = sb("v", [P, TB, NH, 2 * DK])
        sn = sb("sn", [P, TB, S])
        mn = sb("mn", [P, 2, TB])
        pr = sb("pr", [P, 2, TB, S])
        pt = sb("pt", [P, 2, TB, S])
        ot = sb("ot", [P, S])
        inv = sb("inv", [P, TB, TB])
        on = sb("on", [P, TB, D])
        ont = sb("ont", [P, DC, S])
        xb = sb("xb", [P, TB, D])
        ga = sb("ga", [P, D])
        gab = sb("gab", [P, D])
        gated = sb("gated", [P, TB, D])
        mod2 = sb("mod2", [P, 2 * D])
        stats = sb("stats", [P, TB, 6])
        mv = sb("mv", [P, TB, 2])
        rstd = sb("rstd", [P, TB])
        power = sb("power", [P, TB])
        w_raw = sb("w_raw", [P, 2, WC])
        w_split = sb("w_split", [P, 2, PIECES, WC], BF16)
        ps_s = ctx.enter_context(nc.psum_tensor("b_ps_s", [P, 2, S], F32))
        ps_t = ctx.enter_context(nc.psum_tensor("b_ps_t", [P, TB, S], F32))
        ps_o = ctx.enter_context(nc.psum_tensor("b_ps_o", [P, S], F32))
        ps_m = ctx.enter_context(nc.psum_tensor("b_ps_m", [P, S], F32))

        flip_zeroed, power_set = sem("flip_zeroed"), sem("power_set")
        dve_passed, pool_passed, sp_passed = sem("dve_passed"), sem("pool_passed"), sem("sp_passed")
        zeroed, ident_ready, ones_set, bq_scaled = sem("zeroed"), sem("ident_ready"), sem("ones_set"), sem("bq_scaled")
        x_in = sem("x_in")
        h1, wqkv, wo, gate, b_col, b_v, b_o = ahead.h1, ahead.wqkv, ahead.wo, ahead.gate, ahead.b_col, ahead.b_v, ahead.b_o
        h1_in, w_in, const_in, bq_in, gate_in = ahead.h1_in, ahead.w_in, ahead.const_in, ahead.bq_in, ahead.gate_in
        parts_out = [sem("parts_out0"), sem("parts_out1")]
        stack_in = [sem("stack_in0"), sem("stack_in1")]
        scored, biased, exped = sem("scored"), sem("biased"), sem("exped")
        turned, out_dve, out_act, weighed = sem("turned"), sem("out_dve"), sem("out_act"), sem("weighed")
        ot_out, used, freed = sem("ot_out"), sem("used"), sem("freed")
        w_piece_in = [sem("w_piece_in0"), sem("w_piece_in1")]
        stats_done, mv_done, eps_added, rstd_done, centred, h2_done, h2_out = (
            sem("stats_done"), sem("mv_done"), sem("eps_added"), sem("rstd_done"), sem("centred"), sem("h2_done"), sem("h2_out"))
        w_high, w_low, w_stored = sem("w_high"), sem("w_low"), sem("w_stored")
        split_step, split_done, inv_done = sem("split_step"), sem("split_done"), sem("inv_done")
        v_moved, gab_done, xg_done, gated_done, x1_done, x1_out = (
            sem("v_moved"), sem("gab_done"), sem("xg_done"), sem("gated_done"), sem("x1_done"), sem("x1_out"))

        def uses_of(kind):
            return [(n, u) for n, u in USES
                    if not (kind == "first" and u in FROM_BEFORE) and not (kind == "last" and u in FOR_NEXT)]

        def uses_before(b, kind):
            return len(FOR_NEXT) if kind == "first" else len(FOR_NEXT) + len(uses_of("first")) + (b - 1) * len(USES)

        def use(b, kind, name):
            return uses_before(b, kind) + [u for _, u in uses_of(kind)].index(name)

        def end_use(name):
            return uses_before(B - 1, "last") + len(uses_of("last")) + FROM_BEFORE.index(name)

        def by_batches(engine, batch):
            batch(0, "first")
            with engine.Fori(1, B - 1) as b:
                batch(b, "middle")
            batch(B - 1, "last")

        def split(engine, k, done, reads, passed=None):
            engine.wait_ge(freed, reads)
            at_least(engine, parts_out[k % 2], (done - k % 2) * 8)
            out = parts[:, k % 2, :, :]
            if passed is not None:
                apart(engine, passed)
            engine.tensor_copy(out[:, 0, :], qf[:, k % 2, :]).then_inc(split_step, 1)
            engine.wait_ge(split_step, done * 3 + 1)
            engine.tensor_tensor(rest[:, :], qf[:, k % 2, :], out[:, 0, :], ALU.subtract).then_inc(split_step, 1)
            engine.wait_ge(split_step, done * 3 + 2)
            if passed is not None:
                apart(engine, passed)
            engine.tensor_copy(out[:, 1, :], rest[:, :]).then_inc(split_step, 1)
            engine.wait_ge(split_step, done * 3 + 3)
            engine.tensor_tensor(out[:, 2, :], rest[:, :], out[:, 1, :], ALU.subtract).then_inc(split_done, 1)
            engine.wait_ge(split_done, done + 1)

        block = ctx.enter_context(nc.Block())

        @block.sync
        def _(sp):
            def store_parts(b, k, name, k_done):
                of, half = (0 if name[0] == "q" else 1), int(name[1])
                sp.wait_ge(split_done, k_done)
                sp.dma_start(splits[bass.ds(b, 1), of, half, :, :, :].rearrange("b s p t -> p (b s) t"),
                             parts[:, k % 2, :, :]).then_inc(parts_out[k % 2], 16)

            def load_stack(b, half):
                for k in range(2):
                    sp.wait_ge(parts_out[k], b * 32 + half * 16 + 16)
                for stack, of, which in ((qs, 0, Q_PART), (ks, 1, K_PART)):
                    for g, part in enumerate(which):
                        sp.dma_start(stack[g * DK:(g + 1) * DK, half, :, :],
                                     splits[bass.ds(b, 1), of, half, part, :, :].rearrange("b (h d) t -> d (b h) t", d=DK)
                                     ).then_inc(stack_in[half], 16)

            def load_x(b, at):
                at_least(sp, used, at)
                apart(sp, sp_passed)
                at_least(sp, h2_out, b * 16)
                apart(sp, sp_passed)
                sp.dma_start(xb[:, :, :], x[bass.ds(b, 1), :, :].rearrange("b (t p) d -> p (b t) d", p=P)).then_inc(x_in, 16)
                sp.dma_start(ga[:, :], mod_rows[bass.ds(b, 1), 2 * D:3 * D].to_broadcast([P, D])).then_inc(x_in, 16)
                sp.dma_start(mod2[:, :], mod_rows[bass.ds(b, 1), 3 * D:5 * D].to_broadcast([P, 2 * D])).then_inc(x_in, 16)

            def store_h2(b):
                sp.wait_ge(h2_done, (b + 1) * TB)
                apart(sp, sp_passed)
                sp.dma_start(h2_rows[bass.ds(b * S, S), :].rearrange("(t p) d -> p t d", p=P), xb[:, :, :]).then_inc(h2_out, 16)

            def store_x1(b, j):
                sp.wait_ge(x1_done, b * 2 + j + 1)
                sp.dma_start(x1[bass.ds(b, 1), 2 * j * P:2 * (j + 1) * P, :].rearrange("b (t p) d -> p (b t) d", p=P),
                             gated[:, 2 * j:2 * j + 2, :]).then_inc(x1_out, 16)

            def load_pieces(b, k):
                at_least(sp, w_low, b * 4 + 2 * k)
                for i in range(2):
                    if k == 0:
                        sp.dma_start(w_raw[:, i, :], w_up_t[bass.ds(b, 1), i * P:(i + 1) * P, :].rearrange("e p n -> (e p) n")
                                     ).then_inc(w_piece_in[i], 16)
                    else:
                        sp.dma_start(w_raw[:, i, :].rearrange("p (c n) -> p c n", n=D),
                                     w_down_t[bass.ds(b, 1), i * NI // 2:(i + 1) * NI // 2, :].rearrange("e (c p) n -> p (e c) n", p=P)
                                     ).then_inc(w_piece_in[i], 16)

            def store_pieces(b, k):
                sp.wait_ge(w_low, b * 4 + 2 * k + 2)
                for i in range(2):
                    sp.dma_start(w_parts[bass.ds(b, 1), k, :, :, i * WC:(i + 1) * WC].rearrange("e s p n -> p (e s) n"),
                                 w_split[:, i, :, :]).then_inc(w_stored, 16)

            for half in range(2):
                for k in range(2 * half, 2 * half + 2):
                    store_parts(0, k, FOR_NEXT[k], k + 1)
                load_stack(0, half)

            def batch(b, kind):
                if kind != "first":
                    load_x(b - 1, uses_before(b, kind) - 1)
                if kind == "first":
                    sp.wait_ge(h1_in, 32)
                    for group in range(2, GROUPS):
                        ahead.load(sp, ext_rows, group)
                load_pieces(b, 0)
                if kind != "last":
                    for k in range(2):
                        store_parts(b + 1, k, FOR_NEXT[k], (b + 1) * 4 + k + 1)
                store_pieces(b, 0)
                load_pieces(b, 1)
                if kind != "last":
                    sp.wait_ge(scored, (b * NH + HALF) * TB)
                    apart(sp, sp_passed)
                    load_stack(b + 1, 0)
                if kind != "first":
                    for j in range(2):
                        store_x1(b - 1, j)
                if kind != "last":
                    for k in range(2, 4):
                        store_parts(b + 1, k, FOR_NEXT[k], (b + 1) * 4 + k + 1)
                store_pieces(b, 1)
                if kind != "first":
                    store_h2(b - 1)
                if kind != "last":
                    sp.wait_ge(scored, (b + 1) * NH * TB)
                    apart(sp, sp_passed)
                    load_stack(b + 1, 1)

            by_batches(sp, batch)
            load_x(B - 1, uses_before(B - 1, "last") + len(uses_of("last")))
            for j in range(2):
                store_x1(B - 1, j)
            store_h2(B - 1)
            sp.wait_ge(h2_out, 16 * B)
            sp.wait_ge(x1_out, 16 * 2 * B)
            sp.wait_ge(w_stored, 16 * 4 * NE)

        @block.gpsimd
        def _(pool):
            make_identity(pool, ident, zeroed, ident_ready)
            pool.memset(flip[:, :], 0.0).then_inc(flip_zeroed, 1)
            pool.wait_ge(flip_zeroed, 1)
            pool.affine_select(out=flip[:, :], in_=flip[:, :], compare_op=ALU.not_equal, fill=1.0, base=1 - P,
                               pattern=[[1, P]], channel_multiplier=1).then_inc(ident_ready, 1)
            pool.memset(v[:, :, :, :], 0.0).then_inc(zeroed, 1)
            pool.wait_ge(zeroed, 2)
            pool.memset(v[:, :, :, DK:DK + 1], 1.0).then_inc(ones_set, 1)

            def load_h1(b, at):
                at_least(pool, used, at)
                pool.dma_start(h1[:, :, :], h1t[bass.ds(b, 1), :, :, :].rearrange("b p c s -> (b p) c s")).then_inc(h1_in, 16)

            def move_v(b, half, reads):
                pool.wait_ge(freed, reads)
                at_least(pool, weighed, (b - 1) * NH + (half + 1) * HALF)
                apart(pool, pool_passed)
                pool.tensor_copy(v[:, :, half * HALF:(half + 1) * HALF, 0:DK],
                                 v_next[:, :, half * P:(half + 1) * P].rearrange("p t (h d) -> p t h d", d=DK)).then_inc(v_moved, 1)

            def split_piece(b, n):
                i = n % 2
                pool.wait_ge(w_piece_in[i], b * 32 + n // 2 * 16 + 16)
                at_least(pool, w_stored, b * 64 + (n - i) * 16)
                apart(pool, pool_passed)
                pool.tensor_copy(w_split[:, i, 0, :], w_raw[:, i, :]).then_inc(w_high, 1)
                pool.wait_ge(w_high, b * 4 + n + 1)
                pool.tensor_tensor(w_split[:, i, 1, :], w_raw[:, i, :], w_split[:, i, 0, :], ALU.subtract).then_inc(w_low, 1)

            def residual(b):
                pool.wait_ge(x_in, b * 48 + 48)
                at_least(pool, xg_done, b * TB)
                pool.tensor_tensor(gab[:, :], ga[:, :], b_o[:, :], ALU.mult).then_inc(gab_done, 1)
                pool.wait_ge(gab_done, b + 1)
                for t in range(TB):
                    pool.tensor_tensor(xb[:, t, :], xb[:, t, :], gab[:, :], ALU.add).then_inc(xg_done, 1)

            def add_x(b, j):
                pool.wait_ge(gated_done, b * 2 + j + 1)
                pool.wait_ge(xg_done, b * TB + TB)
                pool.tensor_tensor(gated[:, 2 * j:2 * j + 2, :], gated[:, 2 * j:2 * j + 2, :], xb[:, 2 * j:2 * j + 2, :],
                                   ALU.add).then_inc(x1_done, 1)

            def deviation(b):
                pool.wait_ge(mv_done, (b + 1) * TB)
                at_least(pool, h2_done, b * TB)
                apart(pool, pool_passed)
                pool.tensor_scalar(rstd[:, :], mv[:, :, 1], LN_EPS, None, ALU.add).then_inc(eps_added, 1)
                pool.wait_ge(eps_added, b + 1)
                pool.tensor_tensor(rstd[:, :], rstd[:, :], power[:, :], ALU.pow).then_inc(rstd_done, 1)

            pool.memset(power[:, :], -0.5).then_inc(power_set, 1)
            pool.wait_ge(power_set, 1)
            pool.wait_ge(const_in, 32)
            pool.wait_ge(ones_set, 1)
            load_h1(1, len(FOR_NEXT))
            for half in range(2):
                move_v(0, half, len(FOR_NEXT))

            def batch(b, kind):
                if kind == "middle":
                    load_h1(b + 1, uses_before(b, kind) - 1)
                if kind != "first":
                    residual(b - 1)
                if kind != "last":
                    split(pool, 0, (b + 1) * 4, use(b, kind, "q0") + 1, pool_passed)
                split_piece(b, 0)
                if kind != "first":
                    move_v(b, 1, uses_before(b, kind) - 1)
                if kind != "last":
                    split(pool, 1, (b + 1) * 4 + 1, use(b, kind, "k0") + 1, pool_passed)
                split_piece(b, 1)
                if kind != "first":
                    for j in range(2):
                        add_x(b - 1, j)
                for k in range(2, 4):
                    if kind != "last":
                        split(pool, k, (b + 1) * 4 + k, use(b, kind, FOR_NEXT[k]) + 1, pool_passed)
                    if k == 2 and kind != "first":
                        deviation(b - 1)
                    split_piece(b, k)
                if kind != "last":
                    move_v(b + 1, 0, use(b, kind, "v1") + 1)

            by_batches(pool, batch)
            residual(B - 1)
            for j in range(2):
                add_x(B - 1, j)
            deviation(B - 1)

        @block.scalar
        def _(act):
            def project_out(name, done, at):
                c = ("q0", "q1", "k0", "k1").index(name)
                act.wait_ge(used, at + 1)
                at_least(act, split_done, done - 1)
                k = FOR_NEXT.index(name)
                tiles = ps_m[:, :].rearrange("p (t i) -> p t i", i=P)
                act.activation(qf[:, k % 2, :].rearrange("p (t i) -> p t i", i=P), tiles[:, :, ::-1] if name[0] == "q" else tiles,
                               ACT.Identity, bias=b_col[:, c:c + 1],
                               scale=(DK ** -0.5 if name[0] == "q" else 1.0)).then_inc(freed, 1)

            def exp(h, m, t):
                act.wait_ge(biased, h * TB + t + 1)
                act.activation(pr[:, m, t, :], sn[:, t, :], ACT.Exp, bias=mn[:, m, t:t + 1], scale=-1.0).then_inc(exped, 1)

            def evacuate(h, m):
                act.wait_ge(turned, h * 2 + 2)
                at_least(act, weighed, h - 1)
                act.activation(pt[:, m, 2:4, :], ps_t[:, 2:4, :], ACT.Copy).then_inc(out_act, 1)

            def turn_out(c, at):
                act.wait_ge(used, at + 1)
                act.activation(ont[:, c, :], ps_m[:, :], ACT.Copy).then_inc(freed, 1)

            def outputs(g, at):
                act.wait_ge(weighed, g * TB + TB)
                at_least(act, used, at)
                act.activation(ot[:, :], ps_o[:, :], ACT.Copy).then_inc(ot_out, 1)

            def read_shared(b, n, kind):
                for m, u in uses_of(kind):
                    if m == n and u in FOR_NEXT[:4]:
                        project_out(u, (b + 1) * 4 + FOR_NEXT.index(u), use(b, kind, u))
                    elif m == n and u[:4] in ("turn", "rows"):
                        turn_out(int(u[4]), use(b, kind, u))

            act.wait_ge(bq_scaled, 1)
            for k in range(4):
                project_out(FOR_NEXT[k], k, k)

            def batch(b, kind):
                for n in range(NH):
                    h = b * NH + n
                    at_least(act, turned, (h - 1) * 2)
                    exp(h, n % 2, 0)
                    exp(h, n % 2, 1)
                    read_shared(b, n, kind)
                    if kind != "first" or n > 0:
                        evacuate(h - 1, (n + 1) % 2)
                    exp(h, n % 2, 2)
                    exp(h, n % 2, 3)
                    if n == 1 and kind != "first":
                        outputs(b * GROUPS - 1, uses_before(b, kind))
                    if n in (5, 9, 13):
                        g = (n - 5) // TB
                        if g == 0:
                            outputs(b * GROUPS, 0 if kind == "first" else use(b, kind, "back3") + 1)
                        else:
                            outputs(b * GROUPS + g, use(b, kind, f"back{g - 1}") + 1)
                    read_shared(b, n + 0.5, kind)

            by_batches(act, batch)
            evacuate(B * NH - 1, 1)
            outputs(B * GROUPS - 1, uses_before(B - 1, "last") + len(uses_of("last")))
            for name in ("turn", "rows"):
                for c in range(DC):
                    turn_out(c, end_use(f"{name}{c}"))

        @block.vector
        def _(dve):
            dve.wait_ge(bq_in, 16)
            dve.tensor_scalar(b_col[:, 0:2], b_col[:, 0:2], DK ** -0.5, None, ALU.mult).then_inc(bq_scaled, 1)
            for k in range(4):
                split(dve, k, k, k + 1)
            dve.wait_ge(const_in, 32)

            def add_bias(b, n, t):
                k = (b * NH + n) * TB + t
                dve.wait_ge(scored, k + 1)
                at_least(dve, exped, k - TB + 1)
                apart(dve, dve_passed)
                at = (TB - 1 - t) * P
                dve.tensor_tensor_reduce(sn[:, t, :], ps_s[:, t % 2, :], ahead.tile[:, n, at:at + S], -1.0, BIG, ALU.add, ALU.min,
                                         mn[:, n % 2, t:t + 1]).then_inc(biased, 1)

            def evacuate(h, m):
                dve.wait_ge(turned, h * 2 + 1)
                at_least(dve, weighed, h - 1)
                dve.tensor_copy(pt[:, m, 0:2, :], ps_t[:, 0:2, :]).then_inc(out_dve, 1)

            def values(b, j, at):
                dve.wait_ge(used, at + 1)
                at_least(dve, v_moved, b * 2)
                dve.tensor_tensor(v_next[:, 2 * j:2 * j + 2, :], ps_m[:, :].rearrange("p (t n) -> p t n", n=D),
                                  b_v[:, :].unsqueeze(1).to_broadcast([P, 2, D]), ALU.add).then_inc(freed, 1)

            def back(b, g, at):
                dve.wait_ge(used, at + 1)
                turned_back = ps_m[:, :].rearrange("p (h t w) -> p h t w", h=TB, t=TB)
                dve.reciprocal(inv[:, :, :], turned_back[:, :, :, DK]).then_inc(inv_done, 1)
                dve.wait_ge(inv_done, b * GROUPS + g + 1)
                dve.tensor_tensor(on[:, :, g * TB * DK:(g + 1) * TB * DK].rearrange("p t (h d) -> p h t d", d=DK),
                                  turned_back[:, :, :, 0:DK], inv[:, :, :].unsqueeze(3).to_broadcast([P, TB, TB, DK]),
                                  ALU.mult).then_inc(freed, 1)

            def gate_out(b, j, at):
                dve.wait_ge(used, at + 1)
                dve.wait_ge(x_in, b * 48 + 48)
                at_least(dve, x1_out, b * 32)
                dve.tensor_tensor(gated[:, 2 * j:2 * j + 2, :], ps_m[:, :].rearrange("p (t n) -> p t n", n=D),
                                  ga[:, :].unsqueeze(1).to_broadcast([P, 2, D]), ALU.mult).then_inc(freed, 1)
                dve.wait_ge(freed, at + 1)
                dve.sem_inc(gated_done, 1)

            def moments(b):
                dve.wait_ge(x1_done, b * 2 + 2)
                for t in range(TB):
                    dve.bn_stats(stats[:, t, :], gated[:, t, :]).then_inc(stats_done, 1)
                at_least(dve, rstd_done, b)
                dve.wait_ge(stats_done, (b + 1) * TB)
                apart(dve, dve_passed)
                for t in range(TB):
                    dve.bn_aggr(mv[:, t, :], stats[:, t, :]).then_inc(mv_done, 1)

            def centre(b):
                dve.wait_ge(mv_done, (b + 1) * TB)
                apart(dve, dve_passed)
                for t in range(TB):
                    dve.scalar_tensor_tensor(out=xb[:, t, :], in0=gated[:, t, :], scalar=mv[:, t, 0:1], in1=mod2[:, D:2 * D],
                                             op0=ALU.subtract, op1=ALU.mult).then_inc(centred, 1)

            def normal(b):
                dve.wait_ge(rstd_done, b + 1)
                dve.wait_ge(centred, (b + 1) * TB)
                apart(dve, dve_passed)
                for t in range(TB):
                    dve.scalar_tensor_tensor(out=xb[:, t, :], in0=xb[:, t, :], scalar=rstd[:, t:t + 1], in1=mod2[:, 0:D],
                                             op0=ALU.mult, op1=ALU.add).then_inc(h2_done, 1)

            def keep_logits(b, at):
                dve.wait_ge(used, at + 1)
                dve.tensor_copy(logits[:, bass.ds(b * TB, TB), :],
                                ps_m[:, 0:TB * NE].rearrange("p (t e) -> p t e", e=NE)).then_inc(freed, 1)

            def between(b, n, kind):
                for m, u in uses_of(kind):
                    if m == n and u == "back3":
                        back(b - 1, 3, use(b, kind, u))
                    elif m == n and u[:4] == "back":
                        back(b, int(u[4]), use(b, kind, u))
                    elif m == n and u[:3] == "out":
                        gate_out(b - 1, int(u[3]), use(b, kind, u))
                    elif m == n and u[0] == "v":
                        values(b + 1, int(u[1]), use(b, kind, u))
                    elif m == n and u == "logits":
                        keep_logits(b - 1, use(b, kind, u))
                if kind != "first" and n == MOMENTS:
                    moments(b - 1)
                if kind != "first" and n == CENTRED:
                    centre(b - 1)
                if kind != "first" and n == NORMAL:
                    normal(b - 1)

            for j in range(2):
                values(0, j, 4 + j)

            def batch(b, kind):
                for n in range(NH):
                    if kind == "first" and n % TB == 0:
                        dve.wait_ge(ahead.loaded[n // TB], 16 * TB)
                    add_bias(b, n, 0)
                    add_bias(b, n, 1)
                    between(b, n, kind)
                    if kind != "first" or n > 0:
                        evacuate(b * NH + n - 1, (n + 1) % 2)
                    add_bias(b, n, 2)
                    add_bias(b, n, 3)
                    between(b, n + 0.5, kind)

            by_batches(dve, batch)
            evacuate(B * NH - 1, 1)
            back(B - 1, 3, end_use("back3"))
            for j in range(2):
                gate_out(B - 1, j, end_use(f"out{j}"))
            moments(B - 1)
            centre(B - 1)
            normal(B - 1)
            keep_logits(B - 1, end_use("logits"))

        @block.tensor
        def _(pe):
            def score(b, n, t):
                k = (b * NH + n) * TB + t
                at_least(pe, biased, k - 1)
                half, m = n // HALF, n % HALF
                pe.matmul(ps_s[:, t % 2, :], qs[:, half, m, t * P:(t + 1) * P], ks[:, half, m, :],
                          start=True, stop=True).then_inc(scored, 1)

            def turn_probabilities(h, m, pair):
                at_least(pe, out_act if pair else out_dve, h)
                for j in (2 * pair, 2 * pair + 1):
                    for t in range(TB):
                        mm = pe.transpose(ps_t[:, j, t * P:(t + 1) * P], pr[:, m, t, j * P:(j + 1) * P], ident[:, :])
                mm.then_inc(turned, 1)

            def weigh(b, n):
                h = b * NH + n
                pe.wait_ge(out_dve, h + 1)
                pe.wait_ge(out_act, h + 1)
                if n % HALF == 0:
                    pe.wait_ge(v_moved, b * 2 + n // HALF + 1)
                if n % TB == 0:
                    at_least(pe, ot_out, b * GROUPS + n // TB)
                for j in range(TB):
                    for t in range(TB):
                        mm = pe.matmul(ps_o[2 * DK * t:2 * DK * (t + 1), n % TB * P:(n % TB + 1) * P], v[:, j, n, :],
                                       pt[:, n % 2, j, t * P:(t + 1) * P], start=(j == 0), stop=(j == TB - 1))
                mm.then_inc(weighed, 1)

            def project(b, name, at):
                at_least(pe, freed, at)
                pe.wait_ge(h1_in, b * 16 + 16)
                if name[0] == "v":
                    for t in range(2):
                        for c in range(DC):
                            j = 2 * int(name[1]) + t
                            mm = pe.matmul(ps_m[:, t * D:(t + 1) * D], h1[:, c, j * P:(j + 1) * P], wqkv[:, c, 2 * D:3 * D],
                                           start=(c == 0), stop=(c == DC - 1))
                else:
                    col = ("q0", "q1", "k0", "k1").index(name) * P
                    for c in range(DC):
                        mm = pe.matmul(ps_m[:, :], wqkv[:, c, col:col + P], h1[:, c, :], start=(c == 0), stop=(c == DC - 1))
                mm.then_inc(used, 1)

            def back(g, at):
                pe.wait_ge(ot_out, g + 1)
                at_least(pe, freed, at)
                for i in range(TB):
                    mm = pe.transpose(ps_m[:, i * P:(i + 1) * P], ot[:, i * P:(i + 1) * P], ident[:, :])
                mm.then_inc(used, 1)

            def turn_outputs(c, at):
                at_least(pe, freed, at)
                for t in range(TB):
                    mm = pe.transpose(ps_m[:, t * P:(t + 1) * P], on[:, t, c * P:(c + 1) * P], flip[:, :])
                mm.then_inc(used, 1)

            def project_outputs(j, at):
                at_least(pe, freed, at)
                for t in range(2):
                    for c in range(DC):
                        mm = pe.matmul(ps_m[:, t * D:(t + 1) * D], ont[:, c, (2 * j + t) * P:(2 * j + t + 1) * P], wo[:, c, :],
                                       start=(c == 0), stop=(c == DC - 1))
                mm.then_inc(used, 1)

            def turn_rows(b, c, at):
                pe.wait_ge(h2_done, (b + 1) * TB)
                at_least(pe, freed, at)
                for t in range(TB):
                    mm = pe.transpose(ps_m[:, t * P:(t + 1) * P], xb[:, t, c * P:(c + 1) * P], ident[:, :])
                mm.then_inc(used, 1)

            def route_rows(at):
                at_least(pe, freed, at)
                for t in range(TB):
                    for c in range(DC):
                        mm = pe.matmul(ps_m[:, t * NE:(t + 1) * NE], ont[:, c, t * P:(t + 1) * P], gate[:, c, :],
                                       start=(c == 0), stop=(c == DC - 1))
                mm.then_inc(used, 1)

            def shared(b, n, kind):
                for m, u in uses_of(kind):
                    at = use(b, kind, u)
                    if m != n:
                        continue
                    if u in FOR_NEXT:
                        project(b + 1, u, at)
                    elif u == "back3":
                        back(b * GROUPS - 1, at)
                    elif u[:4] == "back":
                        back(b * GROUPS + int(u[4]), at)
                    elif u[:4] == "turn":
                        turn_outputs(int(u[4]), at)
                    elif u[:4] == "rows":
                        turn_rows(b - 1, int(u[4]), at)
                    elif u == "logits":
                        route_rows(at)
                    else:
                        project_outputs(int(u[3]), at)

            pe.wait_ge(gate_in, 16)
            pe.wait_ge(w_in, 32)
            for k, name in enumerate(FOR_NEXT):
                project(0, name, k)
            pe.wait_ge(ident_ready, 2)

            def batch(b, kind):
                for n in range(NH):
                    h = b * NH + n
                    if n % HALF == 0:
                        pe.wait_ge(stack_in[n // HALF], (b + 1) * 32 * len(Q_PART))
                    score(b, n, 0)
                    score(b, n, 1)
                    shared(b, n, kind)
                    if kind != "first" or n > 0:
                        pe.wait_ge(exped, h * TB)
                        turn_probabilities(h - 1, (n + 1) % 2, 0)
                        score(b, n, 2)
                        turn_probabilities(h - 1, (n + 1) % 2, 1)
                    else:
                        score(b, n, 2)
                    score(b, n, 3)
                    if n > 1:
                        weigh(b, n - 2)
                    elif kind != "first":
                        weigh(b - 1, n + NH - 2)
                    shared(b, n + 0.5, kind)

            by_batches(pe, batch)
            pe.wait_ge(exped, B * NH * TB)
            for pair in range(2):
                turn_probabilities(B * NH - 1, 1, pair)
            weigh(B - 1, NH - 2)
            weigh(B - 1, NH - 1)
            back(B * GROUPS - 1, end_use("back3"))
            for c in range(DC):
                turn_outputs(c, end_use(f"turn{c}"))
            for j in range(2):
                project_outputs(j, end_use(f"out{j}"))
            for c in range(DC):
                turn_rows(B - 1, c, end_use(f"rows{c}"))
            route_rows(end_use("logits"))


TT = 2
ROWS = TT * P
MAX_TILES = 2 * B * S // ROWS + NE - 1
STEPS = B * S // ROWS
RUN_TILES = MAX_TILES + MAX_TILES % 2
TABLE = RUN_TILES + 2
SPARE = 2
SLOT, LOADED = range(2)


def load_weights(engine, kept, w_parts, e):
    for k, w in enumerate((kept.wu, kept.wd)):
        engine.dma_start(w[:, e % 2, :, :, :].rearrange("p s c n -> p s (c n)"),
                         w_parts[e, k, :, :, :].rearrange("s p n -> p s n")).then_inc(kept.w_ready[e % 2], 16)


class Kept:

    def __init__(self, nc, ctx):
        def sb(name, shape, dt=F32):
            return ctx.enter_context(nc.sbuf_tensor("k_" + name, shape, dt))

        self.x1 = sb("x1", [P, NT, D])
        self.h2 = sb("h2", [P, NT, D])
        self.gb = sb("gb", [P, B, D])
        self.w_ready = [ctx.enter_context(nc.semaphore(f"k_w_ready{slot}")) for slot in range(2)]
        self.gates = sb("gates", [P, 2, NT])
        self.rows = sb("rows", [P, 2, NT], U32)
        self.tokens = sb("tokens", [P, TABLE * TT], U32)
        self.results = sb("results", [P, TABLE * TT], U32)
        self.tiles = sb("tiles", [P, 2, TABLE], I32)
        self.filled = sb("filled", [P, NE], I32)
        self.wu = sb("wu", [P, 2, PIECES, DC, NI], BF16)
        self.wd = sb("wd", [P, 2, PIECES, NIC, D], BF16)


def route(nc, kept, logits, x1, mod_rows, expert_bias, w_parts, h2_rows):
    FILLS = TABLE * TT
    BY_POOL = 3 * NT // 4
    AT_ONCE = 8
    with ExitStack() as ctx:
        def sb(name, shape, dt=F32):
            return ctx.enter_context(nc.sbuf_tensor("c_" + name, shape, dt))

        def sem(name):
            return ctx.enter_context(nc.semaphore("c_" + name))

        before = sb("before", [P, P], BF16)
        ones = sb("ones", [P, P], BF16)
        up_to = sb("up_to", [P, NE, NE])
        ints = sb("ints", [P, NE + STEPS + TABLE + P], I32)
        nums = sb("nums", [P, NE + STEPS + TABLE + P])
        swing = sb("swing", [P, NE])
        e_bias = sb("e_bias", [P, NE])
        weights = sb("weights", [P, NT, NE])
        per_tok = sb("per_tok", [P, 4, NT])
        top = sb("top", [P, NT, 8])
        top_i = sb("top_i", [P, NT, 8], U32)
        top_f = sb("top_f", [P, NT, 2])
        hot = sb("hot", [P, 2, NT, NE])
        both = sb("both", [P, NT, NE], BF16)
        run = sb("run", [P, 2, NT, NE])
        rank = sb("rank", [P, NT, NE])
        picked = sb("picked", [P, 2, NT, NE])
        places = sb("places", [P, 2, NT])
        more = sb("more", [P, NE, STEPS])
        n_tiles = sb("n_tiles", [P, NE])
        mixed = sb("mixed", [P, NE, NE])
        filled = sb("filled", [P, NE])
        start = sb("start", [P, NE])
        last_tile = sb("last_tile", [P, 1])
        index = sb("index", [P, TABLE])
        passed = sb("passed", [P, TABLE, NE])
        scaled = sb("scaled", [P, TABLE, NE])
        row = sb("row", [P, 2, TABLE])
        place_u = sb("place_u", [P, 2, 2 * NT], U32)
        place_f = sb("place_f", [P, 2, 2 * NT])
        place_in = sb("place_in", [P, 1], I32)
        place = sb("place", [P, 1])
        row_in = sb("row_in", [P, FILLS], I32)
        row_number = sb("row_number", [P, FILLS])
        source = sb("source", [P, 4, FILLS])
        hot_rest = sb("hot_rest", [P, 2 * NT, P], BF16)
        hot_fill = sb("hot_fill", [P, 2 * NT, FILLS], BF16)
        fill_by = sb("fill_by", [P, 2, 2 * NT, FILLS], BF16)
        found = sb("found", [P, 2, FILLS])
        ps_f = ctx.enter_context(nc.psum_tensor("c_ps_f", [P, 512], F32))
        ps_r = ctx.enter_context(nc.psum_tensor("c_ps_r", [P, 2, NT, 2 * NE], F32))
        iota_e, steps, iota_t, iota_p = (nums[:, 0:NE], nums[:, NE:NE + STEPS], nums[:, NE + STEPS:NE + STEPS + TABLE],
                                         nums[:, NE + STEPS + TABLE:])

        consts_ready, pool_step = sem("consts_ready"), sem("pool_step")
        kept_in, e_bias_in = sem("kept_in"), sem("e_bias_in")
        shifted, exped, hot_done, ranked, placed = sem("shifted"), sem("exped"), sem("hot_done"), sem("ranked"), sem("placed")
        chained = sem("chained")
        fill_act = sem("fill_act")
        rest_done, rest_dve, fill_hot, fill_done, tokens_found = (
            sem("rest_done"), sem("rest_dve"), sem("fill_hot"), sem("fill_done"), sem("tokens_found"))
        block = ctx.enter_context(nc.Block())

        @block.sync
        def _(sp):
            sp.dma_start(e_bias[:, :], expert_bias.rearrange("(a e) -> a e", a=1).to_broadcast([P, NE])).then_inc(e_bias_in, 16)
            for e in range(2):
                load_weights(sp, kept, w_parts, e)
            sp.dma_start(kept.x1[:, :, :], x1.rearrange("b (t p) d -> p (b t) d", p=P)).then_inc(kept_in, 16)
            sp.dma_start(kept.h2[:, :, :], h2_rows.rearrange("(t p) d -> p t d", p=P)).then_inc(kept_in, 16)
            sp.dma_start(kept.gb[:, :, :], mod_rows[:, 5 * D:6 * D].unsqueeze(0).to_broadcast([P, B, D])).then_inc(kept_in, 16)
            sp.wait_ge(kept_in, 48)

        @block.gpsimd
        def _(pool):
            pool.memset(before[:, :], 1.0).then_inc(pool_step, 1)
            pool.memset(up_to[:, :, :], 1.0).then_inc(pool_step, 1)
            pool.memset(ones[:, :], 1.0).then_inc(consts_ready, 1)
            for at, n, step in ((0, NE, 1), (NE, STEPS, ROWS), (NE + STEPS, TABLE, 1), (NE + STEPS + TABLE, P, 1)):
                pool.iota(ints[:, at:at + n], pattern=[[step, n]], base=0, channel_multiplier=0).then_inc(pool_step, 1)
            pool.iota(row_in[:, :], pattern=[[P, FILLS]], base=0, channel_multiplier=1).then_inc(pool_step, 1)
            pool.iota(place_in[:, :], pattern=[[0, 1]], base=1, channel_multiplier=1).then_inc(pool_step, 1)
            pool.wait_ge(pool_step, 8)
            pool.tensor_copy(row_number[:, :], row_in[:, :]).then_inc(consts_ready, 1)
            pool.tensor_copy(place[:, :], place_in[:, :]).then_inc(consts_ready, 1)
            pool.tensor_copy(nums[:, :], ints[:, :]).then_inc(consts_ready, 1)
            pool.affine_select(out=before[:, :], in_=before[:, :], compare_op=ALU.is_gt, fill=0.0, base=0,
                               pattern=[[1, P]], channel_multiplier=-1).then_inc(consts_ready, 1)
            pool.affine_select(out=up_to[:, :, :], in_=up_to[:, :, :], compare_op=ALU.is_ge, fill=0.0, base=0,
                               pattern=[[1, NE], [-1, NE]], channel_multiplier=0).then_inc(consts_ready, 1)
            pool.wait_ge(placed, 1)
            pool.wait_ge(consts_ready, 6)
            for i in range(2 * NT - BY_POOL, 2 * NT):
                pool.tensor_scalar(hot_rest[:, i, :], iota_p, place_f[:, 1, i:i + 1], None, ALU.is_equal).then_inc(rest_done, 1)

        @block.scalar
        def _(act):
            act.wait_ge(shifted, 1)
            act.activation(weights[:, :, :], logits[:, :, :], ACT.Exp).then_inc(exped, 1)
            act.wait_ge(consts_ready, 6)
            for i in range(0, 2 * NT, AT_ONCE):
                at = slice(i, i + AT_ONCE)
                act.wait_ge(fill_hot, i // AT_ONCE + 1)
                act.activation(fill_by[:, 1, at, :], hot_fill[:, at, :], ACT.Copy, scale=place[:, :]).then_inc(fill_act, 1)

        @block.vector
        def _(dve):
            count = [0]

            def link(ins):
                count[0] += 1
                ins.then_inc(chained, 1)
                dve.wait_ge(chained, count[0])

            dve.memset(swing[:, 0:NE:2], 1.0)
            link(dve.memset(swing[:, 1:NE:2], -1.0))
            dve.wait_ge(e_bias_in, 16)
            link(dve.tensor_tensor(logits[:, :, :], logits[:, :, :], e_bias[:, :].unsqueeze(1).to_broadcast([P, NT, NE]), ALU.add))
            link(dve.tensor_reduce(per_tok[:, 0, :], logits[:, :, :], AX.X, ALU.max))
            dve.tensor_tensor(logits[:, :, :], logits[:, :, :], per_tok[:, 0, :].unsqueeze(2).to_broadcast([P, NT, NE]),
                              ALU.subtract).then_inc(shifted, 1)
            dve.wait_ge(exped, 1)
            link(dve.tensor_reduce(per_tok[:, 1, :], weights[:, :, :], AX.X, ALU.add))
            link(dve.reciprocal(per_tok[:, 2, :], per_tok[:, 1, :]))
            link(dve.tensor_tensor(weights[:, :, :], weights[:, :, :], per_tok[:, 2, :].unsqueeze(2).to_broadcast([P, NT, NE]), ALU.mult))
            for t in range(NT):
                ins = dve.max(top[:, t, :], weights[:, t, :])
            link(ins)
            for t in range(NT):
                ins = dve.max_index(top_i[:, t, :], top[:, t, :], weights[:, t, :])
            link(ins)
            link(dve.tensor_tensor(per_tok[:, 3, :], top[:, :, 0], top[:, :, 1], ALU.add))
            link(dve.tensor_scalar(per_tok[:, 3, :], per_tok[:, 3, :], GATE_EPS, None, ALU.add))
            link(dve.reciprocal(per_tok[:, 3, :], per_tok[:, 3, :]))
            for k in range(2):
                dve.tensor_tensor(kept.gates[:, k, :], top[:, :, k], per_tok[:, 3, :], ALU.mult)
            link(dve.tensor_copy(top_f[:, :, :], top_i[:, :, 0:2]))
            dve.wait_ge(consts_ready, 6)
            for k in range(2):
                ins = dve.tensor_tensor(hot[:, k, :, :], iota_e.unsqueeze(1).to_broadcast([P, NT, NE]),
                                        top_f[:, :, k:k + 1].to_broadcast([P, NT, NE]), ALU.is_equal)
            link(ins)
            dve.tensor_tensor(both[:, :, :], hot[:, 0, :, :], hot[:, 1, :, :], ALU.add).then_inc(hot_done, 1)
            dve.wait_ge(ranked, 1)
            link(dve.tensor_copy(run[:, 0, :, :], ps_r[:, 1, :, 0:NE]))
            a, shift = 0, 1
            while shift < NT:
                dve.tensor_copy(run[:, 1 - a, 0:shift, :], run[:, a, 0:shift, :])
                link(dve.tensor_tensor(run[:, 1 - a, shift:NT, :], run[:, a, shift:NT, :], run[:, a, 0:NT - shift, :], ALU.add))
                a, shift = 1 - a, 2 * shift
            counts = run[:, a, NT - 1, :]
            link(dve.tensor_tensor(rank[:, :, :], run[:, a, :, :], ps_r[:, 1, :, 0:NE], ALU.subtract))
            link(dve.tensor_tensor(rank[:, :, :], rank[:, :, :], ps_r[:, 0, :, 0:NE], ALU.add))
            link(dve.tensor_tensor(more[:, :, :], counts.unsqueeze(2).to_broadcast([P, NE, STEPS]),
                                   steps.unsqueeze(1).to_broadcast([P, NE, STEPS]), ALU.is_gt))
            link(dve.tensor_reduce(n_tiles[:, :], more[:, :, :], AX.X, ALU.add))
            link(dve.tensor_tensor(mixed[:, :, :], up_to[:, :, :], n_tiles[:, :].unsqueeze(1).to_broadcast([P, NE, NE]), ALU.mult))
            link(dve.tensor_reduce(filled[:, :], mixed[:, :, :], AX.X, ALU.add))
            link(dve.tensor_tensor(start[:, :], filled[:, :], n_tiles[:, :], ALU.subtract))
            link(dve.tensor_scalar(start[:, :], start[:, :], float(ROWS), None, ALU.mult))
            link(dve.tensor_tensor(rank[:, :, :], rank[:, :, :], start[:, :].unsqueeze(1).to_broadcast([P, NT, NE]), ALU.add))
            for k in range(2):
                ins = dve.tensor_tensor(picked[:, k, :, :], hot[:, k, :, :], rank[:, :, :], ALU.mult)
            link(ins)
            link(dve.tensor_reduce(places[:, :, :], picked[:, :, :, :], AX.X, ALU.add))
            link(dve.tensor_copy(kept.rows[:, :, :], places[:, :, :]))
            rows = kept.rows[:, :, :].rearrange("p k t -> p (k t)")
            dve.tensor_scalar(place_u[:, 0, :], rows, P.bit_length() - 1, None, ALU.logical_shift_right)
            link(dve.tensor_scalar(place_u[:, 1, :], rows, P - 1, None, ALU.bitwise_and))
            link(dve.tensor_copy(place_f[:, :, :], place_u[:, :, :]))
            dve.sem_inc(placed, 1)
            for i in range(0, 2 * NT, AT_ONCE):
                at = slice(i, i + AT_ONCE)
                if i < 2 * NT - BY_POOL:
                    dve.tensor_tensor(hot_rest[:, at, :], iota_p.unsqueeze(1).to_broadcast([P, AT_ONCE, P]),
                                      place_f[:, 1, at].unsqueeze(2).to_broadcast([P, AT_ONCE, P]), ALU.is_equal).then_inc(rest_dve, 1)
                dve.tensor_tensor(hot_fill[:, at, :], iota_p[:, 0:FILLS].unsqueeze(1).to_broadcast([P, AT_ONCE, FILLS]),
                                  place_f[:, 0, at].unsqueeze(2).to_broadcast([P, AT_ONCE, FILLS]), ALU.is_equal).then_inc(fill_hot, 1)
                dve.wait_ge(fill_hot, i // AT_ONCE + 1)
                dve.tensor_tensor(fill_by[:, 0, at, :], hot_fill[:, at, :],
                                  iota_p[:, i:i + AT_ONCE].unsqueeze(2).to_broadcast([P, AT_ONCE, FILLS]),
                                  ALU.mult).then_inc(fill_done, 1)
            link(dve.tensor_scalar(kept.filled[:, :], filled[:, :], 1.0, None, ALU.add))
            link(dve.tensor_scalar(last_tile[:, :], filled[:, NE - 1:NE], -1.0, None, ALU.add))
            link(dve.tensor_scalar(index[:, :], iota_t, last_tile[:, :], None, ALU.min))
            link(dve.tensor_tensor(passed[:, :, :], index[:, :].unsqueeze(2).to_broadcast([P, TABLE, NE]),
                                   filled[:, :].unsqueeze(1).to_broadcast([P, TABLE, NE]), ALU.is_ge))
            link(dve.tensor_reduce(row[:, 0, :], passed[:, :, :], AX.X, ALU.add))
            link(dve.tensor_tensor(scaled[:, :, :], passed[:, :, :], swing[:, :].unsqueeze(1).to_broadcast([P, TABLE, NE]), ALU.mult))
            link(dve.tensor_reduce(row[:, 1, :], scaled[:, :, :], AX.X, ALU.add))
            link(dve.tensor_scalar(scaled[:, :, 0], iota_t, last_tile[:, :], float(SPARE), ALU.is_gt, ALU.mult))
            dve.tensor_tensor(kept.tiles[:, SLOT, :], scaled[:, :, 0], row[:, 1, :], ALU.max)
            link(dve.tensor_tensor(row[:, 0, :], row[:, 0, :], row[:, 1, :], ALU.subtract))
            dve.tensor_scalar(kept.tiles[:, LOADED, :], row[:, 0, :], 16.0, 32.0, ALU.mult, ALU.add)
            dve.wait_ge(tokens_found, 1)
            link(dve.tensor_copy(found[:, :, :], ps_f[:, 0:2 * FILLS]))
            link(dve.scalar_tensor_tensor(out=source[:, 0, :], in0=found[:, 0, :], scalar=float(P), in1=found[:, 1, :],
                                          op0=ALU.mult, op1=ALU.add))
            link(dve.tensor_scalar(source[:, 1, :], source[:, 0, :], float(B * S), float(-B * S), ALU.is_gt, ALU.mult))
            link(dve.tensor_tensor(source[:, 1, :], source[:, 1, :], source[:, 0, :], ALU.add))
            dve.tensor_scalar(kept.tokens[:, :], source[:, 1, :], -1.0, 0.0, ALU.add, ALU.max)
            link(dve.tensor_scalar(source[:, 2, :], row_number[:, :], float(2 * B * S + 1), None, ALU.add))
            link(dve.tensor_scalar(source[:, 3, :], source[:, 0, :], 0.0, None, ALU.is_equal))
            link(dve.tensor_tensor(source[:, 2, :], source[:, 2, :], source[:, 3, :], ALU.mult))
            dve.scalar_tensor_tensor(out=kept.results[:, :], in0=source[:, 0, :], scalar=-1.0, in1=source[:, 2, :],
                                     op0=ALU.add, op1=ALU.add)

        @block.tensor
        def _(pe):
            pe.wait_ge(hot_done, 1)
            pe.wait_ge(consts_ready, 6)
            for k, m in enumerate((before, ones)):
                mm = pe.matmul(ps_r[:, k, :, 0:NE], m[:, :], both[:, :, :], start=True, stop=True)
            mm.then_inc(ranked, 1)
            for i in range(2 * NT):
                if i < 2 * NT - BY_POOL:
                    pe.wait_ge(rest_dve, i // AT_ONCE + 1)
                else:
                    pe.wait_ge(rest_done, i - (2 * NT - BY_POOL) + 1)
                pe.wait_ge(fill_done, i // AT_ONCE + 1)
                pe.wait_ge(fill_act, i // AT_ONCE + 1)
                mm = pe.matmul(ps_f[:, 0:2 * FILLS], hot_rest[:, i, :], fill_by[:, :, i, :], start=(i == 0), stop=(i == 2 * NT - 1))
            mm.then_inc(tokens_found, 1)


def experts(nc, kept, w_parts, h2_rows, results):
    BANKS = 4
    with ExitStack() as ctx:
        def sb(name, shape, dt=F32):
            return ctx.enter_context(nc.sbuf_tensor("d_" + name, shape, dt))

        def sem(name):
            return ctx.enter_context(nc.semaphore("d_" + name))

        ident = sb("ident", [P, P])
        tokens = sb("tokens", [P, 2, TT], U32)
        places = sb("places", [P, 2, TT], U32)
        xg = sb("xg", [P, 2, TT, D])
        xp = sb("xp", [P, 2, PIECES, DC * ROWS], BF16)
        g = sb("g", [P, BANKS, 512])
        gp = sb("gp", [P, 2, PIECES, NIC * ROWS], BF16)
        yo = sb("yo", [P, 2, TT, D])
        ps_x = ctx.enter_context(nc.psum_tensor("d_ps_x", [P, 2, DC * ROWS], F32))
        ps_u = ctx.enter_context(nc.psum_tensor("d_ps_u", [P, BANKS, 512], F32))
        ps_y = ctx.enter_context(nc.psum_tensor("d_ps_y", [P, TT, 512], F32))

        zeroed, ident_ready = sem("zeroed"), sem("ident_ready")
        x_in = [sem("x_in0"), sem("x_in1")]
        turned, x_split, upped, gelued, g_split, downed, y_ready = (
            sem("turned"), sem("x_split"), sem("upped"), sem("gelued"), sem("g_split"), sem("downed"), sem("y_ready"))
        x_high, g_high, tokens_set, places_set, pool_passed = (
            sem("x_high"), sem("g_high"), sem("tokens_set"), sem("places_set"), sem("pool_passed"))
        y_out = [sem("y_out0"), sem("y_out1")]

        def by_pairs_of_tiles(engine, step):
            for u in range(2):
                step(u, u)
            with engine.Fori(1, RUN_TILES // 2) as i:
                for u in range(2):
                    step(i * 2 + u, u)

        block = ctx.enter_context(nc.Block())

        @block.sync
        def _(sp):
            for e in range(2, NE):
                sp.wait_ge(kept.w_ready[e % 2], 32 * (e // 2))
                sp.wait_ge(downed, sp.value_load(kept.filled[0:1, e - 2:e - 1], min_val=1, max_val=MAX_TILES + 1))
                load_weights(sp, kept, w_parts, e)
            for slot in range(2):
                sp.wait_ge(kept.w_ready[slot], 32 * (NE // 2))

        @block.gpsimd
        def _(pool):
            def load(t, u):
                at_least(pool, turned, t - 1)
                apart(pool, pool_passed)
                pool.tensor_copy(tokens[:, u, :], kept.tokens[:, bass.ds(t * TT, TT)]).then_inc(tokens_set, 1)
                pool.wait_ge(tokens_set, t + 1)
                apart(pool, pool_passed)
                for i in range(TT):
                    pool.indirect_dma_start(xg[:, u, i, :], None, h2_rows,
                                            bass.IndirectOffsetOnAxis(ap=tokens[:, u, i:i + 1], axis=0)).then_inc(x_in[u], 16)

            make_identity(pool, ident, zeroed, ident_ready)
            for u in range(2):
                load(u, u)

            def scatter(t, u):
                at_least(pool, y_out[u], (t - u) * 16)
                apart(pool, pool_passed)
                pool.tensor_copy(places[:, u, :], kept.results[:, bass.ds(t * TT, TT)]).then_inc(places_set, 1)
                pool.wait_ge(places_set, t + 1)
                apart(pool, pool_passed)
                pool.wait_ge(y_ready, t + 1)
                apart(pool, pool_passed)
                for i in range(TT):
                    pool.indirect_dma_start(results, bass.IndirectOffsetOnAxis(ap=places[:, u, i:i + 1], axis=0),
                                            yo[:, u, i, :], None).then_inc(y_out[u], 16)

            def step(t, u):
                load(t + 2, u)
                if not isinstance(t, int) or t > 0:
                    scatter(t - 1, 1 - u)

            by_pairs_of_tiles(pool, step)
            scatter(RUN_TILES - 1, 1)
            for u in range(2):
                pool.wait_ge(x_in[u], 32 * (RUN_TILES // 2 + 1))
                pool.wait_ge(y_out[u], 32 * (RUN_TILES // 2))

        @block.scalar
        def _(act):
            def gelu(t, j):
                act.wait_ge(upped, t * BANKS + j + 1)
                at_least(act, g_split, (t - 1) * BANKS + j + 1)
                act.activation(g[:, j, :], ps_u[:, j, :], ACT.Gelu).then_inc(gelued, 1)

            def result(t, u):
                act.wait_ge(downed, t + 2)
                at_least(act, y_out[u], (t - u) * 16)
                act.activation(yo[:, u, :, :], ps_y[:, :, 0:D], ACT.Copy).then_inc(y_ready, 1)

            def step(t, u):
                if not isinstance(t, int) or t > 0:
                    result(t - 1, 1 - u)
                for j in range(BANKS):
                    gelu(t, j)

            by_pairs_of_tiles(act, step)
            result(RUN_TILES - 1, 1)

        @block.vector
        def _(dve):
            def split_x(t, u):
                dve.wait_ge(turned, t + 1)
                at_least(dve, upped, (t - 1) * BANKS)
                dve.tensor_copy(xp[:, u, 0, :], ps_x[:, u, :]).then_inc(x_high, 1)
                dve.wait_ge(x_high, t + 1)
                dve.tensor_tensor(xp[:, u, 1, :], ps_x[:, u, :], xp[:, u, 0, :], ALU.subtract).then_inc(x_split, 1)

            def step(t, u):
                split_x(t + 1, 1 - u)
                at_least(dve, downed, t)
                for j in range(BANKS):
                    at = slice(j * 512, (j + 1) * 512)
                    dve.wait_ge(gelued, t * BANKS + j + 1)
                    dve.tensor_copy(gp[:, u, 0, at], g[:, j, :]).then_inc(g_high, 1)
                    dve.wait_ge(g_high, t * BANKS + j + 1)
                    dve.tensor_tensor(gp[:, u, 1, at], g[:, j, :], gp[:, u, 0, at], ALU.subtract).then_inc(g_split, 1)

            split_x(0, 0)
            by_pairs_of_tiles(dve, step)

        @block.tensor
        def _(pe):
            def turn(t, u):
                pe.wait_ge(x_in[u], (t - u) * 16 + 32)
                at_least(pe, x_split, t - 1)
                for c in range(DC):
                    for i in range(TT):
                        mm = pe.transpose(ps_x[:, u, c * ROWS + i * P:c * ROWS + (i + 1) * P], xg[:, u, i, c * P:(c + 1) * P], ident[:, :])
                mm.then_inc(turned, 1)

            PRODUCTS = ((0, 0), (0, 1), (1, 0))

            def up(t, u, slot, loaded):
                pe.wait_ge(kept.w_ready[slot], loaded)
                for j in range(NIC):
                    n = 0
                    for c in range(DC):
                        for w, x in PRODUCTS:
                            mm = pe.matmul(ps_u[:, j // 2, j % 2 * ROWS:(j % 2 + 1) * ROWS], kept.wu[:, slot, w, c, j * P:(j + 1) * P],
                                           xp[:, u, x, c * ROWS:(c + 1) * ROWS], start=(n == 0), stop=(n == 5))
                            n += 1
                    if j % 2 == 1:
                        mm.then_inc(upped, 1)

            def down(t, u, slot):
                at_least(pe, y_ready, t)
                for j in range(NIC):
                    if j % 2 == 0:
                        pe.wait_ge(g_split, t * BANKS + j // 2 + 1)
                    for i in range(TT):
                        for n, (w, x) in enumerate(PRODUCTS):
                            mm = pe.matmul(ps_y[:, i, 0:D], gp[:, u, x, j * ROWS + i * P:j * ROWS + (i + 1) * P],
                                           kept.wd[:, slot, w, j, :], start=(j == 0 and n == 0), stop=(j == NIC - 1 and n == 2))
                mm.then_inc(downed, 1)

            def step(t, u):
                loaded = pe.value_load(kept.tiles[0:1, LOADED, bass.ds(t, 1)], min_val=32, max_val=32 * (NE // 2))
                slot = pe.value_load(kept.tiles[0:1, SLOT, bass.ds(t, 1)], min_val=0, max_val=SPARE)
                turn(t + 1, 1 - u)
                pe.wait_ge(x_split, t + 1)
                with pe.If(slot == 0):
                    up(t, u, 0, loaded)
                    down(t, u, 0)
                with pe.Else():
                    with pe.If(slot == 1):
                        up(t, u, 1, loaded)
                        down(t, u, 1)
                    with pe.Else():
                        pe.sem_inc(upped, BANKS)
                        at_least(pe, y_ready, t)
                        pe.sem_inc(downed, 1)

            pe.wait_ge(ident_ready, 1)
            pe.sem_inc(downed, 1)
            turn(0, 0)
            by_pairs_of_tiles(pe, step)


def combine(nc, kept, results, out):
    with ExitStack() as ctx:
        def sb(name, shape, dt=F32):
            return ctx.enter_context(nc.sbuf_tensor("e_" + name, shape, dt))

        def sem(name):
            return ctx.enter_context(nc.semaphore("e_" + name))

        y = sb("y", [P, B, 2, TB, D])
        stats = sb("stats", [P, 2, TB, 6])
        mv = sb("mv", [P, 2, TB, 2])
        rstd = sb("rstd", [P, 2, TB])
        power = sb("power", [P, TB])
        less = sb("less", [P, 2, TB])
        y_in = [sem(f"y_in{b}") for b in range(B)]
        first, mixed, stats_done, mv_done, rstd_done, less_done = (
            sem("first"), sem("mixed"), sem("stats_done"), sem("mv_done"), sem("rstd_done"), sem("less_done"))
        power_set, eps_added = sem("power_set"), sem("eps_added")
        normal, gated, done, h2_gated, rest_done = sem("normal"), sem("gated"), sem("done"), sem("h2_gated"), sem("rest_done")
        stored = sem("stored")
        block = ctx.enter_context(nc.Block())

        @block.gpsimd
        def _(pool):
            pool.memset(power[:, :], -0.5).then_inc(power_set, 1)
            pool.wait_ge(power_set, 1)

            def deviations(b):
                pool.wait_ge(mv_done, (b + 1) * TB)
                at_least(pool, normal, (b - 1) * TB)
                pool.tensor_scalar(rstd[:, b % 2, :], mv[:, b % 2, :, 1], LN_EPS, None, ALU.add).then_inc(eps_added, 1)
                pool.wait_ge(eps_added, b + 1)
                pool.tensor_tensor(rstd[:, b % 2, :], rstd[:, b % 2, :], power[:, :], ALU.pow).then_inc(rstd_done, 1)

            def rest(b):
                h2 = kept.h2[:, b * TB:(b + 1) * TB, :]
                pool.tensor_tensor(h2, h2, kept.gb[:, b, :].unsqueeze(1).to_broadcast([P, TB, D]), ALU.mult).then_inc(h2_gated, 1)
                pool.wait_ge(h2_gated, b + 1)
                pool.tensor_tensor(h2, h2, kept.x1[:, b * TB:(b + 1) * TB, :], ALU.add).then_inc(rest_done, 1)

            rest(0)
            for b in range(B):
                deviations(b)
                if b + 1 < B:
                    rest(b + 1)

        @block.scalar
        def _(act):
            def weigh(b):
                act.wait_ge(y_in[b], 32)
                for t in range(TB):
                    row = y[:, b, 0, t, :]
                    act.activation(row, row, ACT.Copy, scale=kept.gates[:, 0, b * TB + t:b * TB + t + 1]).then_inc(first, 1)

            def normalise(b):
                u = b % 2
                act.wait_ge(less_done, b + 1)
                for t in range(TB):
                    row = y[:, b, 0, t, :]
                    act.activation(row, row, ACT.Identity, bias=less[:, u, t:t + 1], scale=rstd[:, u, t:t + 1]).then_inc(normal, 1)

            weigh(0)
            weigh(1)
            for b in range(B):
                if b + 2 < B:
                    weigh(b + 2)
                normalise(b)

        @block.vector
        def _(dve):
            def mix(b):
                u = b % 2
                for t in range(TB):
                    i = b * TB + t
                    dve.wait_ge(first, i + 1)
                    dve.scalar_tensor_tensor(out=y[:, b, 0, t, :], in0=y[:, b, 1, t, :],
                                             scalar=kept.gates[:, 1, i:i + 1], in1=y[:, b, 0, t, :],
                                             op0=ALU.mult, op1=ALU.add).then_inc(mixed, 1)
                for t in range(TB):
                    dve.wait_ge(mixed, b * TB + t + 1)
                    dve.bn_stats(stats[:, u, t, :], y[:, b, 0, t, :]).then_inc(stats_done, 1)
                at_least(dve, rstd_done, b - 1)
                for t in range(TB):
                    dve.wait_ge(stats_done, b * TB + t + 1)
                    dve.bn_aggr(mv[:, u, t, :], stats[:, u, t, :]).then_inc(mv_done, 1)

            def offsets(b):
                u = b % 2
                dve.wait_ge(rstd_done, b + 1)
                at_least(dve, normal, (b - 1) * TB)
                dve.scalar_tensor_tensor(out=less[:, u, :], in0=mv[:, u, :, 0], scalar=-1.0, in1=rstd[:, u, :],
                                         op0=ALU.mult, op1=ALU.mult).then_inc(less_done, 1)

            def finish(b):
                whole = y[:, b, 0, :, :]
                dve.wait_ge(normal, (b + 1) * TB)
                dve.tensor_tensor(whole, whole, kept.gb[:, b, :].unsqueeze(1).to_broadcast([P, TB, D]),
                                  ALU.mult).then_inc(gated, 1)
                dve.wait_ge(gated, b + 1)
                dve.wait_ge(rest_done, b + 1)
                dve.tensor_tensor(whole, whole, kept.h2[:, b * TB:(b + 1) * TB, :], ALU.add).then_inc(done, 1)

            mix(0)
            mix(1)
            for b in range(B):
                offsets(b)
                if b + 2 < B:
                    mix(b + 2)
                finish(b)

        @block.sync
        def _(sp):
            for b in range(B):
                for k in range(2):
                    sp.dma_start(y[:, b, k, :, :], results[(k * B + b) * S:(k * B + b + 1) * S, :].rearrange("(t p) d -> p t d", p=P)
                                 ).then_inc(y_in[b], 16)
            for b in range(B):
                sp.wait_ge(done, b + 1)
                sp.dma_start(out[b, :, :].rearrange("(t p) d -> p t d", p=P), y[:, b, 0, :, :]).then_inc(stored, 16)
            sp.wait_ge(stored, 16 * B)


def adaln_block(nc, x, w_qkv, b_qkv, w_out, b_out, rel_rev, gate_t, expert_bias, w_up_t, w_down_t, c_t, wmod, out):
    def scratch(name, shape, dt=F32):
        return nc.dram_tensor(name, shape, dt, kind="Internal").ap()

    mod_rows = scratch("mod_rows", (B, 6 * D))
    ext_rows = scratch("ext_rows", (NH, EXT))
    h1t = scratch("h1t", (B, P, DC, S))
    splits = scratch("splits", (B, 2, 2, PARTS, P, S), BF16)
    x1 = scratch("x1", (B, S, D))
    w_parts = scratch("w_parts", (NE, 2, PIECES, P, WN), BF16)
    h2_rows = scratch("h2_rows", (B * S, D))
    results = scratch("results", (2 * B * S + TABLE * ROWS, D))
    with ExitStack() as ctx:
        logits = ctx.enter_context(nc.sbuf_tensor("logits", [P, NT, NE], F32))
        with ExitStack() as ctx_ahead:
            ahead = Ahead(nc, ctx_ahead)
            prepare(nc, ahead, x, c_t, wmod, rel_rev, w_qkv, b_qkv, w_out, b_out, gate_t, mod_rows, ext_rows, h1t)
            attention(nc, ahead, logits, x, h1t, mod_rows, ext_rows, splits,
                      w_up_t, w_down_t, w_parts, x1, h2_rows)
        kept = Kept(nc, ctx)
        route(nc, kept, logits, x1, mod_rows, expert_bias, w_parts, h2_rows)
        experts(nc, kept, w_parts, h2_rows, results)
        combine(nc, kept, results, out)


def kernel(**inputs):
    import numpy as _np
    import concourse.bacc as _bacc
    from concourse.bass_utils import run_bass_kernel_spmd as _run

    a = {name: _np.asarray(value) for name, value in inputs.items()}
    given = {
        "x": a["L0_attn_x"],
        "w_qkv": a["L0_attn_W_qkv"],
        "b_qkv": a["L0_attn_b_qkv"],
        "w_out": a["L0_attn_W_out"],
        "b_out": a["L0_attn_b_out"],
        "rel_rev": a["L0_attn_rel_bias"].T[:, ::-1],
        "gate_t": a["L0_ffn_gate_w"].T,
        "expert_bias": a["L0_ffn_expert_bias"],
        "w_up_t": a["L0_ffn_w_up"].transpose(0, 2, 1),
        "w_down_t": a["L0_ffn_w_down"].transpose(0, 2, 1),
        "c_t": a["L0_c"].T,
        "wmod": a["L0_wmod"],
    }
    nc = _bacc.Bacc("TRN2", target_bir_lowering=False, num_devices=1)
    arrays, args = {}, {}
    for name, value in given.items():
        value = _np.ascontiguousarray(value)
        arrays[f"in_{name}"] = value
        args[name] = nc.dram_tensor(f"in_{name}", value.shape, mybir.dt.from_np(value.dtype), kind="ExternalInput").ap()
    out = nc.dram_tensor("out", (B, S, D), F32, kind="ExternalOutput").ap()
    adaln_block(nc, out=out, **args)
    r = _run(nc, [arrays], core_ids=[0])
    return r.results[0]["out"]
```
